# Optimizing a Trainium2 kernel written in Bass

```python
import numpy as np
import jax
import jax.numpy as jnp

def _softmax(x, axis=-1):
    return jax.nn.softmax(x, axis=axis)

def _gelu(x):
    return jax.nn.gelu(x, approximate=True)

def _silu(x):
    return jax.nn.silu(x)

def _sigmoid(x):
    return jax.nn.sigmoid(x)

def _layernorm(x, axis=-1, eps=1e-05):
    m = jnp.mean(x, axis=axis, keepdims=True)
    v = jnp.var(x, axis=axis, keepdims=True)
    return (x - m) / jnp.sqrt(v + eps)

def _scatter_add(tgt, idx, src, axis=0):
    return tgt.at[idx].add(src)

def _segment_sum(src, seg, n):
    return jax.ops.segment_sum(src, seg, n)
kernel_name = 'mk_sandwich_d2_jaxref_r8_b76c12'

def setup_inputs(seed: int=0):
    np.random.seed(seed)
    _w = jnp.asarray

    def _L0_attn_setup():
        import math
        import jax, jax.numpy as jnp
        import numpy as np
        B, T, E = (2, 256, 512)
        H, HKV = (32, 8)
        DH = E // H
        G = H // HKV
        ROPE_THETA = 500000.0
        ROPE_FACTOR = 32.0
        HI_FREQ_FACTOR = 4.0
        LO_FREQ_FACTOR = 1.0
        ORIG_CTX = 1024

        def _rope_cos_sin(t_len):
            inv_freq = 1.0 / ROPE_THETA ** (jnp.arange(0, DH, 2, dtype=jnp.float32) / DH)
            wavelen = 2.0 * math.pi / inv_freq
            cut_lo = ORIG_CTX / HI_FREQ_FACTOR
            cut_hi = ORIG_CTX / LO_FREQ_FACTOR
            inv_freq = jnp.where(wavelen > cut_hi, inv_freq / ROPE_FACTOR, inv_freq)
            smooth = (ORIG_CTX / wavelen - LO_FREQ_FACTOR) / (HI_FREQ_FACTOR - LO_FREQ_FACTOR)
            smoothed = (1.0 - smooth) * inv_freq / ROPE_FACTOR + smooth * inv_freq
            is_medium = ~(wavelen < cut_hi) & ~(wavelen > cut_lo)
            inv_freq = jnp.where(is_medium, smoothed, inv_freq)
            pos = jnp.arange(t_len, dtype=jnp.float32)
            freqs = pos[:, None] * inv_freq[None, :]
            emb = jnp.concatenate([freqs, freqs], axis=-1)
            return (jnp.cos(emb), jnp.sin(emb))

        def _rotate_half(x):
            x1, x2 = jnp.split(x, 2, axis=-1)
            return jnp.concatenate([-x2, x1], axis=-1)
        key = jax.random.key(seed)
        kx, kq, kk, kv, ko = jax.random.split(key, 5)
        w = lambda k, shape: jax.random.normal(k, shape, jnp.float32) * 0.02
        return {'x': jax.random.normal(kx, (B, T, E), jnp.float32), 'Wq': w(kq, (E, E)), 'Wk': w(kk, (HKV * DH, E)), 'Wv': w(kv, (HKV * DH, E)), 'Wo': w(ko, (E, E))}
    _L0_attn_in = _L0_attn_setup()

    def _L0_ffn_setup():
        import jax, jax.numpy as jnp
        import numpy as np
        HIDDEN = 512
        MOE_INTER = 128
        SHARED_INTER = 512
        NUM_EXPERTS = 16
        TOP_K = 2

        def _moe_forward(x, gate_w, w_gate_up, w_down, shared_w_gate_up, shared_w_down):
            orig_shape = x.shape
            x2 = x.reshape(-1, orig_shape[-1])
            gu_s = x2 @ shared_w_gate_up.T
            g_s, u_s = jnp.split(gu_s, 2, axis=-1)
            shared_out = jax.nn.silu(g_s) * u_s @ shared_w_down.T
            logits = x2 @ gate_w.T
            probs = jax.nn.softmax(logits, axis=-1)
            topk_vals, topk_idx = jax.lax.top_k(probs, TOP_K)
            topk_vals = topk_vals / jnp.sum(topk_vals, axis=-1, keepdims=True)
            combine = jnp.sum(jax.nn.one_hot(topk_idx, NUM_EXPERTS, dtype=x2.dtype) * topk_vals[..., None], axis=1)
            gu = jnp.einsum('th,eih->eti', x2, w_gate_up)
            g, u = jnp.split(gu, 2, axis=-1)
            act = jax.nn.silu(g) * u
            out_e = jnp.einsum('eti,ehi->eth', act, w_down)
            moe_out = jnp.einsum('eth,te->th', out_e, combine)
            return (moe_out + shared_out).reshape(orig_shape)
        key = jax.random.key(seed)
        ks = jax.random.split(key, 6)
        s = 0.02
        hidden_states = jax.random.normal(ks[0], (2, 256, HIDDEN), dtype=jnp.float32)
        gate_w = jax.random.normal(ks[1], (NUM_EXPERTS, HIDDEN), dtype=jnp.float32) * s
        w_gate_up = jax.random.normal(ks[2], (NUM_EXPERTS, 2 * MOE_INTER, HIDDEN), dtype=jnp.float32) * s
        w_down = jax.random.normal(ks[3], (NUM_EXPERTS, HIDDEN, MOE_INTER), dtype=jnp.float32) * s
        shared_w_gate_up = jax.random.normal(ks[4], (2 * SHARED_INTER, HIDDEN), dtype=jnp.float32) * s
        shared_w_down = jax.random.normal(ks[5], (HIDDEN, SHARED_INTER), dtype=jnp.float32) * s
        return {'hidden_states': hidden_states, 'gate_w': gate_w, 'w_gate_up': w_gate_up, 'w_down': w_down, 'shared_w_gate_up': shared_w_gate_up, 'shared_w_down': shared_w_down}
    _L0_ffn_in = _L0_ffn_setup()

    def _L1_attn_setup():
        import math
        import jax, jax.numpy as jnp
        import numpy as np
        IN_F, OUT_F, HID = (512, 512, 512)
        WINDOW, STRIPES = (6, 3)

        def make_sparse_mask(n_in=IN_F, n_out=OUT_F, window=WINDOW, stripes=STRIPES):
            m = np.zeros((n_in, n_out), dtype=np.float32)
            stride = int(math.sqrt(n_in))
            for k in range(stripes):
                ps = stride * k
                for i in range(0, n_in, window):
                    m[ps + i:ps + i + window, i:i + window] = 1.0
            mb = m.astype(bool)
            return jnp.asarray((mb | mb.T).astype(np.float32))
        key = jax.random.key(seed)
        k1, k2, k3, k4 = jax.random.split(key, 4)
        scale = 1.0 / math.sqrt(IN_F)
        x = jax.random.normal(k1, (8, 96, IN_F), dtype=jnp.float32)
        w1 = jax.random.normal(k2, (HID, IN_F), dtype=jnp.float32) * scale
        w2 = jax.random.normal(k3, (OUT_F, HID), dtype=jnp.float32) * scale
        b2 = jax.random.normal(k4, (OUT_F,), dtype=jnp.float32) * scale
        return {'x': x, 'w1': w1, 'w2': w2, 'b2': b2, 'sparse_mask': make_sparse_mask()}
    _L1_attn_in = _L1_attn_setup()

    def _L1_ffn_setup():
        import jax, jax.numpy as jnp
        import numpy as np
        D_MODEL = 512
        D_HIDDEN = 1376
        RANK = 16
        BATCH, SEQ = (2, 256)

        def _matmul_lora(x, w, a, b, scale=1.0):
            out = jnp.einsum('bsd,hd->bsh', x, w)
            out = out + jnp.einsum('bsr,hr->bsh', jnp.einsum('bsd,rd->bsr', x, a), b) * scale
            return out
        key = jax.random.key(seed)
        ks = jax.random.split(key, 10)
        s = 0.02
        return {'x': jax.random.normal(ks[0], (BATCH, SEQ, D_MODEL), jnp.float32), 'gate_w': jax.random.normal(ks[1], (D_HIDDEN, D_MODEL), jnp.float32) * s, 'up_w': jax.random.normal(ks[2], (D_HIDDEN, D_MODEL), jnp.float32) * s, 'down_w': jax.random.normal(ks[3], (D_MODEL, D_HIDDEN), jnp.float32) * s, 'gate_a': jax.random.normal(ks[4], (RANK, D_MODEL), jnp.float32) * s, 'gate_b': jax.random.normal(ks[5], (D_HIDDEN, RANK), jnp.float32) * s, 'up_a': jax.random.normal(ks[6], (RANK, D_MODEL), jnp.float32) * s, 'up_b': jax.random.normal(ks[7], (D_HIDDEN, RANK), jnp.float32) * s, 'down_a': jax.random.normal(ks[8], (RANK, D_HIDDEN), jnp.float32) * s, 'down_b': jax.random.normal(ks[9], (D_MODEL, RANK), jnp.float32) * s}
    _L1_ffn_in = _L1_ffn_setup()
    _d = {'L0_attn_x': _L0_attn_in['x'], 'L0_attn_Wq': _L0_attn_in['Wq'], 'L0_attn_Wk': _L0_attn_in['Wk'], 'L0_attn_Wv': _L0_attn_in['Wv'], 'L0_attn_Wo': _L0_attn_in['Wo'], 'L0_ffn_gate_w': _L0_ffn_in['gate_w'], 'L0_ffn_w_gate_up': _L0_ffn_in['w_gate_up'], 'L0_ffn_w_down': _L0_ffn_in['w_down'], 'L0_ffn_shared_w_gate_up': _L0_ffn_in['shared_w_gate_up'], 'L0_ffn_shared_w_down': _L0_ffn_in['shared_w_down'], 'L1_attn_w1': _L1_attn_in['w1'], 'L1_attn_w2': _L1_attn_in['w2'], 'L1_attn_b2': _L1_attn_in['b2'], 'L1_attn_sparse_mask': _L1_attn_in['sparse_mask'], 'L1_ffn_gate_w': _L1_ffn_in['gate_w'], 'L1_ffn_up_w': _L1_ffn_in['up_w'], 'L1_ffn_down_w': _L1_ffn_in['down_w'], 'L1_ffn_gate_a': _L1_ffn_in['gate_a'], 'L1_ffn_gate_b': _L1_ffn_in['gate_b'], 'L1_ffn_up_a': _L1_ffn_in['up_a'], 'L1_ffn_up_b': _L1_ffn_in['up_b'], 'L1_ffn_down_a': _L1_ffn_in['down_a'], 'L1_ffn_down_b': _L1_ffn_in['down_b']}
    _x0 = _d['L0_attn_x']
    _d['L0_attn_x'] = jax.random.normal(jax.random.fold_in(jax.random.key(seed), 1), (4, 512, 512), dtype=_x0.dtype)
    del _x0
    return _d

def reference(L0_attn_x, L0_attn_Wq, L0_attn_Wk, L0_attn_Wv, L0_attn_Wo, L0_ffn_gate_w, L0_ffn_w_gate_up, L0_ffn_w_down, L0_ffn_shared_w_gate_up, L0_ffn_shared_w_down, L1_attn_w1, L1_attn_w2, L1_attn_b2, L1_attn_sparse_mask, L1_ffn_gate_w, L1_ffn_up_w, L1_ffn_down_w, L1_ffn_gate_a, L1_ffn_gate_b, L1_ffn_up_a, L1_ffn_up_b, L1_ffn_down_a, L1_ffn_down_b):

    def _L0_attn_ref(x, Wq, Wk, Wv, Wo):
        import math
        import jax, jax.numpy as jnp
        import numpy as np
        B, T, E = (2, 256, 512)
        H, HKV = (32, 8)
        DH = E // H
        G = H // HKV
        ROPE_THETA = 500000.0
        ROPE_FACTOR = 32.0
        HI_FREQ_FACTOR = 4.0
        LO_FREQ_FACTOR = 1.0
        ORIG_CTX = 1024

        def _rope_cos_sin(t_len):
            inv_freq = 1.0 / ROPE_THETA ** (jnp.arange(0, DH, 2, dtype=jnp.float32) / DH)
            wavelen = 2.0 * math.pi / inv_freq
            cut_lo = ORIG_CTX / HI_FREQ_FACTOR
            cut_hi = ORIG_CTX / LO_FREQ_FACTOR
            inv_freq = jnp.where(wavelen > cut_hi, inv_freq / ROPE_FACTOR, inv_freq)
            smooth = (ORIG_CTX / wavelen - LO_FREQ_FACTOR) / (HI_FREQ_FACTOR - LO_FREQ_FACTOR)
            smoothed = (1.0 - smooth) * inv_freq / ROPE_FACTOR + smooth * inv_freq
            is_medium = ~(wavelen < cut_hi) & ~(wavelen > cut_lo)
            inv_freq = jnp.where(is_medium, smoothed, inv_freq)
            pos = jnp.arange(t_len, dtype=jnp.float32)
            freqs = pos[:, None] * inv_freq[None, :]
            emb = jnp.concatenate([freqs, freqs], axis=-1)
            return (jnp.cos(emb), jnp.sin(emb))

        def _rotate_half(x):
            x1, x2 = jnp.split(x, 2, axis=-1)
            return jnp.concatenate([-x2, x1], axis=-1)
        b, t, _ = x.shape
        q = (x @ Wq.T).reshape(b, t, H, DH).transpose(0, 2, 1, 3)
        k = (x @ Wk.T).reshape(b, t, HKV, DH).transpose(0, 2, 1, 3)
        v = (x @ Wv.T).reshape(b, t, HKV, DH).transpose(0, 2, 1, 3)
        cos, sin = _rope_cos_sin(t)
        cos = cos.astype(x.dtype)[None, None]
        sin = sin.astype(x.dtype)[None, None]
        q = q * cos + _rotate_half(q) * sin
        k = k * cos + _rotate_half(k) * sin
        qg = q.reshape(b, HKV, G, t, DH)
        scores = jnp.einsum('bhgtd,bhkd->bhgtk', qg.astype(jnp.float32), k.astype(jnp.float32)) / math.sqrt(DH)
        causal = jnp.tril(jnp.ones((t, t), dtype=bool))
        scores = jnp.where(causal[None, None, None], scores, jnp.finfo(jnp.float32).min)
        attn = jax.nn.softmax(scores, axis=-1).astype(x.dtype)
        ctx = jnp.einsum('bhgtk,bhkd->bhgtd', attn, v)
        out = ctx.reshape(b, H, t, DH).transpose(0, 2, 1, 3).reshape(b, t, E)
        return out @ Wo.T

    def _L0_ffn_ref(hidden_states, gate_w, w_gate_up, w_down, shared_w_gate_up, shared_w_down):
        import jax, jax.numpy as jnp
        import numpy as np
        HIDDEN = 512
        MOE_INTER = 128
        SHARED_INTER = 512
        NUM_EXPERTS = 16
        TOP_K = 2

        def _moe_forward(x, gate_w, w_gate_up, w_down, shared_w_gate_up, shared_w_down):
            orig_shape = x.shape
            x2 = x.reshape(-1, orig_shape[-1])
            gu_s = x2 @ shared_w_gate_up.T
            g_s, u_s = jnp.split(gu_s, 2, axis=-1)
            shared_out = jax.nn.silu(g_s) * u_s @ shared_w_down.T
            logits = x2 @ gate_w.T
            probs = jax.nn.softmax(logits, axis=-1)
            topk_vals, topk_idx = jax.lax.top_k(probs, TOP_K)
            topk_vals = topk_vals / jnp.sum(topk_vals, axis=-1, keepdims=True)
            combine = jnp.sum(jax.nn.one_hot(topk_idx, NUM_EXPERTS, dtype=x2.dtype) * topk_vals[..., None], axis=1)
            gu = jnp.einsum('th,eih->eti', x2, w_gate_up)
            g, u = jnp.split(gu, 2, axis=-1)
            act = jax.nn.silu(g) * u
            out_e = jnp.einsum('eti,ehi->eth', act, w_down)
            moe_out = jnp.einsum('eth,te->th', out_e, combine)
            return (moe_out + shared_out).reshape(orig_shape)
        return _moe_forward(hidden_states, gate_w, w_gate_up, w_down, shared_w_gate_up, shared_w_down)

    def _L1_attn_ref(x, w1, w2, b2, sparse_mask):
        import math
        import jax, jax.numpy as jnp
        import numpy as np
        IN_F, OUT_F, HID = (512, 512, 512)
        WINDOW, STRIPES = (6, 3)

        def make_sparse_mask(n_in=IN_F, n_out=OUT_F, window=WINDOW, stripes=STRIPES):
            m = np.zeros((n_in, n_out), dtype=np.float32)
            stride = int(math.sqrt(n_in))
            for k in range(stripes):
                ps = stride * k
                for i in range(0, n_in, window):
                    m[ps + i:ps + i + window, i:i + window] = 1.0
            mb = m.astype(bool)
            return jnp.asarray((mb | mb.T).astype(np.float32))
        attn = jnp.einsum('ds,td->st', w1, w2) * sparse_mask
        y = jnp.einsum('bds,st->bdt', x, attn) + b2
        return jax.nn.gelu(y, approximate=False)

    def _L1_ffn_ref(x, gate_w, up_w, down_w, gate_a, gate_b, up_a, up_b, down_a, down_b):
        import jax, jax.numpy as jnp
        import numpy as np
        D_MODEL = 512
        D_HIDDEN = 1376
        RANK = 16
        BATCH, SEQ = (2, 256)

        def _matmul_lora(x, w, a, b, scale=1.0):
            out = jnp.einsum('bsd,hd->bsh', x, w)
            out = out + jnp.einsum('bsr,hr->bsh', jnp.einsum('bsd,rd->bsr', x, a), b) * scale
            return out
        gate = _matmul_lora(x, gate_w, gate_a, gate_b)
        up = _matmul_lora(x, up_w, up_a, up_b)
        hidden = jax.nn.silu(gate) * up
        out = _matmul_lora(hidden, down_w, down_a, down_b)
        return out
    x = L0_attn_x
    x = x + _layernorm(_L0_attn_ref(_layernorm(x, axis=-1), L0_attn_Wq, L0_attn_Wk, L0_attn_Wv, L0_attn_Wo), axis=-1)
    x = x + _layernorm(_L0_ffn_ref(_layernorm(x, axis=-1), L0_ffn_gate_w, L0_ffn_w_gate_up, L0_ffn_w_down, L0_ffn_shared_w_gate_up, L0_ffn_shared_w_down), axis=-1)
    x = x + _layernorm(_L1_attn_ref(_layernorm(x, axis=-1), L1_attn_w1, L1_attn_w2, L1_attn_b2, L1_attn_sparse_mask), axis=-1)
    x = x + _layernorm(_L1_ffn_ref(_layernorm(x, axis=-1), L1_ffn_gate_w, L1_ffn_up_w, L1_ffn_down_w, L1_ffn_gate_a, L1_ffn_gate_b, L1_ffn_up_a, L1_ffn_up_b, L1_ffn_down_a, L1_ffn_down_b), axis=-1)
    return x

_drawn_inputs = setup_inputs


def setup_inputs(seed=0):
    import zlib

    import numpy as np

    out = dict(_drawn_inputs(seed))
    spreads = {}
    factors = {}
    for name, (base, spread) in spreads.items():
        noise = np.random.default_rng([zlib.crc32(name.encode()), seed]).standard_normal(out[name].shape)
        drawn = base * np.exp(spread * noise) if base else spread * noise
        out[name] = jnp.asarray(drawn.astype(out[name].dtype))
    for name, factor in factors.items():
        out[name] = (out[name] * factor).astype(out[name].dtype)
    return out
```

```python
from contextlib import ExitStack

import numpy as np
import concourse.bass as bass
from concourse import mybir

F32 = mybir.dt.float32
F32R = mybir.dt.float32r
BF16 = mybir.dt.bfloat16
U32 = mybir.dt.uint32
ALU = mybir.AluOpType
ACT = mybir.ActivationFunctionType
AX_X = mybir.AxisListType.X

P = 128
D = 512
KD = D // P
NB, T = 4, 512
TPB = T // P
NT = NB * TPB
H, HKV, DH = 32, 8, 16
G = H // HKV
QK = (H + HKV) * DH
QKV = QK + HKV * DH
HB = 32
NE, INTER = 16, 128
NSH = 4
UNITS_MOE = NE + NSH
FF = 1376
UNITS_FF = -(-FF // P)
RANK = 16
EPS = 1e-5
MASKED = -1.0e30


def setup_tables():
    inv = (1.0 / np.power(np.float32(500000.0), np.arange(0, DH, 2, dtype=np.float32) / np.float32(DH))).astype(np.float32)
    wavelen = (np.float32(2.0 * np.pi) / inv).astype(np.float32)
    lo, hi = 1024 / 4.0, 1024 / 1.0
    inv2 = np.where(wavelen > hi, inv / np.float32(32.0), inv).astype(np.float32)
    smooth = ((np.float32(1024) / wavelen - np.float32(1.0)) / np.float32(3.0)).astype(np.float32)
    smoothed = ((1 - smooth) * inv2 / np.float32(32.0) + smooth * inv2).astype(np.float32)
    medium = ~(wavelen < hi) & ~(wavelen > lo)
    inv2 = np.where(medium, smoothed, inv2).astype(np.float32)
    ang = (np.arange(T, dtype=np.float32)[:, None] * inv2[None, :]).astype(np.float32)
    cos = np.cos(np.concatenate([ang, ang], 1)).astype(np.float32)
    sin = np.sin(np.concatenate([-ang, ang], 1)).astype(np.float32)
    return np.stack([cos, sin], 1)


def const_phase(nc, s, m, dram):
    with nc.Block(no_gpsimd_drain=True) as block:
        @block.sync
        def _(sp):
            for c in range(NB):
                sp.dma_start(m.x[:, c * TPB:(c + 1) * TPB, :],
                             dram.x[c * T:(c + 1) * T, :].rearrange("(t p) d -> p t d", p=P)).then_inc(s.x_in, 16)

        @block.gpsimd
        def _(pool):
            nc.gpsimd.memset(m.ident[:], 0.0).then_inc(s.const, 1)
            nc.gpsimd.memset(m.ident16[:], 0.0).then_inc(s.const, 1)
            nc.gpsimd.memset(m.causal[:], 0.0).then_inc(s.const, 1)
            nc.gpsimd.memset(m.v_pad[:], 0.0).then_inc(s.const, 1)
            nc.gpsimd.memset(m.combine[:], 1.0).then_inc(s.const, 1)
            nc.gpsimd.memset(m.eps[:], EPS).then_inc(s.const, 1)
            nc.gpsimd.memset(m.zero[:], 0.0).then_inc(s.const, 1)
            pool.wait_ge(s.const, 7)
            for tile in (m.ident, m.ident16):
                nc.gpsimd.affine_select(out=tile[:], in_=tile[:], compare_op=ALU.not_equal, fill=1.0, base=0,
                                        pattern=[[-1, P]], channel_multiplier=1).then_inc(s.const, 1)
            nc.gpsimd.affine_select(out=m.causal[:], in_=m.causal[:], compare_op=ALU.is_ge, fill=MASKED, base=0,
                                    pattern=[[-1, P]], channel_multiplier=1).then_inc(s.const, 1)
            nc.gpsimd.memset(m.v_pad[:, :, :, DH:DH + 1], 1.0).then_inc(s.const, 1)
            pool.wait_ge(s.const, CONSTANTS)


CONSTANTS = 11


def wait_apart(eng, s, sem, value):
    eng.wait_ge(sem, value)
    eng.sem_inc(s.passed, 1)


def ln_moments(nc, v, s, m, sources, stats_sem, moments_sem, c):
    for t, src in enumerate(sources):
        nc.vector.bn_stats(m.stats[:, t, :], src).then_inc(stats_sem, 1)
    wait_apart(v, s, stats_sem, c * TPB + TPB)
    for t in range(TPB):
        nc.vector.bn_aggr(m.mv[:, t, :], m.stats[:, t, :]).then_inc(moments_sem, 1)


def ln_deviation(nc, a, m, moments_sem, dev_sem, c):
    a.wait_ge(moments_sem, c * TPB + TPB)
    nc.scalar.activation(m.dev[:], m.mv[:, :, 1], ACT.Sqrt, bias=m.eps[:]).then_inc(dev_sem, 1)


def ln_rstd(nc, v, m, dev_sem, rstd_sem, c):
    v.wait_ge(dev_sem, c + 1)
    nc.vector.reciprocal(m.rstd[:], m.dev[:]).then_inc(rstd_sem, 1)
    v.wait_ge(rstd_sem, c + 1)


def ln_apply(nc, m, t, out, src):
    return nc.vector.tensor_scalar(out, src, m.mv[:, t, 0:1], m.rstd[:, t:t + 1], ALU.subtract, ALU.mult)


def split_product(nc, out, wh, wl, xh, xl, first=True, last=True):
    nc.tensor.matmul(out, wh, xh, start=first, stop=False)
    nc.tensor.matmul(out, wh, xl, start=False, stop=False)
    return nc.tensor.matmul(out, wl, xh, start=False, stop=last)


def qkv_phase(nc, s, m, dram):
    with ExitStack() as ctx:
        sb = lambda n, shape, dt=F32: ctx.enter_context(nc.sbuf_tensor(n, shape, dt))
        ps = lambda n, shape: ctx.enter_context(nc.psum_tensor(n, shape, F32))
        w_raw = sb("qkv_w_raw", [P, KD, QKV])
        wh, wl = sb("qkv_wh", [P, KD, QKV], F32R), sb("qkv_wl", [P, KD, QKV], F32R)
        rope = sb("rope", [P, TPB, 2, DH])
        xn = sb("qkv_xn", [P, TPB, D])
        xh, xl = sb("qkv_xh", [P, 2, KD, P], F32R), sb("qkv_xl", [P, 2, KD, P], F32R)
        by_cos, by_sin = sb("by_cos", [P, 2, QK]), sb("by_sin", [P, 2, QK])
        rot = sb("rotated", [P, 2, QK])
        NQ = QK // P
        qth, qtl = sb("qkT_h_sb", [P, NQ, T], F32R), sb("qkT_l_sb", [P, NQ, T], F32R)
        ps_t = ps("qkv_ps_t", [P, 2, KD, P])
        ps_qkv = ps("ps_qkv", [P, 2, 2 * 512])
        ps_qt = ps("ps_qt", [P, 2 * 512])
        block = ctx.enter_context(nc.Block(no_gpsimd_drain=True))

        @block.sync
        def _(sp):
            for src, a, b in ((dram.wqT, 0, D), (dram.wkT, D, QK), (dram.wvT, QK, QKV)):
                sp.dma_start(w_raw[:, :, a:b], src.rearrange("(k p) n -> p k n", p=P)).then_inc(s.qkv_w_in, 16)
            sp.dma_start(rope[:], dram.rope.rearrange("(t p) a d -> p t a d", p=P)).then_inc(s.rope_in, 16)
            with sp.Fori(0, NB) as c:
                sp.wait_ge(s.qth_ready, c * TPB + TPB)
                sp.dma_start(dram.qkT_h[:, bass.ds(c * T, T)].rearrange("(j p) t -> p j t", p=P), qth[:].bitcast(F32)).then_inc(s.qkT_out, 16)
                sp.wait_ge(s.qtl_ready, c * TPB + TPB + 1)
                sp.dma_start(dram.qkT_l[:, bass.ds(c * T, T)].rearrange("(j p) t -> p j t", p=P), qtl[:].bitcast(F32)).then_inc(s.qkT_out, 16)
            sp.wait_ge(s.qkT_out, 32 * NB + 32)

        @block.gpsimd
        def _(pool):
            pool.sem_inc(s.qkT_out, 32)
            pool.sem_inc(s.rot_ready, 2)
            with pool.Fori(0, NB) as c:
                for t in range(TPB):
                    pool.wait_ge(s.rope_parts, c * TPB + t + 1)
                    pool.wait_ge(s.q_transposed, c * TPB + t + 1)
                    nc.gpsimd.tensor_tensor(rot[:, t % 2, :], by_cos[:, t % 2, :], by_sin[:, t % 2, :],
                                            ALU.add).then_inc(s.rot_ready, 1)

        @block.scalar
        def _(a):
            a.sem_inc(s.v_ready, 2)
            a.wait_ge(s.qkv_w_in, 48)
            nc.scalar.copy(wh[:], w_raw[:]).then_inc(s.qkv_wh, 1)
            with a.Fori(0, NB) as c:
                ln_deviation(nc, a, m, s.a1_moments, s.a1_dev, c)

                def q_high(t):
                    a.wait_ge(s.q_transposed, c * TPB + t + 3)
                    if t == 0:
                        a.wait_ge(s.qkT_out, c * 32 + 32)
                    nc.scalar.copy(qth[:, :, t * P:(t + 1) * P], ps_qt[:, 0:QK].rearrange("p (j n) -> p j n", n=P)).then_inc(s.qth_ready, 1)

                for t in range(TPB):
                    b = t % 2
                    a.wait_ge(s.a1_tr, c * TPB + t + TPB + 1)
                    a.wait_ge(s.qkv_done, c * TPB + t + 1)
                    nc.scalar.copy(xh[:, b], ps_t[:, b]).then_inc(s.a1_xh, 1)
                    if t:
                        q_high(t - 1)
                    a.wait_ge(s.rope_parts, c * TPB + t + 1)
                    nc.scalar.copy(m.v_pad[:, bass.ds(c * TPB + t, 1), :, 0:DH],
                                   ps_qkv[:, b, QK:QKV].rearrange("p (o g d) -> p o g d", o=1, d=DH)).then_inc(s.v_ready, 1)
                q_high(TPB - 1)

        @block.vector
        def _(v):
            v.sem_inc(s.qtl_ready, 1)
            v.sem_inc(s.a1_xl, 2)
            v.wait_ge(s.qkv_wh, 1)
            nc.vector.tensor_tensor(wl[:], w_raw[:], wh[:], ALU.subtract).then_inc(s.qkv_wl, 1)
            v.wait_ge(s.rope_in, 16)
            with v.Fori(0, NB) as c:
                wait_apart(v, s, s.x_in, c * 16 + 16)
                ln_moments(nc, v, s, m, [m.x[:, bass.ds(c * TPB + t, 1), :] for t in range(TPB)], s.a1_stats, s.a1_moments, c)
                ln_rstd(nc, v, m, s.a1_dev, s.a1_rstd, c)
                for t in range(TPB):
                    v.wait_ge(s.a1_tr, c * TPB + t + 1)
                    ln_apply(nc, m, t, xn[:, t:t + 1, :], m.x[:, bass.ds(c * TPB + t, 1), :]).then_inc(s.a1_xn, 1)

                def q_low(t):
                    v.wait_ge(s.qth_ready, c * TPB + t + 1)
                    if t == 0:
                        v.wait_ge(s.qkT_out, c * 32 + 32)
                    nc.vector.tensor_tensor(qtl[:, :, t * P:(t + 1) * P], ps_qt[:, 0:QK].rearrange("p (j n) -> p j n", n=P),
                                            qth[:, :, t * P:(t + 1) * P], ALU.subtract).then_inc(s.qtl_ready, 1)

                for t in range(TPB):
                    b = t % 2
                    v.wait_ge(s.a1_xh, c * TPB + t + 1)
                    nc.vector.tensor_tensor(xl[:, b], ps_t[:, b], xh[:, b], ALU.subtract).then_inc(s.a1_xl, 1)
                    if t:
                        q_low(t - 1)
                    v.wait_ge(s.qkv_done, c * TPB + t + 3)
                    v.wait_ge(s.rot_ready, c * TPB + t + 1)
                    heads = ps_qkv[:, b, 0:QK].rearrange("p (h d) -> p h d", d=DH)
                    cosv = rope[:, t, 0, :].unsqueeze(1).to_broadcast([P, H + HKV, DH])
                    sinv = rope[:, t, 1, :].unsqueeze(1).to_broadcast([P, H + HKV, DH])
                    co = by_cos[:, b, :].rearrange("p (h d) -> p h d", d=DH)
                    si = by_sin[:, b, :].rearrange("p (h d) -> p h d", d=DH)
                    nc.vector.tensor_tensor(co, heads, cosv, ALU.mult)
                    h2 = DH // 2
                    nc.vector.tensor_tensor(si[:, :, 0:h2], heads[:, :, h2:DH], sinv[:, :, 0:h2], ALU.mult)
                    nc.vector.tensor_tensor(si[:, :, h2:DH], heads[:, :, 0:h2], sinv[:, :, h2:DH], ALU.mult).then_inc(s.rope_parts, 1)
                q_low(TPB - 1)

        @block.tensor
        def _(pe):
            pe.sem_inc(s.a1_tr, TPB)
            pe.sem_inc(s.qkv_done, 2)
            pe.sem_inc(s.q_transposed, 2)
            with pe.Fori(0, NB) as c:
                def q_transpose(t):
                    pe.wait_ge(s.rot_ready, c * TPB + t + 3)
                    pe.wait_ge(s.qtl_ready, c * TPB + t + 1)
                    for j in range(NQ):
                        last = nc.tensor.transpose(ps_qt[:, j * P:(j + 1) * P], rot[:, t % 2, j * P:(j + 1) * P], m.ident[:])
                    last.then_inc(s.q_transposed, 1)

                for t in range(TPB):
                    b = t % 2
                    pe.wait_ge(s.a1_xn, c * TPB + t + 1)
                    pe.wait_ge(s.a1_xl, c * TPB + t + 1)
                    for k in range(KD):
                        last = nc.tensor.transpose(ps_t[:, b, k, :], xn[:, t, k * P:(k + 1) * P], m.ident[:])
                    last.then_inc(s.a1_tr, 1)
                    if t:
                        q_transpose(t - 1)
                    if t == 0:
                        pe.wait_ge(s.qkv_wl, 1)
                    pe.wait_ge(s.a1_xl, c * TPB + t + 3)
                    pe.wait_ge(s.v_ready, c * TPB + t + 1)
                    for lo, hi in ((0, D), (D, QKV)):
                        for k in range(KD):
                            last = split_product(nc, ps_qkv[:, b, lo:hi], xh[:, b, k, :], xl[:, b, k, :],
                                                 wh[:, k, lo:hi], wl[:, k, lo:hi], k == 0, k == KD - 1)
                    last.then_inc(s.qkv_done, 1)
                q_transpose(TPB - 1)


def attention_phase(nc, s, m, dram):
    KS, KM = 3 * DH, 3 * DH + 2
    STEPS = NB * HKV
    with ExitStack() as ctx:
        sb = lambda n, shape, dt=F32: ctx.enter_context(nc.sbuf_tensor(n, shape, dt))
        ps = lambda n, shape: ctx.enter_context(nc.psum_tensor(n, shape, F32))
        qs = [sb(f"q_stack{i}", [KM, G, T], F32R) for i in range(2)]
        ks = [sb(f"k_stack{i}", [KM, T], F32R) for i in range(2)]
        vs = [sb(f"v_step{i}", [P, TPB, HB]) for i in range(2)]
        row_max = [sb(f"row_max{i}", [P, G * TPB]) for i in range(2)]
        max_hl = [sb(f"max_hl{i}", [P, 2 * G * TPB]) for i in range(2)]
        maxT = [sb(f"maxT{i}", [2 * G * TPB, P]) for i in range(2)]
        pT = [sb(f"weightsT{i}", [P, G, T]) for i in range(2)]
        ctxT = [sb(f"ctxT{i}", [P, T]) for i in range(2)]
        rden = [sb(f"rden{i}", [P, TPB, G]) for i in range(2)]
        ps_s = ps("ps_scores", [P, 2, 2, T])
        ps_st = ps("ps_scoresT", [P, 2, T])
        ps_o = ps("ps_ctxT", [P, T])
        ps_x = ps("ps_turned", [P, T])
        block = ctx.enter_context(nc.Block(no_gpsimd_drain=True))
        RG, CG = 2 * TPB, G * TPB

        def pairs(eng, first, both, last):
            first(0)
            with eng.Fori(0, STEPS // 2 - 1) as i:
                both(i * 2 + 1, 1)
                both(i * 2 + 2, 0)
            both(STEPS - 1, 1)
            last(STEPS)

        @block.sync
        def _(sp):
            for b in range(2):
                sp.sem_inc(s.max_in[b], 32)
            sp.wait_ge(s.ones_ready, 2)

            def load(n, b):
                if not (isinstance(n, int) and n < 2):
                    sp.wait_ge(s.ctxT_done, n)
                seq, g = n // HKV, n % HKV
                tok = bass.ds(seq * T, T)
                qrows = bass.ds(g * (G * DH), G * DH)
                krows = bass.ds(g * DH + D, DH)
                for part, src in ((0, dram.qkT_h), (1, dram.qkT_l), (2, dram.qkT_h)):
                    sp.dma_start(qs[b][part * DH:(part + 1) * DH, :, :].bitcast(F32),
                                 src[qrows, tok].rearrange("(h d) t -> d h t", d=DH)).then_inc(s.qs_in[b], 16)
                for part, src in ((0, dram.qkT_h), (1, dram.qkT_h), (2, dram.qkT_l)):
                    sp.dma_start(ks[b][part * DH:(part + 1) * DH, :].bitcast(F32), src[krows, tok]).then_inc(s.qs_in[b], 16)

            def maxima(n, b):
                sp.wait_ge(s.maxT_ready, n + 1)
                for part in range(2):
                    sp.dma_start(qs[b][KS + part:KS + part + 1, :, :].bitcast(F32),
                                 maxT[b][part * G * TPB:(part + 1) * G * TPB, :]).then_inc(s.max_in[b], 16)

            load(0, 0)
            load(1, 1)
            maxima(0, 0)
            with sp.Fori(0, STEPS // 2 - 1) as i:
                load(i * 2 + 2, 0)
                maxima(i * 2 + 1, 1)
                load(i * 2 + 3, 1)
                maxima(i * 2 + 2, 0)
            maxima(STEPS - 1, 1)

        @block.gpsimd
        def _(pool):
            for b in range(2):
                nc.gpsimd.memset(ks[b][:].bitcast(F32), 1.0).then_inc(s.ones_ready, 1)

            def mask(n, b):
                for j in range(TPB):
                    wait_apart(pool, s, s.exps, n * CG + (j + 1) * G + 2)
                    nc.gpsimd.affine_select(out=pT[j % 2][:, :, 0:P], in_=pT[j % 2][:, :, 0:P], compare_op=ALU.is_ge,
                                            fill=0.0, base=0, pattern=[[0, G], [1, P]], channel_multiplier=-1).then_inc(s.masked, 1)

            with pool.Fori(0, STEPS) as n:
                mask(n, 0)

        @block.scalar
        def _(a):
            a.sem_inc(s.exps, 2)
            a.sem_inc(s.ctxT_ready, 1)

            def max_copy(n, b):
                a.wait_ge(s.maxT_turned, n + 1)
                a.wait_ge(s.max_in[b], (n // 2) * 32 + 32)
                nc.scalar.copy(maxT[b][:], ps_x[0:2 * G * TPB, 0:P]).then_inc(s.maxT_ready, 1)

            def exps(n, b):
                for j in range(TPB):
                    for h in range(G):
                        k = j * G + h
                        a.wait_ge(s.scoresT, n * CG + k + 1)
                        if h == 0:
                            a.wait_ge(s.weighted, n * TPB + j + 2 - 1)
                        w = T - j * P
                        nc.scalar.activation(pT[j % 2][:, h, 0:w], ps_st[:, k % 2, 0:w], ACT.Exp, scale=DH ** -0.5).then_inc(s.exps, 1)

            def ctx_copy(n, b):
                a.wait_ge(s.weighted, n * TPB + TPB + 2)
                nc.scalar.copy(ctxT[b][:], ps_o[:]).then_inc(s.ctxT_ready, 1)

            def v_copy(n, b):
                if not isinstance(n, int):
                    a.wait_ge(s.ctxT_done, n)
                seq, g = n // HKV, n % HKV
                nc.scalar.copy(vs[b][:], m.v_pad[:, bass.ds(seq * TPB, TPB), bass.ds(g, 1), :].rearrange("p t o d -> p t (o d)")).then_inc(s.v_in, 1)

            def both(n, b):
                v_copy(n, b)
                exps(n - 1, 1 - b)
                ctx_copy(n - 1, 1 - b)
                max_copy(n, b)

            def first(n):
                v_copy(0, 0)
                max_copy(0, 0)

            def last(n):
                exps(n - 1, 1)
                ctx_copy(n - 1, 1)

            pairs(a, first, both, last)

        @block.vector
        def _(v):
            v.sem_inc(s.row_max, 2)
            v.sem_inc(s.ctx_ready, 1)

            def maxima(n, b):
                for i in range(TPB):
                    for hp in range(2):
                        k = i * 2 + hp
                        v.wait_ge(s.scores, n * RG + k + 1)
                        nc.vector.tensor_reduce(row_max[b][:, 2 * hp * TPB + i:2 * hp * TPB + i + TPB + 1:TPB],
                                                ps_s[:, k % 2, :, 0:(i + 1) * P], AX_X, ALU.max, negate=True).then_inc(s.row_max, 1)
                half = G * TPB
                v.wait_ge(s.row_max, n * RG + RG + 2)
                nc.vector.tensor_copy(max_hl[b][:, 0:half].bitcast(F32R), row_max[b][:]).then_inc(s.max_high, 1)
                v.wait_ge(s.max_high, n + 1)
                nc.vector.tensor_tensor(max_hl[b][:, half:2 * half].bitcast(F32R), row_max[b][:], max_hl[b][:, 0:half], ALU.subtract).then_inc(s.max_low, 1)

            def normalize(n, b):
                seq, g = n // HKV, n % HKV
                v.wait_ge(s.ctxT_done, n + 2)
                blocks = ps_x[:].rearrange("p (i h c) -> p i h c", i=TPB, h=G)
                nc.vector.reciprocal(rden[b][:], blocks[:, :, :, DH]).then_inc(s.rden, 1)
                v.wait_ge(s.rden, n + 1)
                for i in range(TPB):
                    ins = nc.vector.tensor_tensor(m.acc[:, bass.ds(seq * TPB + i, 1), bass.ds(g * (G * DH), G * DH)].rearrange("p o (h d) -> p (o h) d", d=DH),
                                                  blocks[:, i, :, 0:DH], rden[b][:, i, :].unsqueeze(2).to_broadcast([P, G, DH]), ALU.mult)
                ins.then_inc(s.ctx_ready, 1)

            def both(n, b):
                maxima(n, b)
                normalize(n - 1, 1 - b)

            pairs(v, lambda n: maxima(0, 0), both, lambda n: normalize(n - 1, 1))

        @block.tensor
        def _(pe):
            pe.sem_inc(s.weighted, 2)
            pe.sem_inc(s.ctxT_done, 1)

            def scores(n, b):
                pe.wait_ge(s.qs_in[b], (n // 2) * 96 + 96)
                for i in range(TPB):
                    for hp in range(2):
                        k = i * 2 + hp
                        pe.wait_ge(s.row_max, n * RG + k + 1)
                        for o in range(2):
                            h = 2 * hp + o
                            nc.tensor.matmul(ps_s[:, k % 2, o, 0:(i + 1) * P], qs[b][0:KS, h, i * P:(i + 1) * P], ks[b][0:KS, 0:(i + 1) * P], start=True, stop=False)
                            last = nc.tensor.matmul(ps_s[:, k % 2, o, i * P:(i + 1) * P], m.ident16[:], m.causal[:], start=False, stop=True)
                        last.then_inc(s.scores, 1)

            def turn_maxima(n, b):
                pe.wait_ge(s.max_low, n + 1)
                pe.wait_ge(s.ctx_ready, n + 1)
                nc.tensor.transpose(ps_x[0:2 * G * TPB, 0:P], max_hl[b][:], m.ident[:]).then_inc(s.maxT_turned, 1)

            def scoresT(n, b, j):
                for h in range(G):
                    k = j * G + h
                    pe.wait_ge(s.exps, n * CG + k + 1)
                    nc.tensor.matmul(ps_st[:, k % 2, 0:T - j * P], ks[b][0:KM, j * P:(j + 1) * P], qs[b][0:KM, h, j * P:T], start=True, stop=True).then_inc(s.scoresT, 1)

            def weighted(n, b, j):
                pe.wait_ge(s.masked, n * TPB + j + 1)
                for h in range(G):
                    last = nc.tensor.matmul(ps_o[h * HB:(h + 1) * HB, j * P:T], vs[b][:, j, :], pT[j % 2][:, h, 0:T - j * P],
                                            start=j == 0, stop=j == TPB - 1)
                last.then_inc(s.weighted, 1)

            def turn_context(n, b):
                pe.wait_ge(s.ctxT_ready, n + 2)
                for i in range(TPB):
                    last = nc.tensor.transpose(ps_x[:, i * P:(i + 1) * P], ctxT[b][:, i * P:(i + 1) * P], m.ident[:])
                last.then_inc(s.ctxT_done, 1)

            def columns(n, b):
                pe.wait_ge(s.max_in[b], (n // 2) * 32 + 64)
                pe.wait_ge(s.v_in, n + 1)
                for j in range(TPB):
                    scoresT(n, b, j)
                    if j:
                        if j == 1:
                            pe.wait_ge(s.ctxT_ready, n + 1)
                        weighted(n, b, j - 1)
                weighted(n, b, TPB - 1)

            def both(n, b):
                scores(n, b)
                columns(n - 1, 1 - b)
                pe.wait_ge(s.maxT_ready, n)
                turn_context(n - 1, 1 - b)
                turn_maxima(n, b)

            def first(n):
                scores(0, 0)
                turn_maxima(0, 0)

            def last(n):
                columns(n - 1, 1)
                turn_context(n - 1, 1)

            pairs(pe, first, both, last)


def output_phase(nc, s, m, dram):
    with ExitStack() as ctx:
        sb = lambda n, shape, dt=F32: ctx.enter_context(nc.sbuf_tensor(n, shape, dt))
        ps = lambda n, shape: ctx.enter_context(nc.psum_tensor(n, shape, F32))
        w_raw = sb("wo_raw", [P, KD, D])
        wh, wl = sb("wo_h", [P, KD, D], F32R), sb("wo_l", [P, KD, D], F32R)
        g_raw = sb("router_raw", [P, KD, P])
        gh, gl = sb("router_h", [P, KD, P], F32R), sb("router_l", [P, KD, P], F32R)
        ch, cl = sb("ctx_h", [P, 2, KD, P], F32R), sb("ctx_l", [P, 2, KD, P], F32R)
        ct = sb("ctx_tiles", [P, TPB, D])
        yn = sb("o_normed", [P, TPB, D])
        xn = sb("o_xn", [P, TPB, D])
        logitsT = sb("logitsT", [NE, T])
        logits = sb("logits", [P, TPB, NE])
        best, best_at = sb("best", [P, TPB, 8]), sb("best_at", [P, TPB, 8], U32)
        top, top_at = sb("top", [P, NT, 2]), sb("top_at", [P, NT, 2])
        gap, wgt = sb("top_gap", [P, NT]), sb("top_weight", [P, 3, NT])
        expert, one_hot = sb("expert_index", [P, NE]), sb("one_hot", [P, 2, NT, NE])
        ps_t = ps("o_ps_t", [P, 2, KD, P])
        ps_o = ps("o_ps", [P, TPB, D])
        ps_g = ps("o_ps_g", [P, T])
        ps_l = ps("o_ps_l", [P, T])
        block = ctx.enter_context(nc.Block(no_gpsimd_drain=True))

        @block.sync
        def _(sp):
            sp.dma_start(w_raw[:], dram.woT.rearrange("(k p) n -> p k n", p=P)).then_inc(s.wo_in, 16)
            sp.wait_ge(s.router_pad, 1)
            sp.dma_start(g_raw[:, :, 0:NE], dram.routerT.rearrange("(k p) n -> p k n", p=P)).then_inc(s.router_in, 16)

        @block.gpsimd
        def _(pool):
            nc.gpsimd.memset(g_raw[:], 0.0).then_inc(s.router_pad, 1)
            nc.gpsimd.iota(expert[:], [[1, NE]], base=0, channel_multiplier=0, allow_small_or_imprecise_dtypes=True).then_inc(s.expert_index, 1)
            with pool.Fori(0, NB) as c:
                for t in range(TPB):
                    tok = bass.ds(c * TPB + t, 1)
                    wait_apart(pool, s, s.o_tr, c * TPB + t + 1)
                    nc.gpsimd.tensor_copy(ct[:, t:t + 1, :], m.acc[:, tok, :]).then_inc(s.o_ct, 1)
                    wait_apart(pool, s, s.o_ct, c * TPB + t + 1)
                    nc.gpsimd.tensor_copy(m.acc[:, tok, :], m.zero[:, 0:1].unsqueeze(1).to_broadcast([P, 1, D])).then_inc(s.o_zero, 1)
                for t in range(TPB):
                    tok = bass.ds(c * TPB + t, 1)
                    wait_apart(pool, s, s.o_yn, c * TPB + t + 1 + TPB)
                    nc.gpsimd.tensor_tensor(m.x[:, tok, :], m.x[:, tok, :], yn[:, t:t + 1, :], ALU.add).then_inc(s.o_x, 1)
            pool.wait_ge(s.o_zero, NT)

        @block.scalar
        def _(a):
            a.sem_inc(s.logitsT, 1)
            a.wait_ge(s.wo_in, 16)
            nc.scalar.copy(wh[:], w_raw[:]).then_inc(s.wo_h, 1)
            a.wait_ge(s.router_in, 16)
            nc.scalar.copy(gh[:], g_raw[:]).then_inc(s.router_h, 1)
            with a.Fori(0, NB) as c:
                for t in range(TPB):
                    a.wait_ge(s.o_tr, c * TPB + t + 1 + TPB)
                    a.wait_ge(s.o_done, c * TPB + t + 1)
                    nc.scalar.copy(ch[:, t % 2], ps_t[:, t % 2]).then_inc(s.o_ch, 1)
                ln_deviation(nc, a, m, s.b1_moments, s.b1_dev, c)
                ln_deviation(nc, a, m, s.b2_moments, s.b2_dev, c)
                for t in range(TPB):
                    a.wait_ge(s.b2_tr, c * TPB + t + 1)
                    nc.scalar.copy(m.xnh[:, :, bass.ds(c * T + t * P, P)], ps_t[:, t % 2]).then_inc(s.b2_h, 1)
                a.wait_ge(s.router_done, c + 1)
                nc.scalar.copy(logitsT[:], ps_g[0:NE, :]).then_inc(s.logitsT, 1)
            a.wait_ge(s.top_gap, 1)
            nc.scalar.activation(wgt[:, 0, :], gap[:], ACT.Exp).then_inc(s.top_exp, 1)

        @block.vector
        def _(v):
            v.sem_inc(s.o_cl, 2)
            v.sem_inc(s.b2_l, 1)
            v.sem_inc(s.o_yn, TPB)
            v.sem_inc(s.logits, 1)
            v.wait_ge(s.wo_h, 1)
            nc.vector.tensor_tensor(wl[:], w_raw[:], wh[:], ALU.subtract).then_inc(s.wo_l, 1)
            v.wait_ge(s.router_h, 1)
            nc.vector.tensor_tensor(gl[:], g_raw[:], gh[:], ALU.subtract).then_inc(s.router_l, 1)
            with v.Fori(0, NB) as c:
                for t in range(TPB):
                    v.wait_ge(s.o_ch, c * TPB + t + 1)
                    nc.vector.tensor_tensor(cl[:, t % 2], ps_t[:, t % 2], ch[:, t % 2], ALU.subtract).then_inc(s.o_cl, 1)
                v.wait_ge(s.o_done, c * TPB + TPB + 2)
                ln_moments(nc, v, s, m, [ps_o[:, t, :] for t in range(TPB)], s.b1_stats, s.b1_moments, c)
                ln_rstd(nc, v, m, s.b1_dev, s.b1_rstd, c)
                for t in range(TPB):
                    ln_apply(nc, m, t, yn[:, t, :], ps_o[:, t, :]).then_inc(s.o_yn, 1)
                v.wait_ge(s.o_x, c * TPB + TPB)
                ln_moments(nc, v, s, m, [m.x[:, bass.ds(c * TPB + t, 1), :] for t in range(TPB)], s.b2_stats, s.b2_moments, c)
                ln_rstd(nc, v, m, s.b2_dev, s.b2_rstd, c)
                for t in range(TPB):
                    ln_apply(nc, m, t, xn[:, t:t + 1, :], m.x[:, bass.ds(c * TPB + t, 1), :]).then_inc(s.b2_xn, 1)
                for t in range(TPB):
                    cols = bass.ds(c * T + t * P, P)
                    v.wait_ge(s.b2_h, c * TPB + t + 1)
                    nc.vector.tensor_tensor(m.xnl[:, :, cols], ps_t[:, t % 2], m.xnh[:, :, cols], ALU.subtract).then_inc(s.b2_l, 1)
                v.wait_ge(s.logits_turned, c + 1)
                nc.vector.tensor_copy(logits[:], ps_l[:, 0:TPB * NE].rearrange("p (t e) -> p t e", e=NE)).then_inc(s.logits, 1)
                wait_apart(v, s, s.logits, c + 2)
                for t in range(TPB):
                    nc.vector.max(best[:, t, :], logits[:, t, :]).then_inc(s.best, 1)
                wait_apart(v, s, s.best, c * TPB + TPB)
                for t in range(TPB):
                    nc.vector.max_index(best_at[:, t, :], best[:, t, :], logits[:, t, :]).then_inc(s.best_at, 1)
                v.wait_ge(s.best_at, c * TPB + TPB)
                nc.vector.tensor_copy(top[:, bass.ds(c * TPB, TPB), :], best[:, :, 0:2]).then_inc(s.top, 1)
                nc.vector.tensor_copy(top_at[:, bass.ds(c * TPB, TPB), :], best_at[:, :, 0:2]).then_inc(s.top, 1)
            v.wait_ge(s.top, 2 * NB)
            nc.vector.tensor_tensor(gap[:], top[:, :, 1], top[:, :, 0], ALU.subtract).then_inc(s.top_gap, 1)
            v.wait_ge(s.top_exp, 1)
            nc.vector.tensor_scalar_add(wgt[:, 1, :], wgt[:, 0, :], 1.0).then_inc(s.top_weight, 1)
            v.wait_ge(s.top_weight, 1)
            nc.vector.reciprocal(wgt[:, 1, :], wgt[:, 1, :]).then_inc(s.top_weight, 1)
            v.wait_ge(s.top_weight, 2)
            nc.vector.tensor_tensor(wgt[:, 2, :], wgt[:, 0, :], wgt[:, 1, :], ALU.mult).then_inc(s.top_weight, 1)
            v.wait_ge(s.top_weight, 3)
            v.wait_ge(s.expert_index, 1)
            for r in range(2):
                nc.vector.tensor_tensor(one_hot[:, r], expert[:].unsqueeze(1).to_broadcast([P, NT, NE]),
                                        top_at[:, :, r].unsqueeze(2).to_broadcast([P, NT, NE]), ALU.is_equal).then_inc(s.one_hot, 1)
            v.wait_ge(s.one_hot, 2)
            for r in range(2):
                nc.vector.tensor_tensor(one_hot[:, r], one_hot[:, r], wgt[:, 1 + r, :].unsqueeze(2).to_broadcast([P, NT, NE]), ALU.mult).then_inc(s.one_hot, 1)
            v.wait_ge(s.one_hot, 4)
            nc.vector.tensor_tensor(m.combine[:, :, 0:NE], one_hot[:, 0], one_hot[:, 1], ALU.add).then_inc(s.combine, 1)
            v.wait_ge(s.combine, 1)

        @block.tensor
        def _(pe):
            pe.sem_inc(s.o_done, 2)
            pe.sem_inc(s.o_tr, TPB)
            pe.wait_ge(s.wo_l, 1)
            pe.wait_ge(s.router_l, 1)
            with pe.Fori(0, NB) as c:
                for t in range(TPB):
                    b = t % 2
                    pe.wait_ge(s.o_ct, c * TPB + t + 1)
                    pe.wait_ge(s.o_cl, c * TPB + t + 1)
                    if t < 2:
                        pe.wait_ge(s.b2_l, c * TPB + 1)
                    for k in range(KD):
                        last = nc.tensor.transpose(ps_t[:, b, k, :], ct[:, t, k * P:(k + 1) * P], m.ident[:])
                    last.then_inc(s.o_tr, 1)
                    pe.wait_ge(s.o_cl, c * TPB + t + 3)
                    if t == 0:
                        pe.wait_ge(s.o_yn, c * TPB + TPB)
                    for k in range(KD):
                        last = split_product(nc, ps_o[:, t, :], ch[:, b, k, :], cl[:, b, k, :], wh[:, k, :], wl[:, k, :], k == 0, k == KD - 1)
                    last.then_inc(s.o_done, 1)
                for t in range(TPB):
                    b = t % 2
                    pe.wait_ge(s.b2_xn, c * TPB + t + 1)
                    if t >= 2:
                        pe.wait_ge(s.b2_l, c * TPB + t)
                    for k in range(KD):
                        last = nc.tensor.transpose(ps_t[:, b, k, :], xn[:, t, k * P:(k + 1) * P], m.ident[:])
                    last.then_inc(s.b2_tr, 1)
                pe.wait_ge(s.b2_l, c * TPB + TPB + 1)
                pe.wait_ge(s.logitsT, c + 1)
                for k in range(KD):
                    last = split_product(nc, ps_g[:], gh[:, k, :], gl[:, k, :], m.xnh[:, k, bass.ds(c * T, T)], m.xnl[:, k, bass.ds(c * T, T)], k == 0, k == KD - 1)
                last.then_inc(s.router_done, 1)
                pe.wait_ge(s.logitsT, c + 2)
                wait_apart(pe, s, s.logits, c + 1)
                for t in range(TPB):
                    last = nc.tensor.transpose(ps_l[:, t * NE:(t + 1) * NE], logitsT[:, t * P:(t + 1) * P], m.ident[0:NE, 0:NE])
                last.then_inc(s.logits_turned, 1)


def units_phase(nc, s, q, m, dram, name, units, up_down, lora=None):
    STEPS = units * NB
    with ExitStack() as ctx:
        sb = lambda n, shape, dt=F32: ctx.enter_context(nc.sbuf_tensor(f"{name}_{n}", shape, dt))
        ps = lambda n, shape: ctx.enter_context(nc.psum_tensor(f"{name}_{n}", shape, F32))
        NW = KD * 2 * P + D
        w_raw = [sb(f"w_raw{i}", [P, NW]) for i in range(2)]
        wh = [sb(f"wh{i}", [P, NW], F32R) for i in range(2)]
        wl = [sb(f"wl{i}", [P, NW], F32R) for i in range(2)]
        silu = [sb(f"silu{i}", [P, T]) for i in range(2)]
        act = [sb(f"act{i}", [P, T]) for i in range(2)]
        acth = [sb(f"acth{i}", [P, T], F32R) for i in range(2)]
        actl = [sb(f"actl{i}", [P, T], F32R) for i in range(2)]
        if lora:
            la = sb("lora_a", [RANK, 2, D])
            lb = sb("lora_b", [RANK, D])
            lu = [sb(f"lora_unit{i}", [RANK, 3, P]) for i in range(2)]
        ps_g = ps("ps_gate", [P, 2, T])
        ps_u = ps("ps_up", [P, 2, T])
        ps_d = ps("ps_down", [P, TPB, D])
        block = ctx.enter_context(nc.Block(no_gpsimd_drain=True))
        gate_up = lambda w, k, half: w[:, k * 2 * P + half * P:k * 2 * P + (half + 1) * P]
        down = lambda w: w[:, KD * 2 * P:NW]

        def unit_loop(eng, unit):
            unit(0, 0, False)
            with eng.Fori(0, (units - 1) // 2 - units % 2) as i:
                unit(i * 2 + 1, 1, False)
                unit(i * 2 + 2, 0, False)
            if units % 2:
                unit(units - 2, 1, False)
            unit(units - 1, (units - 1) % 2, True)

        @block.sync
        def _(sp):
            if lora:
                for i, src in enumerate((dram.gate_a, dram.up_a)):
                    sp.dma_start(la[:, i, :], src).then_inc(q.lora_in, 16)
                sp.dma_start(lb[:], dram.down_bT).then_inc(q.lora_in, 16)

            def load(u, b):
                if not (isinstance(u, int) and u < 2):
                    sp.wait_ge(q.split_l, u - 1)
                src_u, src_d = up_down
                one = bass.ds(u, 1)
                sp.dma_start(w_raw[b][:, 0:KD * 2 * P].rearrange("p (k n) -> p k n", k=KD),
                             src_u[one].rearrange("u (k p) n -> p (u k) n", p=P)).then_inc(q.w_in[b], 16)
                sp.dma_start(down(w_raw[b]), src_d[one].rearrange("u p n -> p (u n)")).then_inc(q.w_in[b], 16)
                if lora:
                    sp.dma_start(lu[b][:], dram.lora_unit[one].rearrange("u r a n -> r (u a) n")).then_inc(q.w_in[b], 16)

            load(0, 0)
            load(1, 1)
            with sp.Fori(0, (units - 2) // 2) as i:
                load(i * 2 + 2, 0)
                load(i * 2 + 3, 1)
            if units % 2:
                load(units - 1, 0)

        W_IN = 48 if lora else 32

        def split_high(a, u, b):
            if lora:
                a.wait_ge(q.folded, u + 1)
            else:
                a.wait_ge(q.w_in[b], (u // 2) * W_IN + W_IN)
            if not (isinstance(u, int) and u < 2):
                a.wait_ge(q.down_done, (u - 1) * STEP_D)
            nc.scalar.copy(wh[b][:], w_raw[b][:]).then_inc(q.split_h, 1)

        STEP_D = NB * TPB

        @block.scalar
        def _(a):
            def unit(u, b, tail):
                for c in range(NB):
                    a.wait_ge(q.gate_up, u * NB + c + 1)
                    nc.scalar.activation(silu[c % 2][:], ps_g[:, c % 2, :], ACT.Silu).then_inc(q.silu, 1)
                    a.wait_ge(q.product, u * NB + c + 1 + 2)
                    if not (isinstance(u, int) and u == 0 and c < 2):
                        a.wait_ge(q.down_done, (u * NB + c - 1) * TPB)
                    nc.scalar.copy(acth[c % 2][:], act[c % 2][:]).then_inc(q.act_h, 1)
                    if c == 1 and not tail:
                        split_high(a, u + 1, 1 - b)
            split_high(a, 0, 0)
            unit_loop(a, unit)

        @block.vector
        def _(v):
            v.sem_inc(q.product, 2)
            v.sem_inc(q.summed, TPB)

            def fold(u, b):
                v.wait_ge(q.w_in[b], (u // 2) * W_IN + W_IN)
                for i in range(3):
                    v.wait_ge(q.low_rank, u * 3 + i + 1)
                    bank = ps_d[:, i, :]
                    if i < 2:
                        dst = w_raw[b][:, 0:KD * 2 * P].rearrange("p (k a n) -> p k a n", k=KD, a=2)[:, :, i, :]
                        src = bank.rearrange("p (k n) -> p k n", k=KD)
                    else:
                        dst, src = down(w_raw[b]), bank
                    last = nc.vector.tensor_tensor(dst, dst, src, ALU.add)
                last.then_inc(q.folded, 1)

            def prepare(u, b):
                if lora:
                    fold(u, b)
                v.wait_ge(q.split_h, u + 1)
                nc.vector.tensor_tensor(wl[b][:], w_raw[b][:], wh[b][:], ALU.subtract).then_inc(q.split_l, 1)

            def product(u, c):
                b = c % 2
                n = u * NB + c
                v.wait_ge(q.silu, n + 1)
                nc.vector.tensor_tensor(act[b][:], silu[b][:], ps_u[:, b, :], ALU.mult).then_inc(q.product, 1)
                v.wait_ge(q.act_h, n + 1)
                nc.vector.tensor_tensor(actl[b][:], act[b][:], acth[b][:], ALU.subtract).then_inc(q.act_l, 1)

            def sums(u, c):
                for t in range(TPB):
                    v.wait_ge(q.down_done, u * STEP_D + c * TPB + t + 1)
                    acc = m.acc[:, c * TPB + t, :]
                    nc.vector.scalar_tensor_tensor(out=acc, in0=ps_d[:, t, :], scalar=m.combine[:, c * TPB + t, bass.ds(u, 1)] if not lora else 1.0,
                                                   in1=acc, op0=ALU.mult, op1=ALU.add).then_inc(q.summed, 1)

            def unit(u, b, tail):
                for c in range(NB):
                    product(u, c)
                    if c:
                        sums(u, c - 1)
                    elif not isinstance(u, int) or u:
                        sums(u - 1, NB - 1)
                    if c == 1 and not tail:
                        prepare(u + 1, 1 - b)

            prepare(0, 0)
            unit_loop(v, unit)
            sums(units - 1, NB - 1)
            v.wait_ge(q.summed, units * STEP_D + TPB)

        @block.tensor
        def _(pe):
            if lora:
                pe.wait_ge(q.lora_in, 48)

            def low_rank(u, b):
                pe.wait_ge(q.w_in[b], (u // 2) * W_IN + W_IN)
                pe.wait_ge(q.summed, TPB if isinstance(u, int) and u == 0 else (u - 1) * STEP_D + 2 * TPB)
                for i in range(2):
                    for k in range(KD):
                        last = nc.tensor.matmul(ps_d[:, i, k * P:(k + 1) * P], la[:, i, k * P:(k + 1) * P], lu[b][:, i, :], start=True, stop=True)
                    last.then_inc(q.low_rank, 1)
                nc.tensor.matmul(ps_d[:, 2, :], lu[b][:, 2, :], lb[:], start=True, stop=True).then_inc(q.low_rank, 1)

            def gate_up_products(u, b, c):
                n = u * NB + c
                if c == 0:
                    pe.wait_ge(q.split_l, u + 1)
                pe.wait_ge(q.product, n + 1)
                for half, bank in ((0, ps_g), (1, ps_u)):
                    for k in range(KD):
                        last = split_product(nc, bank[:, c % 2, :], gate_up(wh[b], k, half), gate_up(wl[b], k, half),
                                             m.xnh[:, k, c * T:(c + 1) * T], m.xnl[:, k, c * T:(c + 1) * T], k == 0, k == KD - 1)
                last.then_inc(q.gate_up, 1)

            def down_products(u, b, c, tail=False):
                n = u * NB + c
                pe.wait_ge(q.act_l, n + 1)
                if lora and c == 1 and not tail:
                    pe.wait_ge(q.folded, u + 2)
                for t in range(TPB):
                    pe.wait_ge(q.summed, n * TPB + t + 1)
                    cols = slice(t * P, (t + 1) * P)
                    split_product(nc, ps_d[:, t, :], acth[c % 2][:, cols], actl[c % 2][:, cols],
                                  down(wh[b]), down(wl[b])).then_inc(q.down_done, 1)

            def unit(u, b, tail):
                for c in range(NB):
                    gate_up_products(u, b, c)
                    if c:
                        down_products(u, b, c - 1, tail)
                    elif not isinstance(u, int) or u:
                        down_products(u - 1, 1 - b, NB - 1)
                    if lora and c == 1 and not tail:
                        low_rank(u + 1, 1 - b)
            if lora:
                low_rank(0, 0)

            unit_loop(pe, unit)
            down_products(units - 1, (units - 1) % 2, NB - 1)


def weight_product_phase(nc, s, m, dram, ah, al):
    with ExitStack() as ctx:
        sb = lambda n, shape, dt=F32: ctx.enter_context(nc.sbuf_tensor(n, shape, dt))
        w1, w2, mask = sb("w1_raw", [P, KD, D]), sb("w2_raw", [P, KD, D]), sb("mask_raw", [P, KD, D])
        masked = sb("w_masked", [P, 2, D])
        ps_w = ctx.enter_context(nc.psum_tensor("ps_w", [P, 2, D], F32))
        block = ctx.enter_context(nc.Block(no_gpsimd_drain=True))

        @block.sync
        def _(sp):
            for dst, src in ((w1, dram.w1), (w2, dram.w2T), (mask, dram.mask)):
                sp.dma_start(dst[:], src.rearrange("(k p) n -> p k n", p=P)).then_inc(s.w12_in, 16)

        @block.tensor
        def _(pe):
            pe.wait_ge(s.w12_in, 48)
            for j in range(KD):
                if j >= 2:
                    pe.wait_ge(s.w_masked, j - 1)
                for k in range(KD):
                    last = nc.tensor.matmul(ps_w[:, j % 2, :], w1[:, k, j * P:(j + 1) * P], w2[:, k, :], start=k == 0, stop=k == KD - 1)
                last.then_inc(s.w_product, 1)

        @block.vector
        def _(v):
            v.wait_ge(s.w12_in, 48)
            for j in range(KD):
                v.wait_ge(s.w_product, j + 1)
                if j >= 2:
                    v.wait_ge(s.w_low, j - 1)
                nc.vector.tensor_tensor(masked[:, j % 2, :], ps_w[:, j % 2, :], mask[:, j, :], ALU.mult).then_inc(s.w_masked, 1)
                v.wait_ge(s.w_high, j + 1)
                nc.vector.tensor_tensor(al[:, j, :], masked[:, j % 2, :], ah[:, j, :], ALU.subtract).then_inc(s.w_low, 1)
            v.wait_ge(s.w_low, KD)

        @block.scalar
        def _(a):
            for j in range(KD):
                a.wait_ge(s.w_masked, j + 1)
                nc.scalar.copy(ah[:, j, :], masked[:, j % 2, :]).then_inc(s.w_high, 1)


def mix_phase(nc, s, m, dram):
    with ExitStack() as ctx:
        sb = lambda n, shape, dt=F32: ctx.enter_context(nc.sbuf_tensor(n, shape, dt))
        ps = lambda n, shape: ctx.enter_context(nc.psum_tensor(n, shape, F32))
        ah, al = sb("mix_wh", [P, KD, D], F32R), sb("mix_wl", [P, KD, D], F32R)
        weight_product_phase(nc, s, m, dram, ah, al)
        b2 = sb("b2", [P, D])
        yn = sb("mix_normed", [P, TPB, D])
        xn = sb("mix_xn", [P, TPB, D])
        xh, xl = sb("mix_xh", [P, 2, KD, P], F32R), sb("mix_xl", [P, 2, KD, P], F32R)
        ps_t = ps("mix_ps_t", [P, 2, KD, P])
        ps_y = ps("mix_ps_y", [P, TPB, D])
        block = ctx.enter_context(nc.Block(no_gpsimd_drain=True))
        x_tiles = lambda c: [m.x[:, bass.ds(c * TPB + t, 1), :] for t in range(TPB)]

        @block.sync
        def _(sp):
            sp.dma_start(b2[:], dram.b2.to_broadcast([P, D])).then_inc(s.b2_in, 16)

        @block.gpsimd
        def _(pool):
            with pool.Fori(0, NB) as c:
                for t in range(TPB):
                    tok = bass.ds(c * TPB + t, 1)
                    wait_apart(pool, s, s.c1_yn, c * TPB + t + 1)
                    nc.gpsimd.tensor_tensor(m.x[:, tok, :], m.x[:, tok, :], yn[:, t:t + 1, :], ALU.add).then_inc(s.c1_x, 1)
                    nc.gpsimd.tensor_copy(m.acc[:, tok, :], m.zero[:, 0:1].unsqueeze(1).to_broadcast([P, 1, D])).then_inc(s.c1_zero, 1)
                for t in range(TPB):
                    tok = bass.ds(c * TPB + t, 1)
                    wait_apart(pool, s, s.c3_yn, c * TPB + t + 1)
                    nc.gpsimd.tensor_tensor(m.x[:, tok, :], m.x[:, tok, :], yn[:, t:t + 1, :], ALU.add).then_inc(s.c3_x, 1)
            pool.wait_ge(s.c1_zero, NT)

        @block.scalar
        def _(a):
            with a.Fori(0, NB) as c:
                ln_deviation(nc, a, m, s.c1_moments, s.c1_dev, c)
                ln_deviation(nc, a, m, s.c2_moments, s.c2_dev, c)
                for t in range(TPB):
                    a.wait_ge(s.c2_tr, c * TPB + t + 1)
                    a.wait_ge(s.mixed, c * TPB + t + 1)
                    nc.scalar.copy(xh[:, t % 2], ps_t[:, t % 2]).then_inc(s.c2_h, 1)
                for t in range(TPB):
                    a.wait_ge(s.biased, c * TPB + t + 1)
                    nc.scalar.activation(yn[:, t, :], xn[:, t, :], ACT.Gelu).then_inc(s.gelu, 1)
                ln_deviation(nc, a, m, s.c3_moments, s.c3_dev, c)
                ln_deviation(nc, a, m, s.c4_moments, s.c4_dev, c)
                for t in range(TPB):
                    a.wait_ge(s.c4_tr, c * TPB + t + 1)
                    nc.scalar.copy(m.xnh[:, :, bass.ds(c * T + t * P, P)], ps_t[:, t % 2]).then_inc(s.c4_h, 1)

        @block.vector
        def _(v):
            v.sem_inc(s.c2_l, 2)
            v.sem_inc(s.c4_l, 1)
            v.wait_ge(s.b2_in, 16)
            with v.Fori(0, NB) as c:
                acc = [m.acc[:, bass.ds(c * TPB + t, 1), :] for t in range(TPB)]
                ln_moments(nc, v, s, m, acc, s.c1_stats, s.c1_moments, c)
                ln_rstd(nc, v, m, s.c1_dev, s.c1_rstd, c)
                for t in range(TPB):
                    ln_apply(nc, m, t, yn[:, t:t + 1, :], acc[t]).then_inc(s.c1_yn, 1)
                v.wait_ge(s.c1_x, c * TPB + TPB)
                ln_moments(nc, v, s, m, x_tiles(c), s.c2_stats, s.c2_moments, c)
                ln_rstd(nc, v, m, s.c2_dev, s.c2_rstd, c)
                for t in range(TPB):
                    ln_apply(nc, m, t, xn[:, t:t + 1, :], x_tiles(c)[t]).then_inc(s.c2_xn, 1)
                for t in range(TPB):
                    v.wait_ge(s.c2_h, c * TPB + t + 1)
                    nc.vector.tensor_tensor(xl[:, t % 2], ps_t[:, t % 2], xh[:, t % 2], ALU.subtract).then_inc(s.c2_l, 1)
                for t in range(TPB):
                    v.wait_ge(s.mixed, c * TPB + t + 1 + 2)
                    nc.vector.tensor_tensor(xn[:, t, :], ps_y[:, t, :], b2[:], ALU.add).then_inc(s.biased, 1)
                v.wait_ge(s.gelu, c * TPB + TPB)
                ln_moments(nc, v, s, m, [yn[:, t, :] for t in range(TPB)], s.c3_stats, s.c3_moments, c)
                ln_rstd(nc, v, m, s.c3_dev, s.c3_rstd, c)
                for t in range(TPB):
                    ln_apply(nc, m, t, yn[:, t, :], yn[:, t, :]).then_inc(s.c3_yn, 1)
                wait_apart(v, s, s.c3_x, c * TPB + TPB)
                ln_moments(nc, v, s, m, x_tiles(c), s.c4_stats, s.c4_moments, c)
                ln_rstd(nc, v, m, s.c4_dev, s.c4_rstd, c)
                for t in range(TPB):
                    ln_apply(nc, m, t, xn[:, t:t + 1, :], x_tiles(c)[t]).then_inc(s.c4_xn, 1)
                for t in range(TPB):
                    cols = bass.ds(c * T + t * P, P)
                    v.wait_ge(s.c4_h, c * TPB + t + 1)
                    nc.vector.tensor_tensor(m.xnl[:, :, cols], ps_t[:, t % 2], m.xnh[:, :, cols], ALU.subtract).then_inc(s.c4_l, 1)
            v.wait_ge(s.c4_l, NT + 1)

        @block.tensor
        def _(pe):
            pe.sem_inc(s.mixed, 2)
            with pe.Fori(0, NB) as c:
                for t in range(TPB):
                    b = t % 2
                    pe.wait_ge(s.c2_xn, c * TPB + t + 1)
                    pe.wait_ge(s.c2_l, c * TPB + t + 1)
                    if t < 2:
                        pe.wait_ge(s.c4_l, c * TPB + 1)
                    for k in range(KD):
                        last = nc.tensor.transpose(ps_t[:, b, k, :], xn[:, t, k * P:(k + 1) * P], m.ident[:])
                    last.then_inc(s.c2_tr, 1)
                    pe.wait_ge(s.c2_l, c * TPB + t + 3)
                    for k in range(KD):
                        last = split_product(nc, ps_y[:, t, :], xh[:, b, k, :], xl[:, b, k, :], ah[:, k, :], al[:, k, :], k == 0, k == KD - 1)
                    last.then_inc(s.mixed, 1)
                for t in range(TPB):
                    b = t % 2
                    pe.wait_ge(s.c4_xn, c * TPB + t + 1)
                    if t >= 2:
                        pe.wait_ge(s.c4_l, c * TPB + t)
                    for k in range(KD):
                        last = nc.tensor.transpose(ps_t[:, b, k, :], xn[:, t, k * P:(k + 1) * P], m.ident[:])
                    last.then_inc(s.c4_tr, 1)


def final_phase(nc, s, m, dram):
    with ExitStack() as ctx:
        yn = ctx.enter_context(nc.sbuf_tensor("final_normed", [P, TPB, D], F32))
        block = ctx.enter_context(nc.Block(no_gpsimd_drain=True))

        @block.sync
        def _(sp):
            with sp.Fori(0, NB) as c:
                sp.wait_ge(s.d_x, c * TPB + 2 * TPB)
                sp.dma_start(dram.out[bass.ds(c * T, T), :].rearrange("(t p) d -> p t d", p=P),
                             m.x[:, bass.ds(c * TPB, TPB), :]).then_inc(s.stored, 16)
            sp.wait_ge(s.stored, 16 * NB)

        @block.gpsimd
        def _(pool):
            pool.sem_inc(s.d_x, TPB)
            with pool.Fori(0, NB) as c:
                for t in range(TPB):
                    tok = bass.ds(c * TPB + t, 1)
                    wait_apart(pool, s, s.d_yn, c * TPB + t + 1)
                    nc.gpsimd.tensor_tensor(m.x[:, tok, :], m.x[:, tok, :], yn[:, t:t + 1, :], ALU.add).then_inc(s.d_x, 1)

        @block.scalar
        def _(a):
            with a.Fori(0, NB) as c:
                ln_deviation(nc, a, m, s.d_moments, s.d_dev, c)

        @block.vector
        def _(v):
            with v.Fori(0, NB) as c:
                acc = [m.acc[:, bass.ds(c * TPB + t, 1), :] for t in range(TPB)]
                ln_moments(nc, v, s, m, acc, s.d_stats, s.d_moments, c)
                ln_rstd(nc, v, m, s.d_dev, s.d_rstd, c)
                for t in range(TPB):
                    v.wait_ge(s.d_x, c * TPB + t + 1)
                    ln_apply(nc, m, t, yn[:, t:t + 1, :], acc[t]).then_inc(s.d_yn, 1)


class UnitSemaphores:

    def __init__(self, sem, phase):
        self.w_in = [sem(f"{phase}_w_in{b}") for b in range(2)]
        self.split_h = sem(f"{phase}_split_h")
        self.split_l = sem(f"{phase}_split_l")
        self.gate_up = sem(f"{phase}_gate_up")
        self.silu = sem(f"{phase}_silu")
        self.product = sem(f"{phase}_product")
        self.act_h = sem(f"{phase}_act_h")
        self.act_l = sem(f"{phase}_act_l")
        self.down_done = sem(f"{phase}_down_done")
        self.summed = sem(f"{phase}_summed")
        self.lora_in = sem(f"{phase}_lora_in")
        self.low_rank = sem(f"{phase}_low_rank")
        self.folded = sem(f"{phase}_folded")


class Semaphores:
    def __init__(self, sem):
        self.x_in, self.const, self.qkv_w_in, self.rope_in, self.qth_ready, self.qtl_ready = (sem(n) for n in "x_in const qkv_w_in rope_in qth_ready qtl_ready".split())
        self.qkT_out, self.rope_parts, self.q_transposed, self.rot_ready, self.qkv_wh, self.qkv_wl = (sem(n) for n in "qkT_out rope_parts q_transposed rot_ready qkv_wh qkv_wl".split())
        self.a1_moments, self.a1_dev, self.a1_tr, self.a1_xh, self.a1_xl, self.a1_stats = (sem(n) for n in "a1_moments a1_dev a1_tr a1_xh a1_xl a1_stats".split())
        self.a1_rstd, self.a1_xn, self.qkv_done, self.v_ready = (sem(n) for n in "a1_rstd a1_xn qkv_done v_ready".split())
        self.ones_ready, self.ctxT_done, self.maxT_ready, self.exps, self.masked, self.maxT_turned = (sem(n) for n in "ones_ready ctxT_done maxT_ready exps masked maxT_turned".split())
        self.scoresT, self.weighted, self.ctxT_ready, self.v_in, self.row_max, self.ctx_ready = (sem(n) for n in "scoresT weighted ctxT_ready v_in row_max ctx_ready".split())
        self.scores, self.max_high, self.max_low, self.rden = (sem(n) for n in "scores max_high max_low rden".split())
        self.passed, self.wo_in, self.router_pad, self.router_in, self.expert_index, self.o_yn = (sem(n) for n in "passed wo_in router_pad router_in expert_index o_yn".split())
        self.o_x, self.o_tr, self.o_zero, self.o_ct, self.wo_h, self.router_h = (sem(n) for n in "o_x o_tr o_zero o_ct wo_h router_h".split())
        self.o_done, self.o_ch, self.b2_tr, self.b2_h, self.router_done, self.logitsT = (sem(n) for n in "o_done o_ch b2_tr b2_h router_done logitsT".split())
        self.top_gap, self.top_exp = (sem(n) for n in "top_gap top_exp".split())
        self.o_cl, self.wo_l, self.router_l, self.b2_l, self.b2_xn, self.logits_turned = (sem(n) for n in "o_cl wo_l router_l b2_l b2_xn logits_turned".split())
        self.logits, self.best, self.best_at, self.top, self.top_weight, self.one_hot = (sem(n) for n in "logits best best_at top top_weight one_hot".split())
        self.combine = sem("combine")
        self.w12_in, self.w_masked, self.w_product, self.w_high, self.w_low, self.b2_in = (sem(n) for n in "w12_in w_masked w_product w_high w_low b2_in".split())
        self.c1_yn, self.c1_x, self.c1_zero, self.c3_yn, self.c3_x, self.c2_tr = (sem(n) for n in "c1_yn c1_x c1_zero c3_yn c3_x c2_tr".split())
        self.mixed, self.c2_h, self.biased, self.gelu, self.c4_tr, self.c4_h = (sem(n) for n in "mixed c2_h biased gelu c4_tr c4_h".split())
        self.c2_l, self.c4_l, self.c2_xn, self.c4_xn = (sem(n) for n in "c2_l c4_l c2_xn c4_xn".split())
        self.d_x, self.d_yn, self.stored = (sem(n) for n in "d_x d_yn stored".split())
        self.b1_stats, self.b1_moments, self.b1_dev, self.b1_rstd = (sem(n) for n in "b1_stats b1_moments b1_dev b1_rstd".split())
        self.b2_stats, self.b2_moments, self.b2_dev, self.b2_rstd = (sem(n) for n in "b2_stats b2_moments b2_dev b2_rstd".split())
        self.c1_stats, self.c1_moments, self.c1_dev, self.c1_rstd = (sem(n) for n in "c1_stats c1_moments c1_dev c1_rstd".split())
        self.c2_stats, self.c2_moments, self.c2_dev, self.c2_rstd = (sem(n) for n in "c2_stats c2_moments c2_dev c2_rstd".split())
        self.c3_stats, self.c3_moments, self.c3_dev, self.c3_rstd = (sem(n) for n in "c3_stats c3_moments c3_dev c3_rstd".split())
        self.c4_stats, self.c4_moments, self.c4_dev, self.c4_rstd = (sem(n) for n in "c4_stats c4_moments c4_dev c4_rstd".split())
        self.d_stats, self.d_moments, self.d_dev, self.d_rstd = (sem(n) for n in "d_stats d_moments d_dev d_rstd".split())
        self.qs_in, self.max_in = ([sem(f"{n}{b}") for b in range(2)] for n in ("qs_in", "max_in"))
        self.moe, self.ff = UnitSemaphores(sem, "moe"), UnitSemaphores(sem, "ff")


class Memory:

    def __init__(self, sb):
        self.x = sb("x", [P, NT, D])
        self.acc = sb("acc", [P, NT, D])
        self.combine = sb("combine", [P, NT, 32])
        self.ident, self.ident16 = sb("ident", [P, P]), sb("ident16", [P, P], BF16)
        self.causal = sb("causal", [P, P], BF16)
        self.eps, self.zero = sb("eps", [P, 1]), sb("zero", [P, 1])
        self.stats, self.mv = sb("stats", [P, TPB, 6]), sb("mv", [P, TPB, 2])
        self.dev, self.rstd = sb("dev", [P, TPB]), sb("rstd", [P, TPB])


class Dram:

    def __init__(self, nc, ins, out):
        self.x, self.rope, self.mask, self.b2 = ins["x"], ins["rope"], ins["mask"], ins["b2"]
        self.wqT, self.wkT, self.wvT, self.woT = ins["wqT"], ins["wkT"], ins["wvT"], ins["woT"]
        self.routerT, self.moe_gate_up, self.moe_down = ins["routerT"], ins["moe_gate_up"], ins["moe_down"]
        self.w1, self.w2T = ins["w1"], ins["w2T"]
        self.ff_gate_up, self.ff_down, self.lora_unit = ins["ff_gate_up"], ins["ff_down"], ins["lora_unit"]
        self.gate_a, self.up_a, self.down_bT = ins["gate_a"], ins["up_a"], ins["down_bT"]
        self.qkT_h = nc.dram_tensor("qkT_h", [QK, NB * T], F32, kind="Internal").ap()
        self.qkT_l = nc.dram_tensor("qkT_l", [QK, NB * T], F32, kind="Internal").ap()
        self.out = out


def build(nc, ins, out, upto=9):
    with ExitStack() as ctx:
        sem = lambda n: ctx.enter_context(nc.semaphore(n))
        sb = lambda n, shape, dt=F32: ctx.enter_context(nc.sbuf_tensor(n, shape, dt))
        s, m, dram = Semaphores(sem), Memory(sb), Dram(nc, ins, out)
        with nc.sbuf_tensor("v_pad", [P, NT, HKV, HB], F32) as v_pad:
            m.v_pad = v_pad
            const_phase(nc, s, m, dram)
            qkv_phase(nc, s, m, dram)
            if upto > 1:
                attention_phase(nc, s, m, dram)
        if upto > 2:
            with nc.sbuf_tensor("xnh", [P, KD, NB * T], F32R) as m.xnh, nc.sbuf_tensor("xnl", [P, KD, NB * T], F32R) as m.xnl:
                output_phase(nc, s, m, dram)
                if upto > 3:
                    units_phase(nc, s, s.moe, m, dram, "moe", UNITS_MOE, (dram.moe_gate_up, dram.moe_down))
                if upto > 4:
                    mix_phase(nc, s, m, dram)
                if upto > 5:
                    units_phase(nc, s, s.ff, m, dram, "ff", UNITS_FF, (dram.ff_gate_up, dram.ff_down), lora=True)
        if upto > 6:
            final_phase(nc, s, m, dram)







def lay_out(inputs):
    f = lambda k: np.asarray(inputs[k])
    tr = lambda a: np.ascontiguousarray(a.T)
    arrays = {
        "x": f("L0_attn_x").reshape(NB * T, D),
        "wqT": tr(f("L0_attn_Wq")), "wkT": tr(f("L0_attn_Wk")), "wvT": tr(f("L0_attn_Wv")), "woT": tr(f("L0_attn_Wo")),
        "rope": setup_tables(),
        "routerT": tr(f("L0_ffn_gate_w")),
        "w1": f("L1_attn_w1"), "w2T": tr(f("L1_attn_w2")), "mask": f("L1_attn_sparse_mask"),
        "b2": f("L1_attn_b2").reshape(1, D),
        "gate_a": f("L1_ffn_gate_a"), "up_a": f("L1_ffn_up_a"), "down_bT": tr(f("L1_ffn_down_b")),
    }
    shared_up = f("L0_ffn_shared_w_gate_up").reshape(2, NSH, INTER, D).transpose(1, 3, 0, 2).reshape(NSH, D, 2 * INTER)
    shared_down = f("L0_ffn_shared_w_down").T.reshape(NSH, INTER, D)
    arrays["moe_gate_up"] = np.concatenate([f("L0_ffn_w_gate_up").transpose(0, 2, 1), shared_up])
    arrays["moe_down"] = np.concatenate([f("L0_ffn_w_down").transpose(0, 2, 1), shared_down])
    def rows(a):
        out = np.zeros((UNITS_FF * P,) + a.shape[1:], a.dtype)
        out[:FF] = a
        return out.reshape((UNITS_FF, P) + a.shape[1:])
    pair = np.stack([rows(f("L1_ffn_gate_w")), rows(f("L1_ffn_up_w"))], 1)
    arrays["ff_gate_up"] = np.ascontiguousarray(pair.transpose(0, 3, 1, 2)).reshape(UNITS_FF, D, 2 * P)
    arrays["ff_down"] = rows(tr(f("L1_ffn_down_w")))
    lora = np.stack([rows(f("L1_ffn_gate_b")), rows(f("L1_ffn_up_b")), rows(tr(f("L1_ffn_down_a")))], 1)
    arrays["lora_unit"] = np.ascontiguousarray(lora.transpose(0, 3, 1, 2))
    return arrays


def program(nc, shapes, upto=9):
    ins = {n: nc.dram_tensor(f"in_{n}", shape, F32, kind="ExternalInput").ap() for n, shape in shapes.items()}
    out = nc.dram_tensor("out", [NB * T, D], F32, kind="ExternalOutput").ap()
    build(nc, ins, out, upto)


def kernel(**inputs):
    import concourse.bacc as bacc
    from concourse.bass_utils import run_bass_kernel_spmd
    arrays = lay_out(inputs)
    nc = bacc.Bacc("TRN2", target_bir_lowering=False, num_devices=1)
    program(nc, {n: a.shape for n, a in arrays.items()})
    result = run_bass_kernel_spmd(nc, [{f"in_{n}": a for n, a in arrays.items()}], core_ids=[0])
    return result.results[0]["out"].reshape(NB, T, D)
```

```python
from contextlib import ExitStack

import numpy as np
import concourse.bass as bass
from concourse import mybir

F32 = mybir.dt.float32
F32R = mybir.dt.float32r
BF16 = mybir.dt.bfloat16
U32 = mybir.dt.uint32
ALU = mybir.AluOpType
ACT = mybir.ActivationFunctionType
AX_X = mybir.AxisListType.X

P = 128
D = 512
KD = D // P
NB, T = 4, 512
TPB = T // P
NT = NB * TPB
H, HKV, DH = 32, 8, 16
G = H // HKV
QK = (H + HKV) * DH
QKV = QK + HKV * DH
PARTS = 3
STACK = ((0, 0), (1, 0), (2, 0), (0, 1), (1, 1), (0, 2))
HB = 32
NE, INTER = 16, 128
NSH = 4
UNITS_MOE = NE + NSH
FF = 1376
UNITS_FF = -(-FF // P)
RANK = 16
EPS = 1e-5
MASKED = -1.0e30


def setup_tables():
    inv = (1.0 / np.power(np.float32(500000.0), np.arange(0, DH, 2, dtype=np.float32) / np.float32(DH))).astype(np.float32)
    wavelen = (np.float32(2.0 * np.pi) / inv).astype(np.float32)
    lo, hi = 1024 / 4.0, 1024 / 1.0
    inv2 = np.where(wavelen > hi, inv / np.float32(32.0), inv).astype(np.float32)
    smooth = ((np.float32(1024) / wavelen - np.float32(1.0)) / np.float32(3.0)).astype(np.float32)
    smoothed = ((1 - smooth) * inv2 / np.float32(32.0) + smooth * inv2).astype(np.float32)
    medium = ~(wavelen < hi) & ~(wavelen > lo)
    inv2 = np.where(medium, smoothed, inv2).astype(np.float32)
    ang = (np.arange(T, dtype=np.float32)[:, None] * inv2[None, :]).astype(np.float32)
    cos = np.cos(np.concatenate([ang, ang], 1)).astype(np.float32)
    sin = np.sin(np.concatenate([-ang, ang], 1)).astype(np.float32)
    return np.stack([cos, sin], 1)


def const_phase(nc, s, m, dram):
    with nc.Block(no_gpsimd_drain=True) as block:
        @block.sync
        def _(sp):
            for c in range(NB):
                sp.dma_start(m.x[:, c * TPB:(c + 1) * TPB, :],
                             dram.x[c * T:(c + 1) * T, :].rearrange("(t p) d -> p t d", p=P)).then_inc(s.x_in, 16)

        @block.gpsimd
        def _(pool):
            nc.gpsimd.memset(m.ident[:], 0.0).then_inc(s.const, 1)
            nc.gpsimd.memset(m.ident16[:], 0.0).then_inc(s.const, 1)
            nc.gpsimd.memset(m.causal[:], 0.0).then_inc(s.const, 1)
            nc.gpsimd.memset(m.v_pad[:], 0.0).then_inc(s.const, 1)
            nc.gpsimd.memset(m.combine[:], 1.0).then_inc(s.const, 1)
            nc.gpsimd.memset(m.eps[:], EPS).then_inc(s.const, 1)
            nc.gpsimd.memset(m.zero[:], 0.0).then_inc(s.const, 1)
            pool.wait_ge(s.const, 7)
            for tile in (m.ident, m.ident16):
                nc.gpsimd.affine_select(out=tile[:], in_=tile[:], compare_op=ALU.not_equal, fill=1.0, base=0,
                                        pattern=[[-1, P]], channel_multiplier=1).then_inc(s.const, 1)
            nc.gpsimd.affine_select(out=m.causal[:], in_=m.causal[:], compare_op=ALU.is_ge, fill=MASKED, base=0,
                                    pattern=[[-1, P]], channel_multiplier=1).then_inc(s.const, 1)
            nc.gpsimd.memset(m.v_pad[:, :, :, DH:DH + 1], 1.0).then_inc(s.const, 1)
            pool.wait_ge(s.const, CONSTANTS)


CONSTANTS = 11


def wait_apart(eng, s, sem, value):
    eng.wait_ge(sem, value)
    eng.sem_inc(s.passed, 1)


def ln_moments(nc, v, s, m, sources, stats_sem, moments_sem, c):
    for t, src in enumerate(sources):
        nc.vector.bn_stats(m.stats[:, t, :], src).then_inc(stats_sem, 1)
    wait_apart(v, s, stats_sem, c * TPB + TPB)
    for t in range(TPB):
        nc.vector.bn_aggr(m.mv[:, t, :], m.stats[:, t, :]).then_inc(moments_sem, 1)


def ln_deviation(nc, a, m, moments_sem, dev_sem, c):
    a.wait_ge(moments_sem, c * TPB + TPB)
    nc.scalar.activation(m.dev[:], m.mv[:, :, 1], ACT.Sqrt, bias=m.eps[:]).then_inc(dev_sem, 1)


def ln_rstd(nc, v, m, dev_sem, rstd_sem, c):
    v.wait_ge(dev_sem, c + 1)
    nc.vector.reciprocal(m.rstd[:], m.dev[:]).then_inc(rstd_sem, 1)
    v.wait_ge(rstd_sem, c + 1)


def ln_apply(nc, m, t, out, src):
    return nc.vector.tensor_scalar(out, src, m.mv[:, t, 0:1], m.rstd[:, t:t + 1], ALU.subtract, ALU.mult)


def split_product(nc, out, wh, wl, xh, xl, first=True, last=True):
    nc.tensor.matmul(out, wh, xh, start=first, stop=False)
    nc.tensor.matmul(out, wh, xl, start=False, stop=False)
    return nc.tensor.matmul(out, wl, xh, start=False, stop=last)


def qkv_phase(nc, s, m, dram):
    with ExitStack() as ctx:
        sb = lambda n, shape, dt=F32: ctx.enter_context(nc.sbuf_tensor(n, shape, dt))
        ps = lambda n, shape: ctx.enter_context(nc.psum_tensor(n, shape, F32))
        w_raw = sb("qkv_w_raw", [P, KD, QKV])
        wh, wl = sb("qkv_wh", [P, KD, QKV], F32R), sb("qkv_wl", [P, KD, QKV], F32R)
        rope = sb("rope", [P, TPB, 2, DH])
        xn = sb("qkv_xn", [P, TPB, D])
        xh, xl = sb("qkv_xh", [P, 2, KD, P], F32R), sb("qkv_xl", [P, 2, KD, P], F32R)
        by_cos, by_sin = sb("by_cos", [P, 2, QK]), sb("by_sin", [P, 2, QK])
        rot = sb("rotated", [P, 2, QK])
        NQ = QK // P
        parts = sb("qkT_parts", [P, PARTS, NQ, T], BF16)
        rest = sb("qkT_rest", [P, 2, NQ, P])
        ps_t = ps("qkv_ps_t", [P, 2, KD, P])
        ps_qkv = ps("ps_qkv", [P, 2, 2 * 512])
        ps_qt = ps("ps_qt", [P, 2 * 512])
        QK_OUT = 16 * (PARTS * (NQ - 1) + len(STACK))
        block = ctx.enter_context(nc.Block(no_gpsimd_drain=True))

        @block.sync
        def _(sp):
            for src, a, b in ((dram.wqT, 0, D), (dram.wkT, D, QK), (dram.wvT, QK, QKV)):
                sp.dma_start(w_raw[:, :, a:b], src.rearrange("(k p) n -> p k n", p=P)).then_inc(s.qkv_w_in, 16)
            sp.dma_start(rope[:], dram.rope.rearrange("(t p) a d -> p t a d", p=P)).then_inc(s.rope_in, 16)
            sp.sem_inc(s.qkT_out, QK_OUT)
            with sp.Fori(0, NB) as c:
                tok = bass.ds(c * T, T)
                for part, ready in enumerate((s.q_part0, s.q_part1, s.q_part2)):
                    sp.wait_ge(ready, c * TPB + TPB)
                    for j in range(H * DH // P):
                        sp.dma_start(dram.q_parts[j * P // DH:(j + 1) * P // DH, part, :, tok], parts[:, part, j, :]).then_inc(s.qkT_out, 16)
                    for place, (_, k_part) in enumerate(STACK):
                        if k_part == part:
                            sp.dma_start(dram.k_stack[:, place, :, tok], parts[:, part, NQ - 1, :]).then_inc(s.qkT_out, 16)
            sp.wait_ge(s.qkT_out, QK_OUT * (NB + 1))

        @block.gpsimd
        def _(pool):
            def q_third(c, t):
                pool.wait_ge(s.q_part1, c * TPB + t + 1)
                nc.gpsimd.tensor_tensor(parts[:, 2, :, t * P:(t + 1) * P], rest[:, t % 2], parts[:, 1, :, t * P:(t + 1) * P],
                                        ALU.subtract).then_inc(s.q_part2, 1)

            pool.sem_inc(s.rot_ready, 2)
            with pool.Fori(0, NB) as c:
                for t in range(TPB):
                    pool.wait_ge(s.rope_parts, c * TPB + t + 1)
                    pool.wait_ge(s.q_transposed, c * TPB + t + 1)
                    nc.gpsimd.tensor_tensor(rot[:, t % 2, :], by_cos[:, t % 2, :], by_sin[:, t % 2, :],
                                            ALU.add).then_inc(s.rot_ready, 1)
                    if t:
                        q_third(c, t - 1)
                q_third(c, TPB - 1)

        @block.scalar
        def _(a):
            a.sem_inc(s.v_ready, 2)
            a.wait_ge(s.qkv_w_in, 48)
            nc.scalar.copy(wh[:], w_raw[:]).then_inc(s.qkv_wh, 1)
            with a.Fori(0, NB) as c:
                ln_deviation(nc, a, m, s.a1_moments, s.a1_dev, c)

                def q_high(t):
                    a.wait_ge(s.q_transposed, c * TPB + t + 3)
                    if t == 0:
                        a.wait_ge(s.qkT_out, (c + 1) * QK_OUT)
                    nc.scalar.copy(parts[:, 0, :, t * P:(t + 1) * P], ps_qt[:, 0:QK].rearrange("p (j n) -> p j n", n=P)).then_inc(s.q_part0, 1)

                def q_second(t):
                    a.wait_ge(s.q_rest, c * TPB + t + 1 + 1)
                    nc.scalar.copy(parts[:, 1, :, t * P:(t + 1) * P], rest[:, t % 2]).then_inc(s.q_part1, 1)

                for t in range(TPB):
                    b = t % 2
                    a.wait_ge(s.a1_tr, c * TPB + t + TPB + 1)
                    a.wait_ge(s.qkv_done, c * TPB + t + 1)
                    nc.scalar.copy(xh[:, b], ps_t[:, b]).then_inc(s.a1_xh, 1)
                    if t > 1:
                        q_second(t - 2)
                    if t:
                        q_high(t - 1)
                    a.wait_ge(s.rope_parts, c * TPB + t + 1)
                    nc.scalar.copy(m.v_pad[:, bass.ds(c * TPB + t, 1), :, 0:DH],
                                   ps_qkv[:, b, QK:QKV].rearrange("p (o g d) -> p o g d", o=1, d=DH)).then_inc(s.v_ready, 1)
                q_second(TPB - 2)
                q_high(TPB - 1)
                q_second(TPB - 1)

        @block.vector
        def _(v):
            v.sem_inc(s.q_rest, 1)
            v.sem_inc(s.a1_xl, 2)
            v.wait_ge(s.qkv_wh, 1)
            nc.vector.tensor_tensor(wl[:], w_raw[:], wh[:], ALU.subtract).then_inc(s.qkv_wl, 1)
            v.wait_ge(s.rope_in, 16)
            with v.Fori(0, NB) as c:
                wait_apart(v, s, s.x_in, c * 16 + 16)
                ln_moments(nc, v, s, m, [m.x[:, bass.ds(c * TPB + t, 1), :] for t in range(TPB)], s.a1_stats, s.a1_moments, c)
                ln_rstd(nc, v, m, s.a1_dev, s.a1_rstd, c)
                for t in range(TPB):
                    v.wait_ge(s.a1_tr, c * TPB + t + 1)
                    ln_apply(nc, m, t, xn[:, t:t + 1, :], m.x[:, bass.ds(c * TPB + t, 1), :]).then_inc(s.a1_xn, 1)

                def q_remainder(t):
                    v.wait_ge(s.q_part0, c * TPB + t + 1)
                    if t > 1:
                        v.wait_ge(s.q_part2, c * TPB + t - 1)
                    nc.vector.tensor_tensor(rest[:, t % 2], ps_qt[:, 0:QK].rearrange("p (j n) -> p j n", n=P),
                                            parts[:, 0, :, t * P:(t + 1) * P], ALU.subtract).then_inc(s.q_rest, 1)

                for t in range(TPB):
                    b = t % 2
                    v.wait_ge(s.a1_xh, c * TPB + t + 1)
                    nc.vector.tensor_tensor(xl[:, b], ps_t[:, b], xh[:, b], ALU.subtract).then_inc(s.a1_xl, 1)
                    if t:
                        q_remainder(t - 1)
                    v.wait_ge(s.qkv_done, c * TPB + t + 3)
                    v.wait_ge(s.rot_ready, c * TPB + t + 1)
                    heads = ps_qkv[:, b, 0:QK].rearrange("p (h d) -> p h d", d=DH)
                    cosv = rope[:, t, 0, :].unsqueeze(1).to_broadcast([P, H + HKV, DH])
                    sinv = rope[:, t, 1, :].unsqueeze(1).to_broadcast([P, H + HKV, DH])
                    co = by_cos[:, b, :].rearrange("p (h d) -> p h d", d=DH)
                    si = by_sin[:, b, :].rearrange("p (h d) -> p h d", d=DH)
                    nc.vector.tensor_tensor(co, heads, cosv, ALU.mult)
                    h2 = DH // 2
                    nc.vector.tensor_tensor(si[:, :, 0:h2], heads[:, :, h2:DH], sinv[:, :, 0:h2], ALU.mult)
                    nc.vector.tensor_tensor(si[:, :, h2:DH], heads[:, :, 0:h2], sinv[:, :, h2:DH], ALU.mult).then_inc(s.rope_parts, 1)
                q_remainder(TPB - 1)

        @block.tensor
        def _(pe):
            pe.sem_inc(s.a1_tr, TPB)
            pe.sem_inc(s.qkv_done, 2)
            pe.sem_inc(s.q_transposed, 2)
            with pe.Fori(0, NB) as c:
                def q_transpose(t):
                    pe.wait_ge(s.rot_ready, c * TPB + t + 3)
                    pe.wait_ge(s.q_rest, c * TPB + t + 1)
                    for j in range(NQ):
                        last = nc.tensor.transpose(ps_qt[:, j * P:(j + 1) * P], rot[:, t % 2, j * P:(j + 1) * P], m.ident[:])
                    last.then_inc(s.q_transposed, 1)

                for t in range(TPB):
                    b = t % 2
                    pe.wait_ge(s.a1_xn, c * TPB + t + 1)
                    pe.wait_ge(s.a1_xl, c * TPB + t + 1)
                    for k in range(KD):
                        last = nc.tensor.transpose(ps_t[:, b, k, :], xn[:, t, k * P:(k + 1) * P], m.ident[:])
                    last.then_inc(s.a1_tr, 1)
                    if t:
                        q_transpose(t - 1)
                    if t == 0:
                        pe.wait_ge(s.qkv_wl, 1)
                    pe.wait_ge(s.a1_xl, c * TPB + t + 3)
                    pe.wait_ge(s.v_ready, c * TPB + t + 1)
                    for lo, hi in ((0, D), (D, QKV)):
                        for k in range(KD):
                            last = split_product(nc, ps_qkv[:, b, lo:hi], xh[:, b, k, :], xl[:, b, k, :],
                                                 wh[:, k, lo:hi], wl[:, k, lo:hi], k == 0, k == KD - 1)
                    last.then_inc(s.qkv_done, 1)
                q_transpose(TPB - 1)


def attention_phase(nc, s, m, dram):
    KS, KM = len(STACK) * DH, len(STACK) * DH + 2
    STEPS = NB * HKV
    BUF = 3
    with ExitStack() as ctx:
        sb = lambda n, shape, dt=F32: ctx.enter_context(nc.sbuf_tensor(n, shape, dt))
        ps = lambda n, shape: ctx.enter_context(nc.psum_tensor(n, shape, F32))
        qs = [sb(f"q_stack{i}", [KM, G, T], BF16) for i in range(BUF)]
        ks = [sb(f"k_stack{i}", [KM, T], BF16) for i in range(BUF)]
        vs = [sb(f"v_step{i}", [P, TPB, HB]) for i in range(BUF)]
        row_max = [sb(f"row_max{i}", [P, G * TPB]) for i in range(BUF)]
        max_hl = [sb(f"max_hl{i}", [P, 2 * G * TPB], BF16) for i in range(BUF)]
        maxT = [sb(f"maxT{i}", [2 * G * TPB, P], BF16) for i in range(BUF)]
        pT = [sb(f"weightsT{i}", [P, G, T]) for i in range(2)]
        ctxT = [sb(f"ctxT{i}", [P, T]) for i in range(BUF)]
        rden = [sb(f"rden{i}", [P, TPB, G]) for i in range(BUF)]
        ps_s = ps("ps_scores", [P, 2, 2, T])
        ps_st = ps("ps_scoresT", [P, 2, T])
        ps_o = ps("ps_ctxT", [P, T])
        ps_x = ps("ps_turned", [P, T])
        block = ctx.enter_context(nc.Block(no_gpsimd_drain=True))
        RG, CG = 2 * TPB, G * TPB

        def steps(eng, first, both, last):
            first()
            with eng.Fori(0, (STEPS - 2) // BUF) as i:
                for o in range(1, BUF + 1):
                    both(i * BUF + o, o % BUF, o - 1, i + o // BUF)
            assert STEPS % BUF == 2
            both(STEPS - 1, 1, 0, STEPS // BUF)
            last()

        @block.sync
        def _(sp):
            for b in range(BUF):
                sp.sem_inc(s.max_in[b], 32)
            sp.wait_ge(s.ones_ready, BUF)

            def load(n, b):
                seq, g = n // HKV, n % HKV
                tok = bass.ds(seq * T, T)
                row = 0
                for parts in (3, 2, 1):
                    sp.dma_start(qs[b][row:row + parts * DH, :, :],
                                 dram.q_parts[bass.ds(g * G, G), 0:parts, :, tok].rearrange("h a d t -> (a d) h t")).then_inc(s.qs_in[b], 16)
                    row += parts * DH
                sp.dma_start(ks[b][0:KS, :], dram.k_stack[bass.ds(g, 1), :, :, tok].rearrange("o a d t -> (o a d) t")).then_inc(s.qs_in[b], 16)

            def maxima(n, b):
                sp.wait_ge(s.maxT_ready, n + 1)
                for part in range(2):
                    sp.dma_start(qs[b][KS + part:KS + part + 1, :, :],
                                 maxT[b][part * G * TPB:(part + 1) * G * TPB, :]).then_inc(s.max_in[b], 16)

            def both(n, b):
                sp.wait_ge(s.ctxT_done, n)
                load(n + 1, (b + 1) % BUF)
                maxima(n, b)

            for n in range(BUF - 1):
                load(n, n)
            maxima(0, 0)
            with sp.Fori(0, (STEPS - 2) // BUF) as i:
                for o in range(1, BUF + 1):
                    both(i * BUF + o, o % BUF)
            maxima(STEPS - 1, 1)

        @block.gpsimd
        def _(pool):
            for b in range(BUF):
                nc.gpsimd.memset(ks[b][:], 1.0).then_inc(s.ones_ready, 1)

            def mask(n):
                for j in range(TPB):
                    wait_apart(pool, s, s.exps, n * CG + (j + 1) * G + 2)
                    nc.gpsimd.affine_select(out=pT[j % 2][:, :, 0:P], in_=pT[j % 2][:, :, 0:P], compare_op=ALU.is_ge,
                                            fill=0.0, base=0, pattern=[[0, G], [1, P]], channel_multiplier=-1).then_inc(s.masked, 1)

            with pool.Fori(0, STEPS) as n:
                mask(n)

        @block.scalar
        def _(a):
            nc.scalar.preload_act_table(ACT.Exp)
            a.sem_inc(s.exps, 2)
            a.sem_inc(s.ctxT_ready, 1)

            def max_copy(n, b, used):
                a.wait_ge(s.maxT_turned, n + 1)
                a.wait_ge(s.max_in[b], used * 32 + 32)
                nc.scalar.copy(maxT[b][:], ps_x.bitcast(BF16)[0:2 * G * TPB, 0:P]).then_inc(s.maxT_ready, 1)

            def exps(n):
                for j in range(TPB):
                    for h in range(G):
                        k = j * G + h
                        a.wait_ge(s.scoresT, n * CG + k + 1)
                        if h == 0:
                            a.wait_ge(s.weighted, n * TPB + j + 2 - 1)
                        w = T - j * P
                        nc.scalar.activation(pT[j % 2][:, h, 0:w], ps_st[:, k % 2, 0:w], ACT.Exp, scale=DH ** -0.5).then_inc(s.exps, 1)

            def ctx_copy(n, b):
                a.wait_ge(s.weighted, n * TPB + TPB + 2)
                nc.scalar.copy(ctxT[b][:], ps_o[:]).then_inc(s.ctxT_ready, 1)

            def v_copy(n, b):
                if not (isinstance(n, int) and n == 0):
                    a.wait_ge(s.ctxT_done, n)
                seq, g = n // HKV, n % HKV
                nc.scalar.copy(vs[b][:], m.v_pad[:, bass.ds(seq * TPB, TPB), bass.ds(g, 1), :].rearrange("p t o d -> p t (o d)")).then_inc(s.v_in, 1)

            def both(n, b, before, used):
                v_copy(n, b)
                exps(n - 1)
                max_copy(n, b, used)
                ctx_copy(n - 1, before)

            def first():
                v_copy(0, 0)
                max_copy(0, 0, 0)

            def last():
                exps(STEPS - 1)
                ctx_copy(STEPS - 1, 1)

            steps(a, first, both, last)

        @block.vector
        def _(v):
            v.sem_inc(s.row_max, 2)
            v.sem_inc(s.ctx_ready, 1)

            def maxima(n, b):
                for k in range(RG):
                        i, hp = TPB - 1 - k // 2, k % 2
                        v.wait_ge(s.scores, n * RG + k + 1)
                        nc.vector.tensor_reduce(row_max[b][:, 2 * hp * TPB + i:2 * hp * TPB + i + TPB + 1:TPB],
                                                ps_s[:, k % 2, :, 0:(i + 1) * P], AX_X, ALU.max, negate=True).then_inc(s.row_max, 1)
                half = G * TPB
                v.wait_ge(s.row_max, n * RG + RG + 2)
                nc.vector.tensor_copy(max_hl[b][:, 0:half], row_max[b][:]).then_inc(s.max_high, 1)
                v.wait_ge(s.max_high, n + 1)
                nc.vector.tensor_tensor(max_hl[b][:, half:2 * half], row_max[b][:], max_hl[b][:, 0:half], ALU.subtract).then_inc(s.max_low, 1)

            def normalize(n, b):
                seq, g = n // HKV, n % HKV
                v.wait_ge(s.ctxT_done, n + 2)
                blocks = ps_x[:].rearrange("p (i h c) -> p i h c", i=TPB, h=G)
                nc.vector.reciprocal(rden[b][:], blocks[:, :, :, DH]).then_inc(s.rden, 1)
                v.wait_ge(s.rden, n + 1)
                for i in range(TPB):
                    ins = nc.vector.tensor_tensor(m.acc[:, bass.ds(seq * TPB + i, 1), bass.ds(g * (G * DH), G * DH)].rearrange("p o (h d) -> p (o h) d", d=DH),
                                                  blocks[:, i, :, 0:DH], rden[b][:, i, :].unsqueeze(2).to_broadcast([P, G, DH]), ALU.mult)
                ins.then_inc(s.ctx_ready, 1)

            def both(n, b, before, used):
                maxima(n, b)
                normalize(n - 1, before)

            steps(v, lambda: maxima(0, 0), both, lambda: normalize(STEPS - 1, 1))

        @block.tensor
        def _(pe):
            pe.sem_inc(s.weighted, 2)
            pe.sem_inc(s.ctxT_done, 1)

            def scores(n, b, used, k):
                i, hp = TPB - 1 - k // 2, k % 2
                if k == 0:
                    pe.wait_ge(s.qs_in[b], used * 64 + 64)
                pe.wait_ge(s.row_max, n * RG + k + 1)
                for o in range(2):
                    h = 2 * hp + o
                    nc.tensor.matmul(ps_s[:, k % 2, o, 0:(i + 1) * P], qs[b][0:KS, h, i * P:(i + 1) * P], ks[b][0:KS, 0:(i + 1) * P], start=True, stop=False)
                    last = nc.tensor.matmul(ps_s[:, k % 2, o, i * P:(i + 1) * P], m.ident16[:], m.causal[:], start=False, stop=True)
                last.then_inc(s.scores, 1)

            def turn_maxima(n, b):
                pe.wait_ge(s.max_low, n + 1)
                if not (isinstance(n, int) and n == 0):
                    pe.wait_ge(s.ctx_ready, n)
                nc.tensor.transpose(ps_x.bitcast(BF16)[0:2 * G * TPB, 0:P], max_hl[b][:], m.ident16[:]).then_inc(s.maxT_turned, 1)

            def scoresT(n, b, used, k):
                j, h = k // G, k % G
                if k == 0:
                    pe.wait_ge(s.max_in[b], used * 32 + 64)
                    pe.wait_ge(s.v_in, n + 1)
                pe.wait_ge(s.exps, n * CG + k + 1)
                nc.tensor.matmul(ps_st[:, k % 2, 0:T - j * P], ks[b][0:KM, j * P:(j + 1) * P], qs[b][0:KM, h, j * P:T], start=True, stop=True).then_inc(s.scoresT, 1)

            def weighted(n, b, j):
                pe.wait_ge(s.masked, n * TPB + j + 1)
                if j == 0:
                    pe.wait_ge(s.ctxT_ready, n + 1)
                for h in range(G):
                    last = nc.tensor.matmul(ps_o[h * HB:(h + 1) * HB, j * P:T], vs[b][:, j, :], pT[j % 2][:, h, 0:T - j * P],
                                            start=j == 0, stop=j == TPB - 1)
                last.then_inc(s.weighted, 1)

            def turn_context(n, b, turned):
                pe.wait_ge(s.maxT_ready, turned)
                pe.wait_ge(s.ctx_ready, n + 1)
                pe.wait_ge(s.ctxT_ready, n + 2)
                for i in range(TPB):
                    last = nc.tensor.transpose(ps_x[:, i * P:(i + 1) * P], ctxT[b][:, i * P:(i + 1) * P], m.ident[:])
                last.then_inc(s.ctxT_done, 1)

            def both(n, b, before, used):
                used_before = used - (1 if b == 0 else 0)
                for j in range(TPB):
                    for o in range(2):
                        scores(n, b, used, 2 * j + o)
                        scoresT(n - 1, before, used_before, j * G + 2 * o)
                        scoresT(n - 1, before, used_before, j * G + 2 * o + 1)
                    if j:
                        weighted(n - 1, before, j - 1)
                turn_maxima(n, b)
                weighted(n - 1, before, TPB - 1)
                turn_context(n - 1, before, n + 1)

            def first():
                for k in range(RG):
                    scores(0, 0, 0, k)
                turn_maxima(0, 0)

            def last():
                n = STEPS - 1
                for j in range(TPB):
                    for h in range(G):
                        scoresT(n, 1, STEPS // BUF, j * G + h)
                    if j:
                        weighted(n, 1, j - 1)
                weighted(n, 1, TPB - 1)
                turn_context(n, 1, n + 1)

            steps(pe, first, both, last)


def output_phase(nc, s, m, dram):
    with ExitStack() as ctx:
        sb = lambda n, shape, dt=F32: ctx.enter_context(nc.sbuf_tensor(n, shape, dt))
        ps = lambda n, shape: ctx.enter_context(nc.psum_tensor(n, shape, F32))
        w_raw = sb("wo_raw", [P, KD, D])
        wh, wl = sb("wo_h", [P, KD, D], F32R), sb("wo_l", [P, KD, D], F32R)
        g_raw = sb("router_raw", [P, KD, P])
        gh, gl = sb("router_h", [P, KD, P], F32R), sb("router_l", [P, KD, P], F32R)
        ch, cl = sb("ctx_h", [P, 2, KD, P], F32R), sb("ctx_l", [P, 2, KD, P], F32R)
        ct = sb("ctx_tiles", [P, TPB, D])
        yn = sb("o_normed", [P, TPB, D])
        xn = sb("o_xn", [P, TPB, D])
        logitsT = sb("logitsT", [NE, T])
        logits = sb("logits", [P, TPB, NE])
        best, best_at = sb("best", [P, TPB, 8]), sb("best_at", [P, TPB, 8], U32)
        top, top_at = sb("top", [P, NT, 2]), sb("top_at", [P, NT, 2])
        gap, wgt = sb("top_gap", [P, NT]), sb("top_weight", [P, 3, NT])
        expert, one_hot = sb("expert_index", [P, NE]), sb("one_hot", [P, 2, NT, NE])
        ps_t = ps("o_ps_t", [P, 2, KD, P])
        ps_o = ps("o_ps", [P, TPB, D])
        ps_g = ps("o_ps_g", [P, T])
        ps_l = ps("o_ps_l", [P, T])
        block = ctx.enter_context(nc.Block(no_gpsimd_drain=True))

        @block.sync
        def _(sp):
            sp.dma_start(w_raw[:], dram.woT.rearrange("(k p) n -> p k n", p=P)).then_inc(s.wo_in, 16)
            sp.wait_ge(s.router_pad, 1)
            sp.dma_start(g_raw[:, :, 0:NE], dram.routerT.rearrange("(k p) n -> p k n", p=P)).then_inc(s.router_in, 16)

        @block.gpsimd
        def _(pool):
            nc.gpsimd.memset(g_raw[:], 0.0).then_inc(s.router_pad, 1)
            nc.gpsimd.iota(expert[:], [[1, NE]], base=0, channel_multiplier=0, allow_small_or_imprecise_dtypes=True).then_inc(s.expert_index, 1)
            with pool.Fori(0, NB) as c:
                for t in range(TPB):
                    tok = bass.ds(c * TPB + t, 1)
                    wait_apart(pool, s, s.o_tr, c * TPB + t + 1)
                    nc.gpsimd.tensor_copy(ct[:, t:t + 1, :], m.acc[:, tok, :]).then_inc(s.o_ct, 1)
                    wait_apart(pool, s, s.o_ct, c * TPB + t + 1)
                    nc.gpsimd.tensor_copy(m.acc[:, tok, :], m.zero[:, 0:1].unsqueeze(1).to_broadcast([P, 1, D])).then_inc(s.o_zero, 1)
                for t in range(TPB):
                    tok = bass.ds(c * TPB + t, 1)
                    wait_apart(pool, s, s.o_yn, c * TPB + t + 1 + TPB)
                    nc.gpsimd.tensor_tensor(m.x[:, tok, :], m.x[:, tok, :], yn[:, t:t + 1, :], ALU.add).then_inc(s.o_x, 1)
            pool.wait_ge(s.o_zero, NT)

        @block.scalar
        def _(a):
            a.sem_inc(s.logitsT, 1)
            a.wait_ge(s.wo_in, 16)
            nc.scalar.copy(wh[:], w_raw[:]).then_inc(s.wo_h, 1)
            a.wait_ge(s.router_in, 16)
            nc.scalar.copy(gh[:], g_raw[:]).then_inc(s.router_h, 1)
            with a.Fori(0, NB) as c:
                for t in range(TPB):
                    a.wait_ge(s.o_tr, c * TPB + t + 1 + TPB)
                    a.wait_ge(s.o_done, c * TPB + t + 1)
                    nc.scalar.copy(ch[:, t % 2], ps_t[:, t % 2]).then_inc(s.o_ch, 1)
                ln_deviation(nc, a, m, s.b1_moments, s.b1_dev, c)
                ln_deviation(nc, a, m, s.b2_moments, s.b2_dev, c)
                for t in range(TPB):
                    a.wait_ge(s.b2_tr, c * TPB + t + 1)
                    nc.scalar.copy(m.xnh[:, :, bass.ds(c * T + t * P, P)], ps_t[:, t % 2]).then_inc(s.b2_h, 1)
                a.wait_ge(s.router_done, c + 1)
                nc.scalar.copy(logitsT[:], ps_g[0:NE, :]).then_inc(s.logitsT, 1)
            a.wait_ge(s.top_gap, 1)
            nc.scalar.activation(wgt[:, 0, :], gap[:], ACT.Exp).then_inc(s.top_exp, 1)

        @block.vector
        def _(v):
            v.sem_inc(s.o_cl, 2)
            v.sem_inc(s.b2_l, 1)
            v.sem_inc(s.o_yn, TPB)
            v.sem_inc(s.logits, 1)
            v.wait_ge(s.wo_h, 1)
            nc.vector.tensor_tensor(wl[:], w_raw[:], wh[:], ALU.subtract).then_inc(s.wo_l, 1)
            v.wait_ge(s.router_h, 1)
            nc.vector.tensor_tensor(gl[:], g_raw[:], gh[:], ALU.subtract).then_inc(s.router_l, 1)
            with v.Fori(0, NB) as c:
                for t in range(TPB):
                    v.wait_ge(s.o_ch, c * TPB + t + 1)
                    nc.vector.tensor_tensor(cl[:, t % 2], ps_t[:, t % 2], ch[:, t % 2], ALU.subtract).then_inc(s.o_cl, 1)
                v.wait_ge(s.o_done, c * TPB + TPB + 2)
                ln_moments(nc, v, s, m, [ps_o[:, t, :] for t in range(TPB)], s.b1_stats, s.b1_moments, c)
                ln_rstd(nc, v, m, s.b1_dev, s.b1_rstd, c)
                for t in range(TPB):
                    ln_apply(nc, m, t, yn[:, t, :], ps_o[:, t, :]).then_inc(s.o_yn, 1)
                v.wait_ge(s.o_x, c * TPB + TPB)
                ln_moments(nc, v, s, m, [m.x[:, bass.ds(c * TPB + t, 1), :] for t in range(TPB)], s.b2_stats, s.b2_moments, c)
                ln_rstd(nc, v, m, s.b2_dev, s.b2_rstd, c)
                for t in range(TPB):
                    ln_apply(nc, m, t, xn[:, t:t + 1, :], m.x[:, bass.ds(c * TPB + t, 1), :]).then_inc(s.b2_xn, 1)
                for t in range(TPB):
                    cols = bass.ds(c * T + t * P, P)
                    v.wait_ge(s.b2_h, c * TPB + t + 1)
                    nc.vector.tensor_tensor(m.xnl[:, :, cols], ps_t[:, t % 2], m.xnh[:, :, cols], ALU.subtract).then_inc(s.b2_l, 1)
                v.wait_ge(s.logits_turned, c + 1)
                nc.vector.tensor_copy(logits[:], ps_l[:, 0:TPB * NE].rearrange("p (t e) -> p t e", e=NE)).then_inc(s.logits, 1)
                wait_apart(v, s, s.logits, c + 2)
                for t in range(TPB):
                    nc.vector.max(best[:, t, :], logits[:, t, :]).then_inc(s.best, 1)
                wait_apart(v, s, s.best, c * TPB + TPB)
                for t in range(TPB):
                    nc.vector.max_index(best_at[:, t, :], best[:, t, :], logits[:, t, :]).then_inc(s.best_at, 1)
                v.wait_ge(s.best_at, c * TPB + TPB)
                nc.vector.tensor_copy(top[:, bass.ds(c * TPB, TPB), :], best[:, :, 0:2]).then_inc(s.top, 1)
                nc.vector.tensor_copy(top_at[:, bass.ds(c * TPB, TPB), :], best_at[:, :, 0:2]).then_inc(s.top, 1)
            v.wait_ge(s.top, 2 * NB)
            nc.vector.tensor_tensor(gap[:], top[:, :, 1], top[:, :, 0], ALU.subtract).then_inc(s.top_gap, 1)
            v.wait_ge(s.top_exp, 1)
            nc.vector.tensor_scalar_add(wgt[:, 1, :], wgt[:, 0, :], 1.0).then_inc(s.top_weight, 1)
            v.wait_ge(s.top_weight, 1)
            nc.vector.reciprocal(wgt[:, 1, :], wgt[:, 1, :]).then_inc(s.top_weight, 1)
            v.wait_ge(s.top_weight, 2)
            nc.vector.tensor_tensor(wgt[:, 2, :], wgt[:, 0, :], wgt[:, 1, :], ALU.mult).then_inc(s.top_weight, 1)
            v.wait_ge(s.top_weight, 3)
            v.wait_ge(s.expert_index, 1)
            for r in range(2):
                nc.vector.tensor_tensor(one_hot[:, r], expert[:].unsqueeze(1).to_broadcast([P, NT, NE]),
                                        top_at[:, :, r].unsqueeze(2).to_broadcast([P, NT, NE]), ALU.is_equal).then_inc(s.one_hot, 1)
            v.wait_ge(s.one_hot, 2)
            for r in range(2):
                nc.vector.tensor_tensor(one_hot[:, r], one_hot[:, r], wgt[:, 1 + r, :].unsqueeze(2).to_broadcast([P, NT, NE]), ALU.mult).then_inc(s.one_hot, 1)
            v.wait_ge(s.one_hot, 4)
            nc.vector.tensor_tensor(m.combine[:, :, 0:NE], one_hot[:, 0], one_hot[:, 1], ALU.add).then_inc(s.combine, 1)
            v.wait_ge(s.combine, 1)

        @block.tensor
        def _(pe):
            pe.sem_inc(s.o_done, 2)
            pe.sem_inc(s.o_tr, TPB)
            pe.wait_ge(s.wo_l, 1)
            pe.wait_ge(s.router_l, 1)
            with pe.Fori(0, NB) as c:
                for t in range(TPB):
                    b = t % 2
                    pe.wait_ge(s.o_ct, c * TPB + t + 1)
                    pe.wait_ge(s.o_cl, c * TPB + t + 1)
                    if t < 2:
                        pe.wait_ge(s.b2_l, c * TPB + 1)
                    for k in range(KD):
                        last = nc.tensor.transpose(ps_t[:, b, k, :], ct[:, t, k * P:(k + 1) * P], m.ident[:])
                    last.then_inc(s.o_tr, 1)
                    pe.wait_ge(s.o_cl, c * TPB + t + 3)
                    if t == 0:
                        pe.wait_ge(s.o_yn, c * TPB + TPB)
                    for k in range(KD):
                        last = split_product(nc, ps_o[:, t, :], ch[:, b, k, :], cl[:, b, k, :], wh[:, k, :], wl[:, k, :], k == 0, k == KD - 1)
                    last.then_inc(s.o_done, 1)
                for t in range(TPB):
                    b = t % 2
                    pe.wait_ge(s.b2_xn, c * TPB + t + 1)
                    if t >= 2:
                        pe.wait_ge(s.b2_l, c * TPB + t)
                    for k in range(KD):
                        last = nc.tensor.transpose(ps_t[:, b, k, :], xn[:, t, k * P:(k + 1) * P], m.ident[:])
                    last.then_inc(s.b2_tr, 1)
                pe.wait_ge(s.b2_l, c * TPB + TPB + 1)
                pe.wait_ge(s.logitsT, c + 1)
                for k in range(KD):
                    last = split_product(nc, ps_g[:], gh[:, k, :], gl[:, k, :], m.xnh[:, k, bass.ds(c * T, T)], m.xnl[:, k, bass.ds(c * T, T)], k == 0, k == KD - 1)
                last.then_inc(s.router_done, 1)
                pe.wait_ge(s.logitsT, c + 2)
                wait_apart(pe, s, s.logits, c + 1)
                for t in range(TPB):
                    last = nc.tensor.transpose(ps_l[:, t * NE:(t + 1) * NE], logitsT[:, t * P:(t + 1) * P], m.ident[0:NE, 0:NE])
                last.then_inc(s.logits_turned, 1)


def units_phase(nc, s, q, m, dram, name, units, up_down, lora=None):
    STEPS = units * NB
    with ExitStack() as ctx:
        sb = lambda n, shape, dt=F32: ctx.enter_context(nc.sbuf_tensor(f"{name}_{n}", shape, dt))
        ps = lambda n, shape: ctx.enter_context(nc.psum_tensor(f"{name}_{n}", shape, F32))
        NW = KD * 2 * P + D
        w_raw = [sb(f"w_raw{i}", [P, NW]) for i in range(2)]
        wh = [sb(f"wh{i}", [P, NW], F32R) for i in range(2)]
        wl = [sb(f"wl{i}", [P, NW], F32R) for i in range(2)]
        silu = [sb(f"silu{i}", [P, T]) for i in range(2)]
        act = [sb(f"act{i}", [P, T]) for i in range(2)]
        acth = [sb(f"acth{i}", [P, T], F32R) for i in range(2)]
        actl = [sb(f"actl{i}", [P, T], F32R) for i in range(2)]
        if lora:
            la = sb("lora_a", [RANK, 2, D])
            lb = sb("lora_b", [RANK, D])
            lu = [sb(f"lora_unit{i}", [RANK, 3, P]) for i in range(2)]
        ps_g = ps("ps_gate", [P, 2, T])
        ps_u = ps("ps_up", [P, 2, T])
        ps_d = ps("ps_down", [P, TPB, D])
        block = ctx.enter_context(nc.Block(no_gpsimd_drain=True))
        gate_up = lambda w, k, half: w[:, k * 2 * P + half * P:k * 2 * P + (half + 1) * P]
        down = lambda w: w[:, KD * 2 * P:NW]

        def unit_loop(eng, unit):
            unit(0, 0, False)
            with eng.Fori(0, (units - 1) // 2 - units % 2) as i:
                unit(i * 2 + 1, 1, False)
                unit(i * 2 + 2, 0, False)
            if units % 2:
                unit(units - 2, 1, False)
            unit(units - 1, (units - 1) % 2, True)

        @block.sync
        def _(sp):
            if lora:
                for i, src in enumerate((dram.gate_a, dram.up_a)):
                    sp.dma_start(la[:, i, :], src).then_inc(q.lora_in, 16)
                sp.dma_start(lb[:], dram.down_bT).then_inc(q.lora_in, 16)

            def load(u, b):
                if not (isinstance(u, int) and u < 2):
                    sp.wait_ge(q.split_l, u - 1)
                src_u, src_d = up_down
                one = bass.ds(u, 1)
                sp.dma_start(w_raw[b][:, 0:KD * 2 * P].rearrange("p (k n) -> p k n", k=KD),
                             src_u[one].rearrange("u (k p) n -> p (u k) n", p=P)).then_inc(q.w_in[b], 16)
                sp.dma_start(down(w_raw[b]), src_d[one].rearrange("u p n -> p (u n)")).then_inc(q.w_in[b], 16)
                if lora:
                    sp.dma_start(lu[b][:], dram.lora_unit[one].rearrange("u r a n -> r (u a) n")).then_inc(q.w_in[b], 16)

            load(0, 0)
            load(1, 1)
            with sp.Fori(0, (units - 2) // 2) as i:
                load(i * 2 + 2, 0)
                load(i * 2 + 3, 1)
            if units % 2:
                load(units - 1, 0)

        W_IN = 48 if lora else 32

        def split_high(a, u, b):
            if lora:
                a.wait_ge(q.folded, u + 1)
            else:
                a.wait_ge(q.w_in[b], (u // 2) * W_IN + W_IN)
            if not (isinstance(u, int) and u < 2):
                a.wait_ge(q.down_done, (u - 1) * STEP_D)
            nc.scalar.copy(wh[b][:], w_raw[b][:]).then_inc(q.split_h, 1)

        STEP_D = NB * TPB

        @block.scalar
        def _(a):
            def unit(u, b, tail):
                for c in range(NB):
                    a.wait_ge(q.gate_up, u * NB + c + 1)
                    nc.scalar.activation(silu[c % 2][:], ps_g[:, c % 2, :], ACT.Silu).then_inc(q.silu, 1)
                    a.wait_ge(q.product, u * NB + c + 1 + 2)
                    if not (isinstance(u, int) and u == 0 and c < 2):
                        a.wait_ge(q.down_done, (u * NB + c - 1) * TPB)
                    nc.scalar.copy(acth[c % 2][:], act[c % 2][:]).then_inc(q.act_h, 1)
                    if c == 1 and not tail:
                        split_high(a, u + 1, 1 - b)
            split_high(a, 0, 0)
            unit_loop(a, unit)

        @block.vector
        def _(v):
            v.sem_inc(q.product, 2)
            v.sem_inc(q.summed, TPB)

            def fold(u, b):
                v.wait_ge(q.w_in[b], (u // 2) * W_IN + W_IN)
                for i in range(3):
                    v.wait_ge(q.low_rank, u * 3 + i + 1)
                    bank = ps_d[:, i, :]
                    if i < 2:
                        dst = w_raw[b][:, 0:KD * 2 * P].rearrange("p (k a n) -> p k a n", k=KD, a=2)[:, :, i, :]
                        src = bank.rearrange("p (k n) -> p k n", k=KD)
                    else:
                        dst, src = down(w_raw[b]), bank
                    last = nc.vector.tensor_tensor(dst, dst, src, ALU.add)
                last.then_inc(q.folded, 1)

            def prepare(u, b):
                if lora:
                    fold(u, b)
                v.wait_ge(q.split_h, u + 1)
                nc.vector.tensor_tensor(wl[b][:], w_raw[b][:], wh[b][:], ALU.subtract).then_inc(q.split_l, 1)

            def product(u, c):
                b = c % 2
                n = u * NB + c
                v.wait_ge(q.silu, n + 1)
                nc.vector.tensor_tensor(act[b][:], silu[b][:], ps_u[:, b, :], ALU.mult).then_inc(q.product, 1)
                v.wait_ge(q.act_h, n + 1)
                nc.vector.tensor_tensor(actl[b][:], act[b][:], acth[b][:], ALU.subtract).then_inc(q.act_l, 1)

            def sums(u, c):
                for t in range(TPB):
                    v.wait_ge(q.down_done, u * STEP_D + c * TPB + t + 1)
                    acc = m.acc[:, c * TPB + t, :]
                    nc.vector.scalar_tensor_tensor(out=acc, in0=ps_d[:, t, :], scalar=m.combine[:, c * TPB + t, bass.ds(u, 1)] if not lora else 1.0,
                                                   in1=acc, op0=ALU.mult, op1=ALU.add).then_inc(q.summed, 1)

            def unit(u, b, tail):
                for c in range(NB):
                    product(u, c)
                    if c:
                        sums(u, c - 1)
                    elif not isinstance(u, int) or u:
                        sums(u - 1, NB - 1)
                    if c == 1 and not tail:
                        prepare(u + 1, 1 - b)

            prepare(0, 0)
            unit_loop(v, unit)
            sums(units - 1, NB - 1)
            v.wait_ge(q.summed, units * STEP_D + TPB)

        @block.tensor
        def _(pe):
            if lora:
                pe.wait_ge(q.lora_in, 48)

            def low_rank(u, b):
                pe.wait_ge(q.w_in[b], (u // 2) * W_IN + W_IN)
                pe.wait_ge(q.summed, TPB if isinstance(u, int) and u == 0 else (u - 1) * STEP_D + 2 * TPB)
                for i in range(2):
                    for k in range(KD):
                        last = nc.tensor.matmul(ps_d[:, i, k * P:(k + 1) * P], la[:, i, k * P:(k + 1) * P], lu[b][:, i, :], start=True, stop=True)
                    last.then_inc(q.low_rank, 1)
                nc.tensor.matmul(ps_d[:, 2, :], lu[b][:, 2, :], lb[:], start=True, stop=True).then_inc(q.low_rank, 1)

            def gate_up_products(u, b, c):
                n = u * NB + c
                if c == 0:
                    pe.wait_ge(q.split_l, u + 1)
                pe.wait_ge(q.product, n + 1)
                for half, bank in ((0, ps_g), (1, ps_u)):
                    for k in range(KD):
                        last = split_product(nc, bank[:, c % 2, :], gate_up(wh[b], k, half), gate_up(wl[b], k, half),
                                             m.xnh[:, k, c * T:(c + 1) * T], m.xnl[:, k, c * T:(c + 1) * T], k == 0, k == KD - 1)
                last.then_inc(q.gate_up, 1)

            def down_products(u, b, c, tail=False):
                n = u * NB + c
                pe.wait_ge(q.act_l, n + 1)
                if lora and c == 1 and not tail:
                    pe.wait_ge(q.folded, u + 2)
                for t in range(TPB):
                    pe.wait_ge(q.summed, n * TPB + t + 1)
                    cols = slice(t * P, (t + 1) * P)
                    split_product(nc, ps_d[:, t, :], acth[c % 2][:, cols], actl[c % 2][:, cols],
                                  down(wh[b]), down(wl[b])).then_inc(q.down_done, 1)

            def unit(u, b, tail):
                for c in range(NB):
                    gate_up_products(u, b, c)
                    if c:
                        down_products(u, b, c - 1, tail)
                    elif not isinstance(u, int) or u:
                        down_products(u - 1, 1 - b, NB - 1)
                    if lora and c == 1 and not tail:
                        low_rank(u + 1, 1 - b)
            if lora:
                low_rank(0, 0)

            unit_loop(pe, unit)
            down_products(units - 1, (units - 1) % 2, NB - 1)


def weight_product_phase(nc, s, m, dram, ah, al):
    with ExitStack() as ctx:
        sb = lambda n, shape, dt=F32: ctx.enter_context(nc.sbuf_tensor(n, shape, dt))
        w1, w2, mask = sb("w1_raw", [P, KD, D]), sb("w2_raw", [P, KD, D]), sb("mask_raw", [P, KD, D])
        masked = sb("w_masked", [P, 2, D])
        ps_w = ctx.enter_context(nc.psum_tensor("ps_w", [P, 2, D], F32))
        block = ctx.enter_context(nc.Block(no_gpsimd_drain=True))

        @block.sync
        def _(sp):
            for dst, src in ((w1, dram.w1), (w2, dram.w2T), (mask, dram.mask)):
                sp.dma_start(dst[:], src.rearrange("(k p) n -> p k n", p=P)).then_inc(s.w12_in, 16)

        @block.tensor
        def _(pe):
            pe.wait_ge(s.w12_in, 48)
            for j in range(KD):
                if j >= 2:
                    pe.wait_ge(s.w_masked, j - 1)
                for k in range(KD):
                    last = nc.tensor.matmul(ps_w[:, j % 2, :], w1[:, k, j * P:(j + 1) * P], w2[:, k, :], start=k == 0, stop=k == KD - 1)
                last.then_inc(s.w_product, 1)

        @block.vector
        def _(v):
            v.wait_ge(s.w12_in, 48)
            for j in range(KD):
                v.wait_ge(s.w_product, j + 1)
                if j >= 2:
                    v.wait_ge(s.w_low, j - 1)
                nc.vector.tensor_tensor(masked[:, j % 2, :], ps_w[:, j % 2, :], mask[:, j, :], ALU.mult).then_inc(s.w_masked, 1)
                v.wait_ge(s.w_high, j + 1)
                nc.vector.tensor_tensor(al[:, j, :], masked[:, j % 2, :], ah[:, j, :], ALU.subtract).then_inc(s.w_low, 1)
            v.wait_ge(s.w_low, KD)

        @block.scalar
        def _(a):
            for j in range(KD):
                a.wait_ge(s.w_masked, j + 1)
                nc.scalar.copy(ah[:, j, :], masked[:, j % 2, :]).then_inc(s.w_high, 1)


def mix_phase(nc, s, m, dram):
    with ExitStack() as ctx:
        sb = lambda n, shape, dt=F32: ctx.enter_context(nc.sbuf_tensor(n, shape, dt))
        ps = lambda n, shape: ctx.enter_context(nc.psum_tensor(n, shape, F32))
        ah, al = sb("mix_wh", [P, KD, D], F32R), sb("mix_wl", [P, KD, D], F32R)
        weight_product_phase(nc, s, m, dram, ah, al)
        b2 = sb("b2", [P, D])
        yn = sb("mix_normed", [P, TPB, D])
        xn = sb("mix_xn", [P, TPB, D])
        xh, xl = sb("mix_xh", [P, 2, KD, P], F32R), sb("mix_xl", [P, 2, KD, P], F32R)
        ps_t = ps("mix_ps_t", [P, 2, KD, P])
        ps_y = ps("mix_ps_y", [P, TPB, D])
        block = ctx.enter_context(nc.Block(no_gpsimd_drain=True))
        x_tiles = lambda c: [m.x[:, bass.ds(c * TPB + t, 1), :] for t in range(TPB)]

        @block.sync
        def _(sp):
            sp.dma_start(b2[:], dram.b2.to_broadcast([P, D])).then_inc(s.b2_in, 16)

        @block.gpsimd
        def _(pool):
            with pool.Fori(0, NB) as c:
                for t in range(TPB):
                    tok = bass.ds(c * TPB + t, 1)
                    wait_apart(pool, s, s.c1_yn, c * TPB + t + 1)
                    nc.gpsimd.tensor_tensor(m.x[:, tok, :], m.x[:, tok, :], yn[:, t:t + 1, :], ALU.add).then_inc(s.c1_x, 1)
                    nc.gpsimd.tensor_copy(m.acc[:, tok, :], m.zero[:, 0:1].unsqueeze(1).to_broadcast([P, 1, D])).then_inc(s.c1_zero, 1)
                for t in range(TPB):
                    tok = bass.ds(c * TPB + t, 1)
                    wait_apart(pool, s, s.c3_yn, c * TPB + t + 1)
                    nc.gpsimd.tensor_tensor(m.x[:, tok, :], m.x[:, tok, :], yn[:, t:t + 1, :], ALU.add).then_inc(s.c3_x, 1)
            pool.wait_ge(s.c1_zero, NT)

        @block.scalar
        def _(a):
            with a.Fori(0, NB) as c:
                ln_deviation(nc, a, m, s.c1_moments, s.c1_dev, c)
                ln_deviation(nc, a, m, s.c2_moments, s.c2_dev, c)
                for t in range(TPB):
                    a.wait_ge(s.c2_tr, c * TPB + t + 1)
                    a.wait_ge(s.mixed, c * TPB + t + 1)
                    nc.scalar.copy(xh[:, t % 2], ps_t[:, t % 2]).then_inc(s.c2_h, 1)
                for t in range(TPB):
                    a.wait_ge(s.biased, c * TPB + t + 1)
                    nc.scalar.activation(yn[:, t, :], xn[:, t, :], ACT.Gelu).then_inc(s.gelu, 1)
                ln_deviation(nc, a, m, s.c3_moments, s.c3_dev, c)
                ln_deviation(nc, a, m, s.c4_moments, s.c4_dev, c)
                for t in range(TPB):
                    a.wait_ge(s.c4_tr, c * TPB + t + 1)
                    nc.scalar.copy(m.xnh[:, :, bass.ds(c * T + t * P, P)], ps_t[:, t % 2]).then_inc(s.c4_h, 1)

        @block.vector
        def _(v):
            v.sem_inc(s.c2_l, 2)
            v.sem_inc(s.c4_l, 1)
            v.wait_ge(s.b2_in, 16)
            with v.Fori(0, NB) as c:
                acc = [m.acc[:, bass.ds(c * TPB + t, 1), :] for t in range(TPB)]
                ln_moments(nc, v, s, m, acc, s.c1_stats, s.c1_moments, c)
                ln_rstd(nc, v, m, s.c1_dev, s.c1_rstd, c)
                for t in range(TPB):
                    ln_apply(nc, m, t, yn[:, t:t + 1, :], acc[t]).then_inc(s.c1_yn, 1)
                v.wait_ge(s.c1_x, c * TPB + TPB)
                ln_moments(nc, v, s, m, x_tiles(c), s.c2_stats, s.c2_moments, c)
                ln_rstd(nc, v, m, s.c2_dev, s.c2_rstd, c)
                for t in range(TPB):
                    ln_apply(nc, m, t, xn[:, t:t + 1, :], x_tiles(c)[t]).then_inc(s.c2_xn, 1)
                for t in range(TPB):
                    v.wait_ge(s.c2_h, c * TPB + t + 1)
                    nc.vector.tensor_tensor(xl[:, t % 2], ps_t[:, t % 2], xh[:, t % 2], ALU.subtract).then_inc(s.c2_l, 1)
                for t in range(TPB):
                    v.wait_ge(s.mixed, c * TPB + t + 1 + 2)
                    nc.vector.tensor_tensor(xn[:, t, :], ps_y[:, t, :], b2[:], ALU.add).then_inc(s.biased, 1)
                v.wait_ge(s.gelu, c * TPB + TPB)
                ln_moments(nc, v, s, m, [yn[:, t, :] for t in range(TPB)], s.c3_stats, s.c3_moments, c)
                ln_rstd(nc, v, m, s.c3_dev, s.c3_rstd, c)
                for t in range(TPB):
                    ln_apply(nc, m, t, yn[:, t, :], yn[:, t, :]).then_inc(s.c3_yn, 1)
                wait_apart(v, s, s.c3_x, c * TPB + TPB)
                ln_moments(nc, v, s, m, x_tiles(c), s.c4_stats, s.c4_moments, c)
                ln_rstd(nc, v, m, s.c4_dev, s.c4_rstd, c)
                for t in range(TPB):
                    ln_apply(nc, m, t, xn[:, t:t + 1, :], x_tiles(c)[t]).then_inc(s.c4_xn, 1)
                for t in range(TPB):
                    cols = bass.ds(c * T + t * P, P)
                    v.wait_ge(s.c4_h, c * TPB + t + 1)
                    nc.vector.tensor_tensor(m.xnl[:, :, cols], ps_t[:, t % 2], m.xnh[:, :, cols], ALU.subtract).then_inc(s.c4_l, 1)
            v.wait_ge(s.c4_l, NT + 1)

        @block.tensor
        def _(pe):
            pe.sem_inc(s.mixed, 2)
            with pe.Fori(0, NB) as c:
                for t in range(TPB):
                    b = t % 2
                    pe.wait_ge(s.c2_xn, c * TPB + t + 1)
                    pe.wait_ge(s.c2_l, c * TPB + t + 1)
                    if t < 2:
                        pe.wait_ge(s.c4_l, c * TPB + 1)
                    for k in range(KD):
                        last = nc.tensor.transpose(ps_t[:, b, k, :], xn[:, t, k * P:(k + 1) * P], m.ident[:])
                    last.then_inc(s.c2_tr, 1)
                    pe.wait_ge(s.c2_l, c * TPB + t + 3)
                    for k in range(KD):
                        last = split_product(nc, ps_y[:, t, :], xh[:, b, k, :], xl[:, b, k, :], ah[:, k, :], al[:, k, :], k == 0, k == KD - 1)
                    last.then_inc(s.mixed, 1)
                for t in range(TPB):
                    b = t % 2
                    pe.wait_ge(s.c4_xn, c * TPB + t + 1)
                    if t >= 2:
                        pe.wait_ge(s.c4_l, c * TPB + t)
                    for k in range(KD):
                        last = nc.tensor.transpose(ps_t[:, b, k, :], xn[:, t, k * P:(k + 1) * P], m.ident[:])
                    last.then_inc(s.c4_tr, 1)


def final_phase(nc, s, m, dram):
    with ExitStack() as ctx:
        yn = ctx.enter_context(nc.sbuf_tensor("final_normed", [P, TPB, D], F32))
        block = ctx.enter_context(nc.Block(no_gpsimd_drain=True))

        @block.sync
        def _(sp):
            with sp.Fori(0, NB) as c:
                sp.wait_ge(s.d_x, c * TPB + 2 * TPB)
                sp.dma_start(dram.out[bass.ds(c * T, T), :].rearrange("(t p) d -> p t d", p=P),
                             m.x[:, bass.ds(c * TPB, TPB), :]).then_inc(s.stored, 16)
            sp.wait_ge(s.stored, 16 * NB)

        @block.gpsimd
        def _(pool):
            pool.sem_inc(s.d_x, TPB)
            with pool.Fori(0, NB) as c:
                for t in range(TPB):
                    tok = bass.ds(c * TPB + t, 1)
                    wait_apart(pool, s, s.d_yn, c * TPB + t + 1)
                    nc.gpsimd.tensor_tensor(m.x[:, tok, :], m.x[:, tok, :], yn[:, t:t + 1, :], ALU.add).then_inc(s.d_x, 1)

        @block.scalar
        def _(a):
            with a.Fori(0, NB) as c:
                ln_deviation(nc, a, m, s.d_moments, s.d_dev, c)

        @block.vector
        def _(v):
            with v.Fori(0, NB) as c:
                acc = [m.acc[:, bass.ds(c * TPB + t, 1), :] for t in range(TPB)]
                ln_moments(nc, v, s, m, acc, s.d_stats, s.d_moments, c)
                ln_rstd(nc, v, m, s.d_dev, s.d_rstd, c)
                for t in range(TPB):
                    v.wait_ge(s.d_x, c * TPB + t + 1)
                    ln_apply(nc, m, t, yn[:, t:t + 1, :], acc[t]).then_inc(s.d_yn, 1)


class UnitSemaphores:

    def __init__(self, sem, phase):
        self.w_in = [sem(f"{phase}_w_in{b}") for b in range(2)]
        self.split_h = sem(f"{phase}_split_h")
        self.split_l = sem(f"{phase}_split_l")
        self.gate_up = sem(f"{phase}_gate_up")
        self.silu = sem(f"{phase}_silu")
        self.product = sem(f"{phase}_product")
        self.act_h = sem(f"{phase}_act_h")
        self.act_l = sem(f"{phase}_act_l")
        self.down_done = sem(f"{phase}_down_done")
        self.summed = sem(f"{phase}_summed")


class Semaphores:
    def __init__(self, sem):
        self.x_in, self.const, self.qkv_w_in, self.rope_in, self.q_rest, self.q_part0 = (sem(n) for n in "x_in const qkv_w_in rope_in q_rest q_part0".split())
        self.qkT_out, self.rope_parts, self.q_transposed, self.rot_ready, self.qkv_wh, self.qkv_wl = (sem(n) for n in "qkT_out rope_parts q_transposed rot_ready qkv_wh qkv_wl".split())
        self.a1_moments, self.a1_dev, self.a1_tr, self.a1_xh, self.a1_xl, self.a1_stats = (sem(n) for n in "a1_moments a1_dev a1_tr a1_xh a1_xl a1_stats".split())
        self.a1_rstd, self.a1_xn, self.qkv_done, self.v_ready = (sem(n) for n in "a1_rstd a1_xn qkv_done v_ready".split())
        self.ones_ready, self.ctxT_done, self.maxT_ready, self.exps, self.masked, self.maxT_turned = (sem(n) for n in "ones_ready ctxT_done maxT_ready exps masked maxT_turned".split())
        self.scoresT, self.weighted, self.ctxT_ready, self.v_in, self.row_max, self.ctx_ready = (sem(n) for n in "scoresT weighted ctxT_ready v_in row_max ctx_ready".split())
        self.scores, self.max_high, self.max_low, self.rden = (sem(n) for n in "scores max_high max_low rden".split())
        self.passed, self.wo_in, self.router_pad, self.router_in, self.expert_index, self.o_yn = (sem(n) for n in "passed wo_in router_pad router_in expert_index o_yn".split())
        self.o_x, self.o_tr, self.o_zero, self.o_ct, self.wo_h, self.router_h = (sem(n) for n in "o_x o_tr o_zero o_ct wo_h router_h".split())
        self.o_done, self.o_ch, self.b2_tr, self.b2_h, self.router_done, self.logitsT = (sem(n) for n in "o_done o_ch b2_tr b2_h router_done logitsT".split())
        self.top_gap, self.top_exp = (sem(n) for n in "top_gap top_exp".split())
        self.o_cl, self.wo_l, self.router_l, self.b2_l, self.b2_xn, self.logits_turned = (sem(n) for n in "o_cl wo_l router_l b2_l b2_xn logits_turned".split())
        self.logits, self.best, self.best_at, self.top, self.top_weight, self.one_hot = (sem(n) for n in "logits best best_at top top_weight one_hot".split())
        self.combine, self.q_part1, self.q_part2 = (sem(n) for n in "combine q_part1 q_part2".split())
        self.w12_in, self.w_masked, self.w_product, self.w_high, self.w_low, self.b2_in = (sem(n) for n in "w12_in w_masked w_product w_high w_low b2_in".split())
        self.c1_yn, self.c1_x, self.c1_zero, self.c3_yn, self.c3_x, self.c2_tr = (sem(n) for n in "c1_yn c1_x c1_zero c3_yn c3_x c2_tr".split())
        self.mixed, self.c2_h, self.biased, self.gelu, self.c4_tr, self.c4_h = (sem(n) for n in "mixed c2_h biased gelu c4_tr c4_h".split())
        self.c2_l, self.c4_l, self.c2_xn, self.c4_xn = (sem(n) for n in "c2_l c4_l c2_xn c4_xn".split())
        self.d_x, self.d_yn, self.stored = (sem(n) for n in "d_x d_yn stored".split())
        self.b1_stats, self.b1_moments, self.b1_dev, self.b1_rstd = (sem(n) for n in "b1_stats b1_moments b1_dev b1_rstd".split())
        self.b2_stats, self.b2_moments, self.b2_dev, self.b2_rstd = (sem(n) for n in "b2_stats b2_moments b2_dev b2_rstd".split())
        self.c1_stats, self.c1_moments, self.c1_dev, self.c1_rstd = (sem(n) for n in "c1_stats c1_moments c1_dev c1_rstd".split())
        self.c2_stats, self.c2_moments, self.c2_dev, self.c2_rstd = (sem(n) for n in "c2_stats c2_moments c2_dev c2_rstd".split())
        self.c3_stats, self.c3_moments, self.c3_dev, self.c3_rstd = (sem(n) for n in "c3_stats c3_moments c3_dev c3_rstd".split())
        self.c4_stats, self.c4_moments, self.c4_dev, self.c4_rstd = (sem(n) for n in "c4_stats c4_moments c4_dev c4_rstd".split())
        self.d_stats, self.d_moments, self.d_dev, self.d_rstd = (sem(n) for n in "d_stats d_moments d_dev d_rstd".split())
        self.qs_in, self.max_in = ([sem(f"{n}{b}") for b in range(3)] for n in ("qs_in", "max_in"))
        self.moe, self.ff = UnitSemaphores(sem, "moe"), UnitSemaphores(sem, "ff")
        self.ff.lora_in, self.ff.low_rank, self.ff.folded = (sem(n) for n in "lora_in low_rank folded".split())


class Memory:

    def __init__(self, sb):
        self.x = sb("x", [P, NT, D])
        self.acc = sb("acc", [P, NT, D])
        self.combine = sb("combine", [P, NT, 32])
        self.ident, self.ident16 = sb("ident", [P, P]), sb("ident16", [P, P], BF16)
        self.causal = sb("causal", [P, P], BF16)
        self.eps, self.zero = sb("eps", [P, 1]), sb("zero", [P, 1])
        self.stats, self.mv = sb("stats", [P, TPB, 6]), sb("mv", [P, TPB, 2])
        self.dev, self.rstd = sb("dev", [P, TPB]), sb("rstd", [P, TPB])


class Dram:

    def __init__(self, nc, ins, out):
        self.x, self.rope, self.mask, self.b2 = ins["x"], ins["rope"], ins["mask"], ins["b2"]
        self.wqT, self.wkT, self.wvT, self.woT = ins["wqT"], ins["wkT"], ins["wvT"], ins["woT"]
        self.routerT, self.moe_gate_up, self.moe_down = ins["routerT"], ins["moe_gate_up"], ins["moe_down"]
        self.w1, self.w2T = ins["w1"], ins["w2T"]
        self.ff_gate_up, self.ff_down, self.lora_unit = ins["ff_gate_up"], ins["ff_down"], ins["lora_unit"]
        self.gate_a, self.up_a, self.down_bT = ins["gate_a"], ins["up_a"], ins["down_bT"]
        self.q_parts = nc.dram_tensor("q_parts", [H, PARTS, DH, NB * T], BF16, kind="Internal").ap()
        self.k_stack = nc.dram_tensor("k_stack", [HKV, len(STACK), DH, NB * T], BF16, kind="Internal").ap()
        self.out = out


def build(nc, ins, out, upto=9):
    with ExitStack() as ctx:
        sem = lambda n: ctx.enter_context(nc.semaphore(n))
        sb = lambda n, shape, dt=F32: ctx.enter_context(nc.sbuf_tensor(n, shape, dt))
        s, m, dram = Semaphores(sem), Memory(sb), Dram(nc, ins, out)
        with nc.sbuf_tensor("v_pad", [P, NT, HKV, HB], F32) as v_pad:
            m.v_pad = v_pad
            const_phase(nc, s, m, dram)
            qkv_phase(nc, s, m, dram)
            if upto > 1:
                attention_phase(nc, s, m, dram)
        if upto > 2:
            with nc.sbuf_tensor("xnh", [P, KD, NB * T], F32R) as m.xnh, nc.sbuf_tensor("xnl", [P, KD, NB * T], F32R) as m.xnl:
                output_phase(nc, s, m, dram)
                if upto > 3:
                    units_phase(nc, s, s.moe, m, dram, "moe", UNITS_MOE, (dram.moe_gate_up, dram.moe_down))
                if upto > 4:
                    mix_phase(nc, s, m, dram)
                if upto > 5:
                    units_phase(nc, s, s.ff, m, dram, "ff", UNITS_FF, (dram.ff_gate_up, dram.ff_down), lora=True)
        if upto > 6:
            final_phase(nc, s, m, dram)







def lay_out(inputs):
    f = lambda k: np.asarray(inputs[k])
    tr = lambda a: np.ascontiguousarray(a.T)
    arrays = {
        "x": f("L0_attn_x").reshape(NB * T, D),
        "wqT": tr(f("L0_attn_Wq")), "wkT": tr(f("L0_attn_Wk")), "wvT": tr(f("L0_attn_Wv")), "woT": tr(f("L0_attn_Wo")),
        "rope": setup_tables(),
        "routerT": tr(f("L0_ffn_gate_w")),
        "w1": f("L1_attn_w1"), "w2T": tr(f("L1_attn_w2")), "mask": f("L1_attn_sparse_mask"),
        "b2": f("L1_attn_b2").reshape(1, D),
        "gate_a": f("L1_ffn_gate_a"), "up_a": f("L1_ffn_up_a"), "down_bT": tr(f("L1_ffn_down_b")),
    }
    shared_up = f("L0_ffn_shared_w_gate_up").reshape(2, NSH, INTER, D).transpose(1, 3, 0, 2).reshape(NSH, D, 2 * INTER)
    shared_down = f("L0_ffn_shared_w_down").T.reshape(NSH, INTER, D)
    arrays["moe_gate_up"] = np.concatenate([f("L0_ffn_w_gate_up").transpose(0, 2, 1), shared_up])
    arrays["moe_down"] = np.concatenate([f("L0_ffn_w_down").transpose(0, 2, 1), shared_down])
    def rows(a):
        out = np.zeros((UNITS_FF * P,) + a.shape[1:], a.dtype)
        out[:FF] = a
        return out.reshape((UNITS_FF, P) + a.shape[1:])
    pair = np.stack([rows(f("L1_ffn_gate_w")), rows(f("L1_ffn_up_w"))], 1)
    arrays["ff_gate_up"] = np.ascontiguousarray(pair.transpose(0, 3, 1, 2)).reshape(UNITS_FF, D, 2 * P)
    arrays["ff_down"] = rows(tr(f("L1_ffn_down_w")))
    lora = np.stack([rows(f("L1_ffn_gate_b")), rows(f("L1_ffn_up_b")), rows(tr(f("L1_ffn_down_a")))], 1)
    arrays["lora_unit"] = np.ascontiguousarray(lora.transpose(0, 3, 1, 2))
    return arrays


def program(nc, shapes, upto=9):
    ins = {n: nc.dram_tensor(f"in_{n}", shape, F32, kind="ExternalInput").ap() for n, shape in shapes.items()}
    out = nc.dram_tensor("out", [NB * T, D], F32, kind="ExternalOutput").ap()
    build(nc, ins, out, upto)


def kernel(**inputs):
    import concourse.bacc as bacc
    from concourse.bass_utils import run_bass_kernel_spmd
    arrays = lay_out(inputs)
    nc = bacc.Bacc("TRN2", target_bir_lowering=False, num_devices=1)
    program(nc, {n: a.shape for n, a in arrays.items()})
    result = run_bass_kernel_spmd(nc, [{f"in_{n}": a for n, a in arrays.items()}], core_ids=[0])
    return result.results[0]["out"].reshape(NB, T, D)
```

```python
from contextlib import ExitStack

import numpy as np
import concourse.bass as bass
from concourse import mybir

F32 = mybir.dt.float32
F32R = mybir.dt.float32r
BF16 = mybir.dt.bfloat16
U32 = mybir.dt.uint32
ALU = mybir.AluOpType
ACT = mybir.ActivationFunctionType
AX_X = mybir.AxisListType.X

P = 128
D = 512
KD = D // P
NB, T = 4, 512
TPB = T // P
NT = NB * TPB
H, HKV, DH = 32, 8, 16
G = H // HKV
QK = (H + HKV) * DH
QKV = QK + HKV * DH
PARTS = 3
STACK = ((0, 0), (1, 0), (2, 0), (0, 1), (1, 1), (0, 2))
HB = 32
NE, INTER = 16, 128
NSH = 4
UNITS_MOE = NE + NSH
FF = 1376
UNITS_FF = -(-FF // P)
NW = KD * 2 * P + D
RANK = 16
GROUP = 32
LORA_ROWS = 3 * GROUP
EPS = 1e-5
MASKED = -1.0e30


def setup_tables():
    inv = (1.0 / np.power(np.float32(500000.0), np.arange(0, DH, 2, dtype=np.float32) / np.float32(DH))).astype(np.float32)
    wavelen = (np.float32(2.0 * np.pi) / inv).astype(np.float32)
    lo, hi = 1024 / 4.0, 1024 / 1.0
    inv2 = np.where(wavelen > hi, inv / np.float32(32.0), inv).astype(np.float32)
    smooth = ((np.float32(1024) / wavelen - np.float32(1.0)) / np.float32(3.0)).astype(np.float32)
    smoothed = ((1 - smooth) * inv2 / np.float32(32.0) + smooth * inv2).astype(np.float32)
    medium = ~(wavelen < hi) & ~(wavelen > lo)
    inv2 = np.where(medium, smoothed, inv2).astype(np.float32)
    ang = (np.arange(T, dtype=np.float32)[:, None] * inv2[None, :]).astype(np.float32)
    cos = np.cos(np.concatenate([ang, ang], 1)).astype(np.float32)
    sin = np.sin(np.concatenate([-ang, ang], 1)).astype(np.float32)
    return np.stack([cos, sin], 1)


def const_phase(nc, s, m, dram):
    with nc.Block(no_gpsimd_drain=True) as block:
        @block.sync
        def _(sp):
            sp.dma_start(m.x[:, 0:TPB, :], dram.x[0:T, :].rearrange("(t p) d -> p t d", p=P)).then_inc(s.x_first_in, 16)

        @block.gpsimd
        def _(pool):
            nc.gpsimd.memset(m.ident[:], 0.0).then_inc(s.const, 1)
            nc.gpsimd.memset(m.ident16[:], 0.0).then_inc(s.const, 1)
            nc.gpsimd.memset(m.causal[:], 0.0).then_inc(s.const, 1)
            nc.gpsimd.memset(m.v_pad[:], 0.0).then_inc(s.const, 1)
            nc.gpsimd.memset(m.combine[:], 1.0).then_inc(s.const, 1)
            nc.gpsimd.memset(m.eps[:], EPS).then_inc(s.const, 1)
            nc.gpsimd.memset(m.router_raw[:], 0.0).then_inc(s.const, 1)
            pool.wait_ge(s.const, 7)
            for tile in (m.ident, m.ident16):
                nc.gpsimd.affine_select(out=tile[:], in_=tile[:], compare_op=ALU.not_equal, fill=1.0, base=0,
                                        pattern=[[-1, P]], channel_multiplier=1).then_inc(s.const, 1)
            nc.gpsimd.affine_select(out=m.causal[:], in_=m.causal[:], compare_op=ALU.is_ge, fill=MASKED, base=0,
                                    pattern=[[-1, P]], channel_multiplier=1).then_inc(s.const, 1)
            nc.gpsimd.memset(m.v_pad[:, :, :, DH:DH + 1], 1.0).then_inc(s.const, 1)
            pool.wait_ge(s.const, CONSTANTS)


CONSTANTS = 11


def wait_apart(eng, s, sem, value):
    eng.wait_ge(sem, value)
    eng.sem_inc(s.passed, 1)


def ln_moments(nc, v, s, n, sources, c):
    for t, src in enumerate(sources):
        nc.vector.bn_stats(n.stats[:, t, :], src).then_inc(n.stats_ready, 1)
    wait_apart(v, s, n.stats_ready, c * TPB + TPB)
    for t in range(TPB):
        nc.vector.bn_aggr(n.mv[:, t, :], n.stats[:, t, :]).then_inc(n.moments_ready, 1)


def ln_deviation(nc, a, m, n, c):
    a.wait_ge(n.moments_ready, c * TPB + TPB)
    nc.scalar.activation(n.dev[:], n.mv[:, :, 1], ACT.Sqrt, bias=m.eps[:]).then_inc(n.dev_ready, 1)


def ln_rstd(nc, v, n, c):
    v.wait_ge(n.dev_ready, c + 1)
    nc.vector.reciprocal(n.rstd[:], n.dev[:]).then_inc(n.rstd_ready, 1)
    v.wait_ge(n.rstd_ready, c + 1)


def ln_apply(nc, n, t, out, src):
    return nc.vector.tensor_scalar(out, src, n.mv[:, t, 0:1], n.rstd[:, t:t + 1], ALU.subtract, ALU.mult)


def zero_last_chunk(nc, pool, s, m, times):
    nc.gpsimd.memset(m.acc[:, NT - TPB:NT, :], 0.0).then_inc(s.acc_zero, 1)
    pool.wait_ge(s.acc_zero, times)


def split_product(nc, out, wh, wl, xh, xl, first=True, last=True):
    nc.tensor.matmul(out, wh, xh, start=first, stop=False)
    nc.tensor.matmul(out, wh, xl, start=False, stop=False)
    return nc.tensor.matmul(out, wl, xh, start=False, stop=last)


def qkv_phase(nc, s, m, dram):
    with ExitStack() as ctx:
        sb = lambda n, shape, dt=F32: ctx.enter_context(nc.sbuf_tensor(n, shape, dt))
        ps = lambda n, shape: ctx.enter_context(nc.psum_tensor(n, shape, F32))
        w_raw = m.acc[:, 0:KD * QKV // D, :].rearrange("p t d -> p (t d)").rearrange("p (k n) -> p k n", k=KD)
        wh, wl = sb("qkv_wh", [P, KD, QKV], F32R), sb("qkv_wl", [P, KD, QKV], F32R)
        rope = sb("rope", [P, TPB, 2, DH])
        xn = sb("qkv_xn", [P, TPB, D])
        xh, xl = sb("qkv_xh", [P, 2, KD, P], F32R), sb("qkv_xl", [P, 2, KD, P], F32R)
        used = KD * QKV // D
        by_cos, by_sin = (m.acc[:, used + i * 5:used + i * 5 + 5, :].rearrange("p t d -> p (t d)")[:, 0:2 * QK].rearrange("p (b n) -> p b n", b=2)
                          for i in range(2))
        rot = by_cos
        NQ = QK // P
        parts = sb("qkT_parts", [P, PARTS, NQ, NB * T], BF16)
        rest = sb("qkT_rest", [P, 2, NQ, P])
        ps_t = ps("qkv_ps_t", [P, 2, KD, P])
        ps_qkv = ps("ps_qkv", [P, 2, 2 * 512])
        ps_qt = ps("ps_qt", [P, 2 * 512])
        QK_OUT = 16 * NQ * PARTS
        block = ctx.enter_context(nc.Block(no_gpsimd_drain=True))

        def chunks(eng, chunk):
            chunk(0, False)
            with eng.Fori(0, NB - 2) as c:
                chunk(c + 1, False)
            chunk(NB - 1, True)

        def before(c, t):
            if t == 0 and isinstance(c, int) and c == 0:
                return None
            return (c, t - 1, c * TPB + t - 1) if t else (c - 1, TPB - 1, c * TPB - 1)

        def after(c, t, last):
            if t == TPB - 1 and last:
                return None
            return (c, t + 1, c * TPB + t + 1) if t < TPB - 1 else (c + 1, 0, c * TPB + TPB)

        columns = lambda c, t: bass.ds(c * T + t * P, P)

        @block.sync
        def _(sp):
            sp.dma_start(w_raw[:, :, 0:D], dram.wqT.rearrange("(k p) n -> p k n", p=P)).then_inc(s.wq_in, 16)
            for src, a, b in ((dram.wkT, D, QK), (dram.wvT, QK, QKV)):
                sp.dma_start(w_raw[:, :, a:b], src.rearrange("(k p) n -> p k n", p=P)).then_inc(s.qkv_w_in, 16)
            sp.dma_start(rope[:], dram.rope.rearrange("(t p) a d -> p t a d", p=P)).then_inc(s.rope_in, 16)
            sp.dma_start(m.x[:, TPB:NT, :], dram.x[T:NB * T, :].rearrange("(t p) d -> p t d", p=P)).then_inc(s.x_in, 16)
            sp.dma_start(m.wo_raw[:], dram.woT.rearrange("(k p) n -> p k n", p=P)).then_inc(s.wo_in, 16)
            sp.dma_start(m.router_raw[:, :, 0:NE], dram.routerT.rearrange("(k p) n -> p k n", p=P)).then_inc(s.router_in, 16)
            with sp.Fori(0, NB) as c:
                tok = bass.ds(c * T, T)
                for part, ready in enumerate((s.q_part0, s.q_part1, s.q_part2)):
                    sp.wait_ge(ready, c * TPB + TPB)
                    for j in range(NQ - 1):
                        sp.dma_start(dram.q_parts[j * P // DH:(j + 1) * P // DH, part, :, tok], parts[:, part, j, tok]).then_inc(s.qkT_out, 16)
                    places = [place for place, (_, k_part) in enumerate(STACK) if k_part == part]
                    sp.dma_start(dram.k_stack[places[0]:places[-1] + 1, :, tok].rearrange("a r t -> r a t"),
                                 parts[:, part, NQ - 1:NQ, tok].to_broadcast([P, len(places), T])).then_inc(s.qkT_out, 16)
            sp.wait_ge(s.qkT_out, QK_OUT * NB)

        @block.gpsimd
        def _(pool):
            def q_third(tile):
                c, t, n = tile
                wait_apart(pool, s, s.q_part1, n + 1)
                nc.gpsimd.tensor_tensor(parts[:, 2, :, columns(c, t)], rest[:, t % 2], parts[:, 1, :, columns(c, t)],
                                        ALU.subtract).then_inc(s.q_part2, 1)

            def chunk(c, last):
                for t in range(TPB):
                    pool.wait_ge(s.rope_parts, c * TPB + t + 1)
                    nc.gpsimd.tensor_tensor(rot[:, t % 2, :], by_cos[:, t % 2, :], by_sin[:, t % 2, :],
                                            ALU.add).then_inc(s.rot_ready, 1)
                    if before(c, t):
                        q_third(before(c, t))

            chunks(pool, chunk)
            q_third((NB - 1, TPB - 1, NT - 1))

        @block.scalar
        def _(a):
            def norm_high(tile):
                c, t, n = tile
                a.wait_ge(s.a1_tr, n + TPB + 1)
                a.wait_ge(s.qkv_done, n + 1)
                nc.scalar.copy(xh[:, t % 2], ps_t[:, t % 2]).then_inc(s.a1_xh, 1)

            def q_high(tile):
                c, t, n = tile
                a.wait_ge(s.q_transposed, n + 3)
                nc.scalar.copy(parts[:, 0, :, columns(c, t)], ps_qt[:, 0:QK].rearrange("p (j n) -> p j n", n=P)).then_inc(s.q_part0, 1)

            def q_second(tile):
                c, t, n = tile
                a.wait_ge(s.q_rest, n + 1 + 1)
                nc.scalar.copy(parts[:, 1, :, columns(c, t)], rest[:, t % 2]).then_inc(s.q_part1, 1)

            a.sem_inc(s.v_ready, 2)
            ln_deviation(nc, a, m, s.norm_a1, 0)
            for lo, hi, arrived, count in ((0, D, s.wq_in, 16), (D, QKV, s.qkv_w_in, 32)):
                a.wait_ge(arrived, count)
                nc.scalar.copy(wh[:, :, lo:hi], w_raw[:, :, lo:hi]).then_inc(s.qkv_wh, 1)
            norm_high((0, 0, 0))

            def chunk(c, last):
                for t in range(TPB):
                    if after(c, t, last):
                        norm_high(after(c, t, last))
                    if before(c, t) and before(*before(c, t)[:2]):
                        q_second(before(*before(c, t)[:2]))
                    if before(c, t):
                        q_high(before(c, t))
                    if t == 1 and not last:
                        ln_deviation(nc, a, m, s.norm_a1, c + 1)
                    a.wait_ge(s.rope_parts, c * TPB + t + 1)
                    nc.scalar.copy(m.v_pad[:, bass.ds(c * TPB + t, 1), :, 0:DH],
                                   ps_qkv[:, t % 2, QK:QKV].rearrange("p (o g d) -> p o g d", o=1, d=DH)).then_inc(s.v_ready, 1)

            chunks(a, chunk)
            q_second((NB - 1, TPB - 2, NT - 2))
            q_high((NB - 1, TPB - 1, NT - 1))
            q_second((NB - 1, TPB - 1, NT - 1))

        @block.vector
        def _(v):
            def moments(c):
                v.wait_ge(s.x_first_in if isinstance(c, int) and c == 0 else s.x_in, 16)
                ln_moments(nc, v, s, s.norm_a1, [m.x[:, bass.ds(c * TPB + t, 1), :] for t in range(TPB)], c)

            def norm(c):
                ln_rstd(nc, v, s.norm_a1, c)
                for t in range(TPB):
                    v.wait_ge(s.a1_tr, c * TPB + t + 1)
                    ln_apply(nc, s.norm_a1, t, xn[:, t:t + 1, :], m.x[:, bass.ds(c * TPB + t, 1), :]).then_inc(s.a1_xn, 1)

            def norm_low(tile):
                c, t, n = tile
                v.wait_ge(s.a1_xh, n + 1)
                v.wait_ge(s.qkv_done, n + 1)
                nc.vector.tensor_tensor(xl[:, t % 2], ps_t[:, t % 2], xh[:, t % 2], ALU.subtract).then_inc(s.a1_xl, 1)

            def q_remainder(tile):
                c, t, n = tile
                v.wait_ge(s.q_part0, n + 1)
                if not (isinstance(n, int) and n < 2):
                    v.wait_ge(s.q_part2, n - 1)
                nc.vector.tensor_tensor(rest[:, t % 2], ps_qt[:, 0:QK].rearrange("p (j n) -> p j n", n=P),
                                        parts[:, 0, :, columns(c, t)], ALU.subtract).then_inc(s.q_rest, 1)

            def rotate(c, t):
                b = t % 2
                v.wait_ge(s.qkv_done, c * TPB + t + 3)
                v.wait_ge(s.q_transposed, c * TPB + t + 1)
                heads = ps_qkv[:, b, 0:QK].rearrange("p (h d) -> p h d", d=DH)
                cosv = rope[:, t, 0, :].unsqueeze(1).to_broadcast([P, H + HKV, DH])
                sinv = rope[:, t, 1, :].unsqueeze(1).to_broadcast([P, H + HKV, DH])
                co = by_cos[:, b, :].rearrange("p (h d) -> p h d", d=DH)
                si = by_sin[:, b, :].rearrange("p (h d) -> p h d", d=DH)
                nc.vector.tensor_tensor(co, heads, cosv, ALU.mult)
                h2 = DH // 2
                nc.vector.tensor_tensor(si[:, :, 0:h2], heads[:, :, h2:DH], sinv[:, :, 0:h2], ALU.mult)
                nc.vector.tensor_tensor(si[:, :, h2:DH], heads[:, :, 0:h2], sinv[:, :, h2:DH], ALU.mult).then_inc(s.rope_parts, 1)

            v.sem_inc(s.q_rest, 1)
            v.sem_inc(s.a1_xl, 2)
            moments(0)
            norm(0)
            for i, (lo, hi) in enumerate(((0, D), (D, QKV))):
                v.wait_ge(s.qkv_wh, i + 1)
                nc.vector.tensor_tensor(wl[:, :, lo:hi], w_raw[:, :, lo:hi], wh[:, :, lo:hi], ALU.subtract).then_inc(s.qkv_wl, 1)
            norm_low((0, 0, 0))
            v.wait_ge(s.rope_in, 16)

            def chunk(c, last):
                for t in range(TPB):
                    if t == 3 and not last:
                        norm(c + 1)
                    if after(c, t, last):
                        norm_low(after(c, t, last))
                    if before(c, t):
                        q_remainder(before(c, t))
                    if t == 1 and not last:
                        moments(c + 1)
                    rotate(c, t)

            chunks(v, chunk)
            q_remainder((NB - 1, TPB - 1, NT - 1))

        @block.tensor
        def _(pe):
            def turn_norm(tile):
                c, t, n = tile
                pe.wait_ge(s.a1_xn, n + 1)
                pe.wait_ge(s.a1_xl, n + 1)
                for k in range(KD):
                    last = nc.tensor.transpose(ps_t[:, t % 2, k, :], xn[:, t, k * P:(k + 1) * P], m.ident[:])
                last.then_inc(s.a1_tr, 1)

            def turn_q(tile):
                c, t, n = tile
                pe.wait_ge(s.rot_ready, n + 1)
                pe.wait_ge(s.q_rest, n + 1)
                for j in range(NQ):
                    last = nc.tensor.transpose(ps_qt[:, j * P:(j + 1) * P], rot[:, t % 2, j * P:(j + 1) * P], m.ident[:])
                last.then_inc(s.q_transposed, 1)

            def products(c, t, which):
                lo, hi = which
                for k in range(KD):
                    last = split_product(nc, ps_qkv[:, t % 2, lo:hi], xh[:, t % 2, k, :], xl[:, t % 2, k, :],
                                         wh[:, k, lo:hi], wl[:, k, lo:hi], k == 0, k == KD - 1)
                return last

            pe.sem_inc(s.a1_tr, TPB)
            pe.sem_inc(s.qkv_done, 2)
            pe.sem_inc(s.q_transposed, 2)
            turn_norm((0, 0, 0))

            def chunk(c, last):
                for t in range(TPB):
                    if after(c, t, last):
                        turn_norm(after(c, t, last))
                    pe.wait_ge(s.a1_xl, c * TPB + t + 3)
                    pe.wait_ge(s.v_ready, c * TPB + t + 1)
                    first = isinstance(c, int) and c == 0 and t == 0
                    if first:
                        pe.wait_ge(s.qkv_wl, 1)
                    products(c, t, (0, D))
                    if before(c, t):
                        turn_q(before(c, t))
                    if first:
                        pe.wait_ge(s.qkv_wl, 2)
                    products(c, t, (D, QKV)).then_inc(s.qkv_done, 1)

            chunks(pe, chunk)
            turn_q((NB - 1, TPB - 1, NT - 1))


def attention_phase(nc, s, m, dram):
    KS, KM = len(STACK) * DH, len(STACK) * DH + 2
    STEPS = NB * HKV
    BUF = 3
    with ExitStack() as ctx:
        sb = lambda n, shape, dt=F32: ctx.enter_context(nc.sbuf_tensor(n, shape, dt))
        ps = lambda n, shape: ctx.enter_context(nc.psum_tensor(n, shape, F32))
        qs = [sb(f"q_stack{i}", [KM, G, T], BF16) for i in range(BUF)]
        ks = [sb(f"k_stack{i}", [KM, T], BF16) for i in range(BUF)]
        vs = [sb(f"v_step{i}", [P, TPB, HB]) for i in range(BUF)]
        row_max = [sb(f"row_max{i}", [P, G * TPB]) for i in range(BUF)]
        max_hl = [sb(f"max_hl{i}", [P, 2 * G * TPB], BF16) for i in range(BUF)]
        maxT = [sb(f"maxT{i}", [2 * G * TPB, P], BF16) for i in range(BUF)]
        pT = [sb(f"weightsT{i}", [P, G, T]) for i in range(2)]
        ctxT = [sb(f"ctxT{i}", [P, T]) for i in range(BUF)]
        rden = [sb(f"rden{i}", [P, TPB, G]) for i in range(BUF)]
        ps_s = ps("ps_scores", [P, 2, 2, T])
        ps_st = ps("ps_scoresT", [P, 2, T])
        ps_o = ps("ps_ctxT", [P, T])
        ps_x = ps("ps_turned", [P, T])
        block = ctx.enter_context(nc.Block(no_gpsimd_drain=True))
        RG, CG, AHEAD, TURN = 2 * TPB, G * TPB, 2, 14

        def steps(eng, first, both, last):
            first()
            with eng.Fori(0, (STEPS - 2) // BUF) as i:
                for o in range(1, BUF + 1):
                    both(i * BUF + o, o % BUF, o - 1, i + o // BUF)
            assert STEPS % BUF == 2
            both(STEPS - 1, 1, 0, STEPS // BUF)
            last()

        @block.sync
        def _(sp):
            for b in range(BUF):
                sp.sem_inc(s.max_in[b], 32)

            def load(n, b):
                seq, g = n // HKV, n % HKV
                tok = bass.ds(seq * T, T)
                row = 0
                for parts in (3, 2, 1):
                    sp.dma_start(qs[b][row:row + parts * DH, :, :],
                                 dram.q_parts[bass.ds(g * G, G), 0:parts, :, tok].rearrange("h a d t -> (a d) h t")).then_inc(s.qs_in[b], 16)
                    row += parts * DH
                sp.dma_start(ks[b][0:KS, :], dram.k_stack[:, bass.ds(g * DH, DH), tok]).then_inc(s.qs_in[b], 16)

            def maxima(n, b):
                sp.wait_ge(s.maxT_ready, n + 1)
                for part in range(2):
                    sp.dma_start(qs[b][KS + part:KS + part + 1, :, :],
                                 maxT[b][part * G * TPB:(part + 1) * G * TPB, :]).then_inc(s.max_in[b], 16)

            def both(n, b):
                sp.wait_ge(s.ctxT_done, n)
                load(n + 1, (b + 1) % BUF)
                maxima(n, b)

            for n in range(BUF - 1):
                load(n, n)
            maxima(0, 0)
            with sp.Fori(0, (STEPS - 2) // BUF) as i:
                for o in range(1, BUF + 1):
                    both(i * BUF + o, o % BUF)
            maxima(STEPS - 1, 1)

        @block.gpsimd
        def _(pool):
            for b in range(BUF):
                nc.gpsimd.memset(ks[b][KS:KM, :], 1.0).then_inc(s.ones_ready, 1)

            def mask(n):
                for j in range(TPB):
                    wait_apart(pool, s, s.exps, n * CG + (j + 1) * G + 2)
                    nc.gpsimd.affine_select(out=pT[j % 2][:, :, 0:P], in_=pT[j % 2][:, :, 0:P], compare_op=ALU.is_ge,
                                            fill=0.0, base=0, pattern=[[0, G], [1, P]], channel_multiplier=-1).then_inc(s.masked, 1)

            with pool.Fori(0, STEPS) as n:
                mask(n)

        @block.scalar
        def _(a):
            nc.scalar.preload_act_table(ACT.Exp)
            a.sem_inc(s.exps, 2)
            a.sem_inc(s.ctxT_ready, 1)

            def max_copy(n, b, used):
                a.wait_ge(s.maxT_turned, n + 1)
                a.wait_ge(s.max_in[b], used * 32 + 32)
                nc.scalar.copy(maxT[b][:], ps_x.bitcast(BF16)[0:2 * G * TPB, 0:P]).then_inc(s.maxT_ready, 1)

            def exps(n, groups):
                for k in groups:
                    j, h = k // G, k % G
                    a.wait_ge(s.scoresT, n * CG + k + 1)
                    if h == 0:
                        a.wait_ge(s.weighted, n * TPB + j + 2 - 1)
                    w = T - j * P
                    nc.scalar.activation(pT[j % 2][:, h, 0:w], ps_st[:, k % 2, 0:w], ACT.Exp, scale=DH ** -0.5).then_inc(s.exps, 1)

            def ctx_copy(n, b):
                a.wait_ge(s.weighted, n * TPB + TPB + 2)
                nc.scalar.copy(ctxT[b][:], ps_o[:]).then_inc(s.ctxT_ready, 1)

            def v_copy(n, b):
                if not (isinstance(n, int) and n == 0):
                    a.wait_ge(s.ctxT_done, n)
                seq, g = n // HKV, n % HKV
                nc.scalar.copy(vs[b][:], m.v_pad[:, bass.ds(seq * TPB, TPB), bass.ds(g, 1), :].rearrange("p t o d -> p t (o d)")).then_inc(s.v_in, 1)

            def both(n, b, before, used):
                exps(n - 1, range(G))
                v_copy(n, b)
                exps(n - 1, range(G, TURN))
                max_copy(n, b, used)
                exps(n - 1, range(TURN, CG))
                ctx_copy(n - 1, before)

            def first():
                v_copy(0, 0)
                max_copy(0, 0, 0)

            def last():
                exps(STEPS - 1, range(CG))
                ctx_copy(STEPS - 1, 1)

            steps(a, first, both, last)

        @block.vector
        def _(v):
            v.sem_inc(s.row_max, 2)
            v.sem_inc(s.ctx_ready, 1)

            def maxima(n, b, groups):
                for k in groups:
                    i, hp = TPB - 1 - k // 2, k % 2
                    v.wait_ge(s.scores, n * RG + k + 1)
                    nc.vector.tensor_reduce(row_max[b][:, 2 * hp * TPB + i:2 * hp * TPB + i + TPB + 1:TPB],
                                            ps_s[:, k % 2, :, 0:(i + 1) * P], AX_X, ALU.max, negate=True).then_inc(s.row_max, 1)

            def split_maxima(n, b):
                half = G * TPB
                v.wait_ge(s.row_max, n * RG + RG + 2)
                nc.vector.tensor_copy(max_hl[b][:, 0:half], row_max[b][:]).then_inc(s.max_high, 1)
                v.wait_ge(s.max_high, n + 1)
                nc.vector.tensor_tensor(max_hl[b][:, half:2 * half], row_max[b][:], max_hl[b][:, 0:half], ALU.subtract).then_inc(s.max_low, 1)

            def normalize(n, b):
                seq, g = n // HKV, n % HKV
                v.wait_ge(s.ctxT_done, n + 2)
                blocks = ps_x[:].rearrange("p (i h c) -> p i h c", i=TPB, h=G)
                nc.vector.reciprocal(rden[b][:], blocks[:, :, :, DH]).then_inc(s.rden, 1)
                v.wait_ge(s.rden, n + 1)
                for i in range(TPB):
                    ins = nc.vector.tensor_tensor(m.acc[:, bass.ds(seq * TPB + i, 1), bass.ds(g * (G * DH), G * DH)].rearrange("p o (h d) -> p (o h) d", d=DH),
                                                  blocks[:, i, :, 0:DH], rden[b][:, i, :].unsqueeze(2).to_broadcast([P, G, DH]), ALU.mult)
                ins.then_inc(s.ctx_ready, 1)

            def first():
                maxima(0, 0, range(RG))
                split_maxima(0, 0)
                maxima(1, 1, range(AHEAD))

            def both(n, b, before, used):
                maxima(n, b, range(AHEAD, RG))
                split_maxima(n, b)
                if not isinstance(n, int):
                    maxima(n + 1, (b + 1) % BUF, range(AHEAD))
                normalize(n - 1, before)

            steps(v, first, both, lambda: normalize(STEPS - 1, 1))

        @block.tensor
        def _(pe):
            pe.sem_inc(s.weighted, 2)
            pe.sem_inc(s.ctxT_done, 1)

            def scores(n, b, used, k):
                i, hp = TPB - 1 - k // 2, k % 2
                if k == 0:
                    pe.wait_ge(s.qs_in[b], used * 64 + 64)
                pe.wait_ge(s.row_max, n * RG + k + 1)
                for o in range(2):
                    h = 2 * hp + o
                    nc.tensor.matmul(ps_s[:, k % 2, o, 0:(i + 1) * P], qs[b][0:KS, h, i * P:(i + 1) * P], ks[b][0:KS, 0:(i + 1) * P], start=True, stop=False)
                    last = nc.tensor.matmul(ps_s[:, k % 2, o, i * P:(i + 1) * P], m.ident16[:], m.causal[:], start=False, stop=True)
                last.then_inc(s.scores, 1)

            def turn_maxima(n, b):
                pe.wait_ge(s.max_low, n + 1)
                if not (isinstance(n, int) and n == 0):
                    pe.wait_ge(s.ctx_ready, n)
                nc.tensor.transpose(ps_x.bitcast(BF16)[0:2 * G * TPB, 0:P], max_hl[b][:], m.ident16[:]).then_inc(s.maxT_turned, 1)

            def scoresT(n, b, used, k):
                j, h = k // G, k % G
                if k == 0:
                    pe.wait_ge(s.max_in[b], used * 32 + 64)
                    pe.wait_ge(s.v_in, n + 1)
                pe.wait_ge(s.exps, n * CG + k + 1)
                nc.tensor.matmul(ps_st[:, k % 2, 0:T - j * P], ks[b][0:KM, j * P:(j + 1) * P], qs[b][0:KM, h, j * P:T], start=True, stop=True).then_inc(s.scoresT, 1)

            def weighted(n, b, j):
                pe.wait_ge(s.masked, n * TPB + j + 1)
                if j == 0:
                    pe.wait_ge(s.ctxT_ready, n + 1)
                for h in range(G):
                    last = nc.tensor.matmul(ps_o[h * HB:(h + 1) * HB, j * P:T], vs[b][:, j, :], pT[j % 2][:, h, 0:T - j * P],
                                            start=j == 0, stop=j == TPB - 1)
                last.then_inc(s.weighted, 1)

            def turn_context(n, b, turned):
                pe.wait_ge(s.maxT_ready, turned)
                pe.wait_ge(s.ctx_ready, n + 1)
                pe.wait_ge(s.ctxT_ready, n + 2)
                for i in range(TPB):
                    last = nc.tensor.transpose(ps_x[:, i * P:(i + 1) * P], ctxT[b][:, i * P:(i + 1) * P], m.ident[:])
                last.then_inc(s.ctxT_done, 1)

            def both(n, b, before, used):
                used_before = used - (1 if b == 0 else 0)
                after, used_after = (b + 1) % BUF, used + (1 if b == BUF - 1 else 0)
                for k in range(0, CG, 2):
                    scoresT(n - 1, before, used_before, k)
                    scoresT(n - 1, before, used_before, k + 1)
                    if AHEAD + k // 2 < RG:
                        scores(n, b, used, AHEAD + k // 2)
                    if k + 2 == TURN:
                        turn_maxima(n, b)
                    if k % G and k > G:
                        weighted(n - 1, before, k // G - 1)
                for k in range(AHEAD):
                    if not isinstance(n, int):
                        scores(n + 1, after, used_after, k)
                    if k == 0:
                        weighted(n - 1, before, TPB - 1)
                turn_context(n - 1, before, n + 1)

            def first():
                for k in range(RG):
                    scores(0, 0, 0, k)
                turn_maxima(0, 0)
                for k in range(AHEAD):
                    scores(1, 1, 0, k)
                pe.wait_ge(s.ones_ready, BUF)

            def last():
                n = STEPS - 1
                for j in range(TPB):
                    for h in range(G):
                        scoresT(n, 1, STEPS // BUF, j * G + h)
                    if j:
                        weighted(n, 1, j - 1)
                weighted(n, 1, TPB - 1)
                turn_context(n, 1, n + 1)

            steps(pe, first, both, last)


def output_phase(nc, s, m, dram):
    with ExitStack() as ctx:
        sb = lambda n, shape, dt=F32: ctx.enter_context(nc.sbuf_tensor(n, shape, dt))
        ps = lambda n, shape: ctx.enter_context(nc.psum_tensor(n, shape, F32))
        w_raw, g_raw = m.wo_raw, m.router_raw
        wh, wl = sb("wo_h", [P, KD, D], F32R), sb("wo_l", [P, KD, D], F32R)
        gh, gl = sb("router_h", [P, KD, P], F32R), sb("router_l", [P, KD, P], F32R)
        ch, cl = sb("ctx_h", [P, TPB, KD, P], F32R), sb("ctx_l", [P, TPB, KD, P], F32R)
        ct = sb("ctx_tiles", [P, TPB, D])
        yn = sb("o_normed", [P, TPB, D])
        xn = sb("o_xn", [P, TPB, D])
        logitsT = sb("logitsT", [NE, T])
        logits = sb("logits", [P, NT, NE])
        best, best_at = sb("best", [P, NT, 8]), sb("best_at", [P, NT, 8], U32)
        top_at = sb("top_at", [P, NT, 2])
        gap, wgt = sb("top_gap", [P, NT]), sb("top_weight", [P, 3, NT])
        expert = sb("expert_index", [P, NE])
        one_hot = w_raw[:, 0, :].rearrange("p (r t e) -> p r t e", r=2, t=NT)
        ps_t = ps("o_ps_t", [P, 2, KD, P])
        ps_o = ps("o_ps", [P, TPB, D])
        ps_g = ps("o_ps_g", [P, T])
        ps_l = ps("o_ps_l", [P, T])
        block = ctx.enter_context(nc.Block(no_gpsimd_drain=True))

        @block.sync
        def _(sp):
            sp.wait_ge(s.wo_l, 1)
            sp.dma_start(m.first_w[:, 0:KD * 2 * P].rearrange("p (k n) -> p k n", k=KD),
                         dram.moe_gate_up[0:1].rearrange("u (k p) n -> p (u k) n", p=P)).then_inc(s.moe.w_in[0], 16)
            sp.dma_start(m.first_w[:, KD * 2 * P:NW], dram.moe_down[0:1].rearrange("u p n -> p (u n)")).then_inc(s.moe.w_in[0], 16)

        @block.gpsimd
        def _(pool):
            nc.gpsimd.iota(expert[:], [[1, NE]], base=0, channel_multiplier=0, allow_small_or_imprecise_dtypes=True).then_inc(s.expert_index, 1)
            with pool.Fori(0, NB) as c:
                for t in range(TPB):
                    tok = bass.ds(c * TPB + t, 1)
                    wait_apart(pool, s, s.o_yn, c * TPB + t + 1 + TPB)
                    nc.gpsimd.tensor_tensor(m.x[:, tok, :], m.x[:, tok, :], yn[:, t:t + 1, :], ALU.add).then_inc(s.o_x, 1)
            pool.wait_ge(s.o_ct, NT)
            zero_last_chunk(nc, pool, s, m, 1)

        @block.scalar
        def _(a):
            nc.scalar.preload_act_table(ACT.Sqrt)
            a.sem_inc(s.logitsT, 1)
            a.sem_inc(s.logits, 1)

            def context(c):
                for t in range(TPB):
                    a.wait_ge(s.o_tr, c * TPB + t + 1)
                    nc.scalar.copy(ct[:, t:t + 1, :], m.acc[:, bass.ds(c * TPB + t, 1), :]).then_inc(s.o_ct, 1)

            def context_high(c):
                for t in range(TPB):
                    a.wait_ge(s.o_tr, c * TPB + t + 1 + TPB)
                    a.wait_ge(s.o_done, c * TPB + t + 1)
                    nc.scalar.copy(ch[:, t], ps_t[:, t % 2]).then_inc(s.o_ch, 1)

            def norm_high(c):
                ln_deviation(nc, a, m, s.norm_b2, c)
                for t in range(TPB):
                    a.wait_ge(s.b2_tr, c * TPB + t + 1)
                    nc.scalar.copy(m.xnh[:, :, bass.ds(c * T + t * P, P)], ps_t[:, t % 2]).then_inc(s.b2_h, 1)

            def router(c):
                a.wait_ge(s.router_done, c + 1)
                nc.scalar.copy(logitsT[:], ps_g[0:NE, :]).then_inc(s.logitsT, 1)
                a.wait_ge(s.logits_turned, c + 1)
                nc.scalar.copy(logits[:, bass.ds(c * TPB, TPB), :], ps_l[:, 0:TPB * NE].rearrange("p (t e) -> p t e", e=NE)).then_inc(s.logits, 1)

            context(0)
            a.wait_ge(s.wo_in, 16)
            nc.scalar.copy(wh[:], w_raw[:]).then_inc(s.wo_h, 1)
            context_high(0)
            a.wait_ge(s.router_in, 16)
            nc.scalar.copy(gh[:], g_raw[:]).then_inc(s.router_h, 1)
            with a.Fori(0, NB - 1) as c:
                ln_deviation(nc, a, m, s.norm_b1, c)
                context(c + 1)
                context_high(c + 1)
                norm_high(c)
                router(c)
            ln_deviation(nc, a, m, s.norm_b1, NB - 1)
            norm_high(NB - 1)
            router(NB - 1)
            a.wait_ge(s.top_gap, 1)
            nc.scalar.activation(wgt[:, 0, :], gap[:], ACT.Exp).then_inc(s.top_exp, 1)

        @block.vector
        def _(v):
            v.sem_inc(s.o_cl, 2)
            v.sem_inc(s.b2_l, 1)
            v.sem_inc(s.o_yn, TPB)
            v.wait_ge(s.wo_h, 1)
            nc.vector.tensor_tensor(wl[:], w_raw[:], wh[:], ALU.subtract).then_inc(s.wo_l, 1)

            def context_low(c):
                for t in range(TPB):
                    v.wait_ge(s.o_ch, c * TPB + t + 1)
                    nc.vector.tensor_tensor(cl[:, t], ps_t[:, t % 2], ch[:, t], ALU.subtract).then_inc(s.o_cl, 1)

            def product_norm(c):
                v.wait_ge(s.o_done, c * TPB + TPB + TPB)
                ln_moments(nc, v, s, s.norm_b1, [ps_o[:, t, :] for t in range(TPB)], c)
                ln_rstd(nc, v, s.norm_b1, c)
                for t in range(TPB):
                    ln_apply(nc, s.norm_b1, t, yn[:, t, :], ps_o[:, t, :]).then_inc(s.o_yn, 1)

            def x_norm(c):
                wait_apart(v, s, s.o_x, c * TPB + TPB)
                ln_moments(nc, v, s, s.norm_b2, [m.x[:, bass.ds(c * TPB + t, 1), :] for t in range(TPB)], c)
                ln_rstd(nc, v, s.norm_b2, c)
                for t in range(TPB):
                    ln_apply(nc, s.norm_b2, t, xn[:, t:t + 1, :], m.x[:, bass.ds(c * TPB + t, 1), :]).then_inc(s.b2_xn, 1)
                for t in range(TPB):
                    cols = bass.ds(c * T + t * P, P)
                    v.wait_ge(s.b2_h, c * TPB + t + 1)
                    nc.vector.tensor_tensor(m.xnl[:, :, cols], ps_t[:, t % 2], m.xnh[:, :, cols], ALU.subtract).then_inc(s.b2_l, 1)

            context_low(0)
            v.wait_ge(s.router_h, 1)
            nc.vector.tensor_tensor(gl[:], g_raw[:], gh[:], ALU.subtract).then_inc(s.router_l, 1)
            with v.Fori(0, NB - 1) as c:
                product_norm(c)
                context_low(c + 1)
                x_norm(c)
            product_norm(NB - 1)
            x_norm(NB - 1)
            v.wait_ge(s.logits, NB + 1)
            for t in range(NT):
                nc.vector.max(best[:, t, :], logits[:, t, :]).then_inc(s.best, 1)
            v.wait_ge(s.best, NT)
            for t in range(NT):
                nc.vector.max_index(best_at[:, t, :], best[:, t, :], logits[:, t, :]).then_inc(s.best_at, 1)
            v.wait_ge(s.best_at, NT)
            nc.vector.tensor_copy(top_at[:], best_at[:, :, 0:2]).then_inc(s.best_at, 1)
            nc.vector.tensor_tensor(gap[:], best[:, :, 1], best[:, :, 0], ALU.subtract).then_inc(s.top_gap, 1)
            v.wait_ge(s.top_exp, 1)
            nc.vector.tensor_scalar_add(wgt[:, 1, :], wgt[:, 0, :], 1.0).then_inc(s.top_weight, 1)
            v.wait_ge(s.top_weight, 1)
            nc.vector.reciprocal(wgt[:, 1, :], wgt[:, 1, :]).then_inc(s.top_weight, 1)
            v.wait_ge(s.top_weight, 2)
            nc.vector.tensor_tensor(wgt[:, 2, :], wgt[:, 0, :], wgt[:, 1, :], ALU.mult).then_inc(s.top_weight, 1)
            v.wait_ge(s.top_weight, 3)
            v.wait_ge(s.expert_index, 1)
            v.wait_ge(s.best_at, NT + 1)
            for r in range(2):
                nc.vector.tensor_tensor(one_hot[:, r], expert[:].unsqueeze(1).to_broadcast([P, NT, NE]),
                                        top_at[:, :, r].unsqueeze(2).to_broadcast([P, NT, NE]), ALU.is_equal).then_inc(s.combine, 1)
            v.wait_ge(s.combine, 2)
            for r in range(2):
                nc.vector.tensor_tensor(one_hot[:, r], one_hot[:, r], wgt[:, 1 + r, :].unsqueeze(2).to_broadcast([P, NT, NE]), ALU.mult).then_inc(s.combine, 1)
            v.wait_ge(s.combine, 4)
            nc.vector.tensor_tensor(m.combine[:, :, 0:NE], one_hot[:, 0], one_hot[:, 1], ALU.add).then_inc(s.combine, 1)
            v.wait_ge(s.combine, 5)

        @block.tensor
        def _(pe):
            pe.sem_inc(s.o_done, TPB)
            pe.sem_inc(s.o_tr, TPB)

            def turn_context(c):
                for t in range(TPB):
                    pe.wait_ge(s.o_ct, c * TPB + t + 1)
                    pe.wait_ge(s.o_cl, c * TPB + t + 1)
                    if t < 2 and not isinstance(c, int):
                        pe.wait_ge(s.b2_l, (c - 1) * TPB + 1)
                    for k in range(KD):
                        last = nc.tensor.transpose(ps_t[:, t % 2, k, :], ct[:, t, k * P:(k + 1) * P], m.ident[:])
                    last.then_inc(s.o_tr, 1)

            def output_product(c, t):
                pe.wait_ge(s.o_cl, c * TPB + t + 3)
                pe.wait_ge(s.o_yn, c * TPB + t + 1)
                for k in range(KD):
                    last = split_product(nc, ps_o[:, t, :], ch[:, t, k, :], cl[:, t, k, :], wh[:, k, :], wl[:, k, :], k == 0, k == KD - 1)
                last.then_inc(s.o_done, 1)

            def turn_norm(c, t):
                pe.wait_ge(s.b2_xn, c * TPB + t + 1)
                if t >= 2:
                    pe.wait_ge(s.b2_l, c * TPB + t)
                elif not isinstance(c, int):
                    pe.wait_ge(s.o_cl, (c + 1) * TPB + t + 3 + 2)
                for k in range(KD):
                    last = nc.tensor.transpose(ps_t[:, t % 2, k, :], xn[:, t, k * P:(k + 1) * P], m.ident[:])
                last.then_inc(s.b2_tr, 1)

            def router(c):
                pe.wait_ge(s.b2_l, c * TPB + TPB + 1)
                pe.wait_ge(s.logitsT, c + 1)
                for k in range(KD):
                    last = split_product(nc, ps_g[:], gh[:, k, :], gl[:, k, :], m.xnh[:, k, bass.ds(c * T, T)], m.xnl[:, k, bass.ds(c * T, T)], k == 0, k == KD - 1)
                last.then_inc(s.router_done, 1)
                pe.wait_ge(s.logitsT, c + 2)
                wait_apart(pe, s, s.logits, c + 1)
                for t in range(TPB):
                    last = nc.tensor.transpose(ps_l[:, t * NE:(t + 1) * NE], logitsT[:, t * P:(t + 1) * P], m.ident[0:NE, 0:NE])
                last.then_inc(s.logits_turned, 1)

            turn_context(0)
            pe.wait_ge(s.wo_l, 1)
            for t in range(TPB):
                output_product(0, t)
            pe.wait_ge(s.router_l, 1)
            with pe.Fori(0, NB - 1) as c:
                turn_context(c + 1)
                for t in range(TPB):
                    if t >= 2:
                        turn_norm(c, 2 * t - 4)
                        turn_norm(c, 2 * t - 3)
                    output_product(c + 1, t)
                router(c)
            for t in range(TPB):
                turn_norm(NB - 1, t)
            router(NB - 1)


def final_steps(nc, s, m, dram):
    norm = s.norm_c4
    tile = lambda whole, c, t: whole[:, c * TPB + t:c * TPB + t + 1, :]

    def vector(v, c, summed):
        v.wait_ge(s.ff.summed, summed)
        ln_moments(nc, v, s, norm, [tile(m.acc, c, t) for t in range(TPB)], NB + c)
        ln_rstd(nc, v, norm, NB + c)
        for t in range(TPB):
            ln_apply(nc, norm, t, tile(m.acc, c, t), tile(m.acc, c, t)).then_inc(s.d_yn, 1)

    def scalar(a, c):
        ln_deviation(nc, a, m, norm, NB + c)

    def pool_sums(pool, c):
        for t in range(TPB):
            pool.wait_ge(s.d_yn, c * TPB + t + 1)
            nc.gpsimd.tensor_tensor(tile(m.x, c, t), tile(m.x, c, t), tile(m.acc, c, t), ALU.add).then_inc(s.d_x, 1)

    def store(sp, c):
        sp.wait_ge(s.d_x, c * TPB + TPB)
        sp.dma_start(dram.out[c * T:(c + 1) * T, :].rearrange("(t p) d -> p t d", p=P),
                     m.x[:, c * TPB:(c + 1) * TPB, :]).then_inc(s.stored, 16)

    return vector, scalar, pool_sums, store


def units_phase(nc, s, q, m, dram, name, units, up_down, lora=None):
    STEPS = units * NB
    with ExitStack() as ctx:
        sb = lambda n, shape, dt=F32: ctx.enter_context(nc.sbuf_tensor(f"{name}_{n}", shape, dt))
        ps = lambda n, shape: ctx.enter_context(nc.psum_tensor(f"{name}_{n}", shape, F32))
        w_raw = [m.first_w, sb("w_raw1", [P, NW])]
        wh = [sb(f"wh{i}", [P, NW], F32R) for i in range(2)]
        wl = [sb(f"wl{i}", [P, NW], F32R) for i in range(2)]
        silu = [sb(f"silu{i}", [P, T]) for i in range(2)]
        act = [sb(f"act{i}", [P, T]) for i in range(2)]
        acth = [sb(f"acth{i}", [P, T], F32R) for i in range(2)]
        actl = [sb(f"actl{i}", [P, T], F32R) for i in range(2)]
        if lora:
            a_raw, a_split = sb("lora_a_raw", [LORA_ROWS, 3, D]), sb("lora_a", [LORA_ROWS, 3, D], F32R)
            b_raw = [sb(f"lora_b_raw{i}", [LORA_ROWS, 3, P]) for i in range(2)]
            b_split = [sb(f"lora_b{i}", [LORA_ROWS, 3, P], F32R) for i in range(2)]
            final_vector, final_scalar, final_pool, store = final_steps(nc, s, m, dram)
        ps_g = ps("ps_gate", [P, 2, T])
        ps_u = ps("ps_up", [P, 2, T])
        ps_d = ps("ps_down", [P, TPB, D])
        block = ctx.enter_context(nc.Block(no_gpsimd_drain=True))
        gate_up = lambda w, k, half: w[:, k * 2 * P + half * P:k * 2 * P + (half + 1) * P]
        down = lambda w: w[:, KD * 2 * P:NW]

        def unit_loop(eng, unit):
            unit(0, 0, False)
            with eng.Fori(0, (units - 1) // 2 - units % 2) as i:
                unit(i * 2 + 1, 1, False)
                unit(i * 2 + 2, 0, False)
            if units % 2:
                unit(units - 2, 1, False)
            unit(units - 1, (units - 1) % 2, True)

        @block.sync
        def _(sp):
            if lora:
                sp.dma_start(a_raw[:], dram.lora_shared).then_inc(q.lora_in, 16)

            def load(u, b):
                if not (isinstance(u, int) and u < 2):
                    sp.wait_ge(q.split_l, u - 1)
                src_u, src_d = up_down
                one = bass.ds(u, 1)
                sp.dma_start(w_raw[b][:, 0:KD * 2 * P].rearrange("p (k n) -> p k n", k=KD),
                             src_u[one].rearrange("u (k p) n -> p (u k) n", p=P)).then_inc(q.w_in[b], 16)
                sp.dma_start(down(w_raw[b]), src_d[one].rearrange("u p n -> p (u n)")).then_inc(q.w_in[b], 16)
                if lora:
                    sp.dma_start(b_raw[b][:], dram.lora_unit[one].rearrange("u r a n -> r (u a) n")).then_inc(q.w_in[b], 16)

            if lora:
                load(0, 0)
            load(1, 1)
            if not lora:
                for dst, src in ((m.w1, dram.w1), (m.w2, dram.w2T)):
                    sp.dma_start(dst[:], src.rearrange("(k p) n -> p k n", p=P)).then_inc(s.w12_in, 16)
            with sp.Fori(0, (units - 2) // 2) as i:
                load(i * 2 + 2, 0)
                load(i * 2 + 3, 1)
            if units % 2:
                load(units - 1, 0)
            if lora:
                for c in range(NB):
                    store(sp, c)
                sp.wait_ge(s.stored, 16 * NB)

        if lora:
            @block.gpsimd
            def _(pool):
                for c in range(NB):
                    final_pool(pool, c)

        W_IN = 48 if lora else 32

        def split_high(a, u, b):
            if lora:
                a.wait_ge(q.folded, u * 3 + 3)
            else:
                a.wait_ge(q.w_in[b], (u // 2) * W_IN + W_IN)
            if not (isinstance(u, int) and u < 2):
                a.wait_ge(q.down_done, (u - 1) * STEP_D)
            nc.scalar.copy(wh[b][:], w_raw[b][:]).then_inc(q.split_h, 1)

        STEP_D = NB * TPB
        SPLIT_AT = 2 if lora else 1

        @block.scalar
        def _(a):
            def lora_high(u, b):
                a.wait_ge(q.w_in[b], (u // 2) * W_IN + W_IN)
                nc.scalar.copy(b_split[b][:], b_raw[b][:]).then_inc(q.lora_h, 1)

            def unit(u, b, tail):
                if lora and not tail:
                    lora_high(u + 1, 1 - b)
                for c in range(NB):
                    a.wait_ge(q.gate_up, u * NB + c + 1)
                    nc.scalar.activation(silu[c % 2][:], ps_g[:, c % 2, :], ACT.Silu).then_inc(q.silu, 1)
                    a.wait_ge(q.product, u * NB + c + 1 + 2)
                    if not (isinstance(u, int) and u == 0 and c < 2):
                        a.wait_ge(q.down_done, (u * NB + c - 1) * TPB)
                    nc.scalar.copy(acth[c % 2][:], act[c % 2][:]).then_inc(q.act_h, 1)
                    if lora and tail and c:
                        final_scalar(a, c - 1)
                    if c == SPLIT_AT and not tail:
                        split_high(a, u + 1, 1 - b)
            if lora:
                a.wait_ge(q.lora_in, 16)
                nc.scalar.copy(a_split[:], a_raw[:]).then_inc(q.lora_h, 1)
                lora_high(0, 0)
            split_high(a, 0, 0)
            unit_loop(a, unit)
            if lora:
                final_scalar(a, NB - 1)

        @block.vector
        def _(v):
            v.sem_inc(q.product, 2)
            v.sem_inc(q.summed, TPB)

            def lora_low(u, b):
                low = slice(2 * GROUP, 3 * GROUP)
                v.wait_ge(q.lora_h, u + 2)
                nc.vector.tensor_tensor(b_split[b][low], b_raw[b][low], b_split[b][low], ALU.subtract).then_inc(q.lora_l, 1)

            def fold(u, b, i, bank):
                if i == 0:
                    v.wait_ge(q.w_in[b], (u // 2) * W_IN + W_IN)
                v.wait_ge(q.low_rank, u * 3 + i + 1)
                if i < 2:
                    dst = w_raw[b][:, 0:KD * 2 * P].rearrange("p (k a n) -> p k a n", k=KD, a=2)[:, :, i, :]
                    src = ps_d[:, bank, :].rearrange("p (k n) -> p k n", k=KD)
                else:
                    dst, src = down(w_raw[b]), ps_d[:, bank, :]
                nc.vector.tensor_tensor(dst, dst, src, ALU.add).then_inc(q.folded, 1)

            def prepare(u, b):
                v.wait_ge(q.split_h, u + 1)
                nc.vector.tensor_tensor(wl[b][:], w_raw[b][:], wh[b][:], ALU.subtract).then_inc(q.split_l, 1)

            def product(u, c):
                b = c % 2
                n = u * NB + c
                v.wait_ge(q.silu, n + 1)
                nc.vector.tensor_tensor(act[b][:], silu[b][:], ps_u[:, b, :], ALU.mult).then_inc(q.product, 1)

            def product_low(u, c):
                b = c % 2
                n = u * NB + c
                v.wait_ge(q.act_h, n + 1)
                nc.vector.tensor_tensor(actl[b][:], act[b][:], acth[b][:], ALU.subtract).then_inc(q.act_l, 1)

            def sums(u, c):
                for t in range(TPB):
                    v.wait_ge(q.down_done, u * STEP_D + c * TPB + t + 1)
                    acc = m.acc[:, c * TPB + t, :]
                    if isinstance(u, int) and u == 0:
                        nc.vector.tensor_scalar_mul(acc, ps_d[:, t, :], m.combine[:, c * TPB + t, 0:1] if not lora else 1.0).then_inc(q.summed, 1)
                        continue
                    nc.vector.scalar_tensor_tensor(out=acc, in0=ps_d[:, t, :], scalar=m.combine[:, c * TPB + t, bass.ds(u, 1)] if not lora else 1.0,
                                                   in1=acc, op0=ALU.mult, op1=ALU.add).then_inc(q.summed, 1)

            def unit(u, b, tail):
                if lora and not tail:
                    lora_low(u + 1, 1 - b)
                for c in range(NB):
                    product(u, c)
                    if lora and c < 3 and not tail:
                        fold(u + 1, 1 - b, c, TPB - 1)
                    product_low(u, c)
                    if c:
                        sums(u, c - 1)
                        if lora and tail:
                            final_vector(v, c - 1, u * STEP_D + c * TPB + TPB)
                    elif not isinstance(u, int) or u:
                        sums(u - 1, NB - 1)
                    if c == SPLIT_AT and not tail:
                        prepare(u + 1, 1 - b)

            if lora:
                low = slice(GROUP, 2 * GROUP)
                v.wait_ge(q.lora_h, 1)
                nc.vector.tensor_tensor(a_split[low], a_raw[low], a_split[low], ALU.subtract).then_inc(q.lora_l, 1)
                lora_low(0, 0)
                for i in range(3):
                    fold(0, 0, i, i)
            prepare(0, 0)
            unit_loop(v, unit)
            sums(units - 1, NB - 1)
            if lora:
                final_vector(v, NB - 1, units * STEP_D + TPB)
            v.wait_ge(q.summed, units * STEP_D + TPB)

        @block.tensor
        def _(pe):
            def low_rank(u, b, i, bank):
                if i == 0:
                    pe.wait_ge(q.lora_l, u + 2)
                if i < 2:
                    for k in range(KD):
                        last = nc.tensor.matmul(ps_d[:, bank, k * P:(k + 1) * P], a_split[:, i, k * P:(k + 1) * P], b_split[b][:, i, :], start=True, stop=True)
                else:
                    last = nc.tensor.matmul(ps_d[:, bank, :], b_split[b][:, 2, :], a_split[:, 2, :], start=True, stop=True)
                last.then_inc(q.low_rank, 1)

            def gate_up_products(u, b, c):
                n = u * NB + c
                if c == 0:
                    pe.wait_ge(q.split_l, u + 1)
                pe.wait_ge(q.product, n + 1)
                for half, bank in ((0, ps_g), (1, ps_u)):
                    for k in range(KD):
                        last = split_product(nc, bank[:, c % 2, :], gate_up(wh[b], k, half), gate_up(wl[b], k, half),
                                             m.xnh[:, k, c * T:(c + 1) * T], m.xnl[:, k, c * T:(c + 1) * T], k == 0, k == KD - 1)
                last.then_inc(q.gate_up, 1)

            def down_products(u, b, c, folded=None):
                n = u * NB + c
                pe.wait_ge(q.act_l, n + 1)
                for t in range(TPB):
                    if t == TPB - 1 and folded is not None:
                        pe.wait_ge(q.folded, folded)
                    pe.wait_ge(q.summed, n * TPB + t + 1)
                    cols = slice(t * P, (t + 1) * P)
                    split_product(nc, ps_d[:, t, :], acth[c % 2][:, cols], actl[c % 2][:, cols],
                                  down(wh[b]), down(wl[b])).then_inc(q.down_done, 1)

            def unit(u, b, tail):
                for c in range(NB):
                    gate_up_products(u, b, c)
                    folded = None
                    if lora and c < 3 and not tail:
                        if isinstance(u, int) and u == 0 and c == 1:
                            pe.wait_ge(q.folded, 3 + 1)
                        if not (isinstance(u, int) and u == 0 and c == 0):
                            pe.wait_ge(q.summed, (u * NB + c) * TPB)
                        low_rank(u + 1, 1 - b, c, TPB - 1)
                        folded = (u + 1) * 3 + c + 1
                    if c:
                        down_products(u, b, c - 1, folded)
                    elif not isinstance(u, int) or u:
                        down_products(u - 1, 1 - b, NB - 1, folded)
            if lora:
                for i in range(3):
                    low_rank(0, 0, i, i)

            unit_loop(pe, unit)
            down_products(units - 1, (units - 1) % 2, NB - 1)


def mix_norms(nc, s, m, yn, xn):
    tiles = lambda whole, c: [whole[:, bass.ds(c * TPB + t, 1), :] for t in range(TPB)]

    def vector_sum_norm(v, c):
        ln_moments(nc, v, s, s.norm_c1, tiles(m.acc, c), c)
        ln_rstd(nc, v, s.norm_c1, c)
        for t in range(TPB):
            ln_apply(nc, s.norm_c1, t, yn[:, t:t + 1, :], tiles(m.acc, c)[t]).then_inc(s.c1_yn, 1)

    def vector_x_moments(v, c):
        wait_apart(v, s, s.c1_x, c * TPB + TPB)
        ln_moments(nc, v, s, s.norm_c2, tiles(m.x, c), c)

    def vector_x_norm(v, c):
        ln_rstd(nc, v, s.norm_c2, c)
        for t in range(TPB):
            ln_apply(nc, s.norm_c2, t, xn[:, t:t + 1, :], tiles(m.x, c)[t]).then_inc(s.c2_xn, 1)

    def pool_sums(pool, c):
        for t in range(TPB):
            tok = bass.ds(c * TPB + t, 1)
            wait_apart(pool, s, s.c1_yn, c * TPB + t + 1)
            nc.gpsimd.tensor_tensor(m.x[:, tok, :], m.x[:, tok, :], yn[:, t:t + 1, :], ALU.add).then_inc(s.c1_x, 1)

    return vector_sum_norm, vector_x_moments, vector_x_norm, pool_sums


def weight_product_phase(nc, s, m, dram, ah, al, norms):
    vector_sum_norm, vector_x_moments, vector_x_norm, pool_sums = norms
    with ExitStack() as ctx:
        sb = lambda n, shape, dt=F32: ctx.enter_context(nc.sbuf_tensor(n, shape, dt))
        w1, w2, mask = m.w1, m.w2, sb("mask_raw", [P, KD, D])
        masked = sb("w_masked", [P, KD, D])
        ps_w = ctx.enter_context(nc.psum_tensor("ps_w", [P, KD, D], F32))
        block = ctx.enter_context(nc.Block(no_gpsimd_drain=True))

        @block.sync
        def _(sp):
            sp.dma_start(mask[:], dram.mask.rearrange("(k p) n -> p k n", p=P)).then_inc(s.mask_in, 16)

        @block.tensor
        def _(pe):
            pe.wait_ge(s.w12_in, 32)
            for j in range(KD):
                for k in range(KD):
                    last = nc.tensor.matmul(ps_w[:, j, :], w1[:, k, j * P:(j + 1) * P], w2[:, k, :], start=k == 0, stop=k == KD - 1)
                last.then_inc(s.w_product, 1)

        @block.gpsimd
        def _(pool):
            pool_sums(pool, 0)

        @block.vector
        def _(v):
            def masked_product(j):
                v.wait_ge(s.w_product, j + 1)
                nc.vector.tensor_tensor(masked[:, j, :], ps_w[:, j, :], mask[:, j, :], ALU.mult).then_inc(s.w_masked, 1)

            def low_part(j):
                v.wait_ge(s.w_high, j + 1)
                nc.vector.tensor_tensor(al[:, j, :], masked[:, j, :], ah[:, j, :], ALU.subtract).then_inc(s.w_low, 1)

            vector_sum_norm(v, 0)
            v.wait_ge(s.mask_in, 16)
            masked_product(0)
            low_part(0)
            masked_product(1)
            low_part(1)
            vector_x_moments(v, 0)
            masked_product(2)
            vector_x_norm(v, 0)
            masked_product(3)
            low_part(2)
            low_part(3)
            v.wait_ge(s.w_low, KD)

        @block.scalar
        def _(a):
            ln_deviation(nc, a, m, s.norm_c1, 0)
            for j in range(KD):
                a.wait_ge(s.w_masked, j + 1)
                nc.scalar.copy(ah[:, j, :], masked[:, j, :]).then_inc(s.w_high, 1)
                if j == 1:
                    ln_deviation(nc, a, m, s.norm_c2, 0)


def mix_phase(nc, s, m, dram):
    with ExitStack() as ctx:
        sb = lambda n, shape, dt=F32: ctx.enter_context(nc.sbuf_tensor(n, shape, dt))
        ps = lambda n, shape: ctx.enter_context(nc.psum_tensor(n, shape, F32))
        ah, al = sb("mix_wh", [P, KD, D], F32R), sb("mix_wl", [P, KD, D], F32R)
        yn = sb("mix_normed", [P, TPB, D])
        xn = sb("mix_xn", [P, TPB, D])
        norms = mix_norms(nc, s, m, yn, xn)
        vector_sum_norm, vector_x_moments, vector_x_norm, pool_sums = norms
        weight_product_phase(nc, s, m, dram, ah, al, norms)
        gn, b2 = m.w1, m.w2[:, 0, :]
        xh, xl = sb("mix_xh", [P, TPB, KD, P], F32R), sb("mix_xl", [P, TPB, KD, P], F32R)
        ps_t = ps("mix_ps_t", [P, 2, KD, P])
        ps_t4 = ps("mix_ps_t4", [P, 2, KD, P])
        ps_y = ps("mix_ps_y", [P, TPB, D])
        block = ctx.enter_context(nc.Block(no_gpsimd_drain=True))
        x_tiles = lambda c: [m.x[:, bass.ds(c * TPB + t, 1), :] for t in range(TPB)]

        @block.sync
        def _(sp):
            sp.dma_start(b2, dram.b2.to_broadcast([P, D])).then_inc(s.b2_in, 16)

        @block.gpsimd
        def _(pool):
            def gelu_sums(c):
                for t in range(TPB):
                    tok = bass.ds(c * TPB + t, 1)
                    wait_apart(pool, s, s.c3_yn, c * TPB + t + 1)
                    nc.gpsimd.tensor_tensor(m.x[:, tok, :], m.x[:, tok, :], gn[:, t:t + 1, :], ALU.add).then_inc(s.c3_x, 1)

            with pool.Fori(0, NB - 1) as c:
                pool_sums(pool, c + 1)
                gelu_sums(c)
            gelu_sums(NB - 1)
            zero_last_chunk(nc, pool, s, m, 2)

        @block.scalar
        def _(a):
            def high_parts(c):
                for t in range(TPB):
                    a.wait_ge(s.c2_tr, c * TPB + t + 1)
                    a.wait_ge(s.mixed, c * TPB + t + 1)
                    nc.scalar.copy(xh[:, t], ps_t[:, t % 2]).then_inc(s.c2_h, 1)

            def gelu(c):
                for t in range(TPB):
                    a.wait_ge(s.biased, c * TPB + t + 1)
                    nc.scalar.activation(gn[:, t, :], gn[:, t, :], ACT.Gelu).then_inc(s.gelu, 1)

            def last_norm(c):
                ln_deviation(nc, a, m, s.norm_c4, c)
                for t in range(TPB):
                    a.wait_ge(s.c4_tr, c * TPB + t + 1)
                    nc.scalar.copy(m.xnh[:, :, bass.ds(c * T + t * P, P)], ps_t4[:, t % 2]).then_inc(s.c4_h, 1)

            high_parts(0)
            with a.Fori(0, NB - 1) as c:
                ln_deviation(nc, a, m, s.norm_c1, c + 1)
                gelu(c)
                ln_deviation(nc, a, m, s.norm_c2, c + 1)
                ln_deviation(nc, a, m, s.norm_c3, c)
                high_parts(c + 1)
                last_norm(c)
            gelu(NB - 1)
            ln_deviation(nc, a, m, s.norm_c3, NB - 1)
            last_norm(NB - 1)

        @block.vector
        def _(v):
            def low_parts(c):
                for t in range(TPB):
                    v.wait_ge(s.c2_h, c * TPB + t + 1)
                    v.wait_ge(s.mixed, c * TPB + t + 1)
                    nc.vector.tensor_tensor(xl[:, t], ps_t[:, t % 2], xh[:, t], ALU.subtract).then_inc(s.c2_l, 1)

            def bias(c):
                for t in range(TPB):
                    v.wait_ge(s.mixed, c * TPB + t + 1 + TPB)
                    nc.vector.tensor_tensor(gn[:, t, :], ps_y[:, t, :], b2, ALU.add).then_inc(s.biased, 1)

            def gelu_moments(c):
                v.wait_ge(s.gelu, c * TPB + TPB)
                ln_moments(nc, v, s, s.norm_c3, [gn[:, t, :] for t in range(TPB)], c)

            def gelu_norm(c):
                ln_rstd(nc, v, s.norm_c3, c)
                for t in range(TPB):
                    ln_apply(nc, s.norm_c3, t, gn[:, t, :], gn[:, t, :]).then_inc(s.c3_yn, 1)

            def last_norm(c):
                wait_apart(v, s, s.c3_x, c * TPB + TPB)
                ln_moments(nc, v, s, s.norm_c4, x_tiles(c), c)
                ln_rstd(nc, v, s.norm_c4, c)
                for t in range(TPB):
                    ln_apply(nc, s.norm_c4, t, xn[:, t:t + 1, :], x_tiles(c)[t]).then_inc(s.c4_xn, 1)
                for t in range(TPB):
                    cols = bass.ds(c * T + t * P, P)
                    v.wait_ge(s.c4_h, c * TPB + t + 1)
                    nc.vector.tensor_tensor(m.xnl[:, :, cols], ps_t4[:, t % 2], m.xnh[:, :, cols], ALU.subtract).then_inc(s.c4_l, 1)

            v.sem_inc(s.c2_l, 2)
            v.sem_inc(s.c4_l, 2)
            low_parts(0)
            v.wait_ge(s.b2_in, 16)
            with v.Fori(0, NB - 1) as c:
                vector_sum_norm(v, c + 1)
                bias(c)
                vector_x_moments(v, c + 1)
                gelu_moments(c)
                vector_x_norm(v, c + 1)
                gelu_norm(c)
                low_parts(c + 1)
                last_norm(c)
            bias(NB - 1)
            gelu_moments(NB - 1)
            gelu_norm(NB - 1)
            last_norm(NB - 1)
            v.wait_ge(s.c4_l, NT + 2)

        @block.tensor
        def _(pe):
            def turn(c, t):
                pe.wait_ge(s.c2_xn, c * TPB + t + 1)
                pe.wait_ge(s.c2_l, c * TPB + t + 1)
                for k in range(KD):
                    last = nc.tensor.transpose(ps_t[:, t % 2, k, :], xn[:, t, k * P:(k + 1) * P], m.ident[:])
                last.then_inc(s.c2_tr, 1)

            def mix(c, t):
                pe.wait_ge(s.c2_l, c * TPB + t + 3)
                for k in range(KD):
                    last = split_product(nc, ps_y[:, t, :], xh[:, t, k, :], xl[:, t, k, :], ah[:, k, :], al[:, k, :], k == 0, k == KD - 1)
                last.then_inc(s.mixed, 1)

            def turn_last(c, t):
                pe.wait_ge(s.c4_xn, c * TPB + t + 1)
                pe.wait_ge(s.c4_l, c * TPB + t + 1)
                for k in range(KD):
                    last = nc.tensor.transpose(ps_t4[:, t % 2, k, :], xn[:, t, k * P:(k + 1) * P], m.ident[:])
                last.then_inc(s.c4_tr, 1)

            def products(c, last_of=None):
                for t in range(TPB):
                    turn(c, t)
                for t in range(TPB):
                    if t >= 2 and last_of is not None:
                        turn_last(last_of, 2 * t - 4)
                        turn_last(last_of, 2 * t - 3)
                    mix(c, t)

            pe.sem_inc(s.mixed, TPB)
            products(0)
            with pe.Fori(0, NB - 1) as c:
                products(c + 1, c)
            for t in range(TPB):
                turn_last(NB - 1, t)


class UnitSemaphores:

    def __init__(self, sem, phase):
        self.w_in = [sem(f"{phase}_w_in{b}") for b in range(2)]
        self.split_h = sem(f"{phase}_split_h")
        self.split_l = sem(f"{phase}_split_l")
        self.gate_up = sem(f"{phase}_gate_up")
        self.silu = sem(f"{phase}_silu")
        self.product = sem(f"{phase}_product")
        self.act_h = sem(f"{phase}_act_h")
        self.act_l = sem(f"{phase}_act_l")
        self.down_done = sem(f"{phase}_down_done")
        self.summed = sem(f"{phase}_summed")


class Norm:

    def __init__(self, sem, sb, name):
        self.stats_ready, self.moments_ready = sem(f"{name}_stats_ready"), sem(f"{name}_moments_ready")
        self.dev_ready, self.rstd_ready = sem(f"{name}_dev_ready"), sem(f"{name}_rstd_ready")
        self.stats, self.mv = sb(f"{name}_stats", [P, TPB, 6]), sb(f"{name}_mv", [P, TPB, 2])
        self.dev, self.rstd = sb(f"{name}_dev", [P, TPB]), sb(f"{name}_rstd", [P, TPB])


class Semaphores:
    def __init__(self, sem, sb):
        self.norm_a1, self.norm_b1, self.norm_b2 = (Norm(sem, sb, n) for n in ("a1", "b1", "b2"))
        self.norm_c1, self.norm_c2, self.norm_c3, self.norm_c4 = (Norm(sem, sb, n) for n in ("c1", "c2", "c3", "c4"))
        self.x_in, self.const, self.qkv_w_in, self.rope_in, self.q_rest, self.q_part0 = (sem(n) for n in "x_in const qkv_w_in rope_in q_rest q_part0".split())
        self.qkT_out, self.rope_parts, self.q_transposed, self.rot_ready, self.qkv_wh, self.qkv_wl = (sem(n) for n in "qkT_out rope_parts q_transposed rot_ready qkv_wh qkv_wl".split())
        self.a1_tr, self.a1_xh, self.a1_xl = (sem(n) for n in "a1_tr a1_xh a1_xl".split())
        self.a1_xn, self.qkv_done, self.v_ready = (sem(n) for n in "a1_xn qkv_done v_ready".split())
        self.ones_ready, self.ctxT_done, self.maxT_ready, self.exps, self.masked, self.maxT_turned = (sem(n) for n in "ones_ready ctxT_done maxT_ready exps masked maxT_turned".split())
        self.scoresT, self.weighted, self.ctxT_ready, self.v_in, self.row_max, self.ctx_ready = (sem(n) for n in "scoresT weighted ctxT_ready v_in row_max ctx_ready".split())
        self.scores, self.max_high, self.max_low, self.rden = (sem(n) for n in "scores max_high max_low rden".split())
        self.passed, self.wo_in, self.router_in, self.expert_index, self.o_yn = (sem(n) for n in "passed wo_in router_in expert_index o_yn".split())
        self.o_x, self.o_tr, self.o_ct, self.wo_h, self.router_h = (sem(n) for n in "o_x o_tr o_ct wo_h router_h".split())
        self.o_done, self.o_ch, self.b2_tr, self.b2_h, self.router_done, self.logitsT = (sem(n) for n in "o_done o_ch b2_tr b2_h router_done logitsT".split())
        self.top_gap, self.top_exp = (sem(n) for n in "top_gap top_exp".split())
        self.o_cl, self.wo_l, self.router_l, self.b2_l, self.b2_xn, self.logits_turned = (sem(n) for n in "o_cl wo_l router_l b2_l b2_xn logits_turned".split())
        self.logits, self.best, self.best_at, self.top_weight = (sem(n) for n in "logits best best_at top_weight".split())
        self.combine, self.q_part1, self.q_part2 = (sem(n) for n in "combine q_part1 q_part2".split())
        self.w12_in, self.w_masked, self.w_product, self.w_high, self.w_low, self.b2_in = (sem(n) for n in "w12_in w_masked w_product w_high w_low b2_in".split())
        self.c1_yn, self.c1_x, self.mask_in, self.c3_yn, self.c3_x, self.c2_tr = (sem(n) for n in "c1_yn c1_x mask_in c3_yn c3_x c2_tr".split())
        self.mixed, self.c2_h, self.biased, self.gelu, self.c4_tr, self.c4_h = (sem(n) for n in "mixed c2_h biased gelu c4_tr c4_h".split())
        self.c2_l, self.c4_l, self.c2_xn, self.c4_xn = (sem(n) for n in "c2_l c4_l c2_xn c4_xn".split())
        self.d_x, self.d_yn, self.stored = (sem(n) for n in "d_x d_yn stored".split())
        self.acc_zero, self.x_first_in, self.wq_in = sem("acc_zero"), sem("x_first_in"), sem("wq_in")
        self.qs_in, self.max_in = ([sem(f"{n}{b}") for b in range(3)] for n in ("qs_in", "max_in"))
        self.moe, self.ff = UnitSemaphores(sem, "moe"), UnitSemaphores(sem, "ff")
        self.ff.lora_in, self.ff.low_rank, self.ff.folded, self.ff.lora_h, self.ff.lora_l = (sem(n) for n in "lora_in low_rank folded lora_h lora_l".split())


class Memory:

    def __init__(self, sb):
        self.x = sb("x", [P, NT, D])
        self.acc = sb("acc", [P, NT, D])
        self.combine = sb("combine", [P, NT, 32])
        self.wo_raw, self.router_raw = sb("wo_raw", [P, KD, D]), sb("router_raw", [P, KD, P])
        self.first_w = self.wo_raw[:, KD - NW // D:KD, :].rearrange("p k n -> p (k n)")
        self.ident, self.ident16 = sb("ident", [P, P]), sb("ident16", [P, P], BF16)
        self.causal = sb("causal", [P, P], BF16)
        self.eps = sb("eps", [P, 1])


class Dram:

    def __init__(self, nc, ins, out):
        self.x, self.rope, self.mask, self.b2 = ins["x"], ins["rope"], ins["mask"], ins["b2"]
        self.wqT, self.wkT, self.wvT, self.woT = ins["wqT"], ins["wkT"], ins["wvT"], ins["woT"]
        self.routerT, self.moe_gate_up, self.moe_down = ins["routerT"], ins["moe_gate_up"], ins["moe_down"]
        self.w1, self.w2T = ins["w1"], ins["w2T"]
        self.ff_gate_up, self.ff_down, self.lora_unit = ins["ff_gate_up"], ins["ff_down"], ins["lora_unit"]
        self.lora_shared = ins["lora_shared"]
        self.q_parts = nc.dram_tensor("q_parts", [H, PARTS, DH, NB * T], BF16, kind="Internal").ap()
        self.k_stack = nc.dram_tensor("k_stack", [len(STACK), HKV * DH, NB * T], BF16, kind="Internal").ap()
        self.out = out


def build(nc, ins, out):
    with ExitStack() as ctx:
        sem = lambda n: ctx.enter_context(nc.semaphore(n))
        sb = lambda n, shape, dt=F32: ctx.enter_context(nc.sbuf_tensor(n, shape, dt))
        s, m, dram = Semaphores(sem, sb), Memory(sb), Dram(nc, ins, out)
        with nc.sbuf_tensor("v_pad", [P, NT, HKV, HB], F32) as m.v_pad:
            const_phase(nc, s, m, dram)
            qkv_phase(nc, s, m, dram)
            attention_phase(nc, s, m, dram)
        with nc.sbuf_tensor("xnh", [P, KD, NB * T], F32R) as m.xnh, nc.sbuf_tensor("xnl", [P, KD, NB * T], F32R) as m.xnl:
            output_phase(nc, s, m, dram)
            with nc.sbuf_tensor("w1_raw", [P, KD, D], F32) as m.w1, nc.sbuf_tensor("w2_raw", [P, KD, D], F32) as m.w2:
                units_phase(nc, s, s.moe, m, dram, "moe", UNITS_MOE, (dram.moe_gate_up, dram.moe_down))
                mix_phase(nc, s, m, dram)
            units_phase(nc, s, s.ff, m, dram, "ff", UNITS_FF, (dram.ff_gate_up, dram.ff_down), lora=True)


def lay_out(inputs):
    f = lambda k: np.asarray(inputs[k])
    tr = lambda a: np.ascontiguousarray(a.T)
    arrays = {
        "x": f("L0_attn_x").reshape(NB * T, D),
        "wqT": tr(f("L0_attn_Wq")), "wkT": tr(f("L0_attn_Wk")), "wvT": tr(f("L0_attn_Wv")), "woT": tr(f("L0_attn_Wo")),
        "rope": setup_tables(),
        "routerT": tr(f("L0_ffn_gate_w")),
        "w1": f("L1_attn_w1"), "w2T": tr(f("L1_attn_w2")), "mask": f("L1_attn_sparse_mask"),
        "b2": f("L1_attn_b2").reshape(1, D),
    }
    shared_up = f("L0_ffn_shared_w_gate_up").reshape(2, NSH, INTER, D).transpose(1, 3, 0, 2).reshape(NSH, D, 2 * INTER)
    shared_down = f("L0_ffn_shared_w_down").T.reshape(NSH, INTER, D)
    arrays["moe_gate_up"] = np.concatenate([f("L0_ffn_w_gate_up").transpose(0, 2, 1), shared_up])
    arrays["moe_down"] = np.concatenate([f("L0_ffn_w_down").transpose(0, 2, 1), shared_down])
    def rows(a):
        out = np.zeros((UNITS_FF * P,) + a.shape[1:], a.dtype)
        out[:FF] = a
        return out.reshape((UNITS_FF, P) + a.shape[1:])
    pair = np.stack([rows(f("L1_ffn_gate_w")), rows(f("L1_ffn_up_w"))], 1)
    arrays["ff_gate_up"] = np.ascontiguousarray(pair.transpose(0, 3, 1, 2)).reshape(UNITS_FF, D, 2 * P)
    arrays["ff_down"] = rows(tr(f("L1_ffn_down_w")))
    lora = np.stack([rows(f("L1_ffn_gate_b")), rows(f("L1_ffn_up_b")), rows(tr(f("L1_ffn_down_a")))], 1)
    def groups(a):
        out = np.zeros(a.shape[:-3] + (3, GROUP) + a.shape[-2:], a.dtype)
        out[..., 0:RANK, :, :] = a[..., None, :, :, :]
        return out.reshape(a.shape[:-3] + (LORA_ROWS,) + a.shape[-2:])
    arrays["lora_unit"] = groups(lora.transpose(0, 3, 1, 2))
    arrays["lora_shared"] = groups(np.stack([f("L1_ffn_gate_a"), f("L1_ffn_up_a"), tr(f("L1_ffn_down_b"))], 1))
    return arrays


def program(nc, shapes):
    ins = {n: nc.dram_tensor(f"in_{n}", shape, F32, kind="ExternalInput").ap() for n, shape in shapes.items()}
    out = nc.dram_tensor("out", [NB * T, D], F32, kind="ExternalOutput").ap()
    build(nc, ins, out)


def kernel(**inputs):
    import concourse.bacc as bacc
    from concourse.bass_utils import run_bass_kernel_spmd
    arrays = lay_out(inputs)
    nc = bacc.Bacc("TRN2", target_bir_lowering=False, num_devices=1)
    program(nc, {n: a.shape for n, a in arrays.items()})
    result = run_bass_kernel_spmd(nc, [{f"in_{n}": a for n, a in arrays.items()}], core_ids=[0])
    return result.results[0]["out"].reshape(NB, T, D)
```
